# Optimizing a Trainium2 kernel written in Bass

```python
import numpy as np
import jax
import jax.numpy as jnp

def _softmax(x, axis=-1):
    return jax.nn.softmax(x, axis=axis)

def _gelu(x):
    return jax.nn.gelu(x, approximate=True)

def _silu(x):
    return jax.nn.silu(x)

def _sigmoid(x):
    return jax.nn.sigmoid(x)

def _layernorm(x, axis=-1, eps=1e-05):
    m = jnp.mean(x, axis=axis, keepdims=True)
    v = jnp.var(x, axis=axis, keepdims=True)
    return (x - m) / jnp.sqrt(v + eps)

def _scatter_add(tgt, idx, src, axis=0):
    return tgt.at[idx].add(src)

def _segment_sum(src, seg, n):
    return jax.ops.segment_sum(src, seg, n)
kernel_name = 'mk_adaln_d2_jaxref_r8_2d658a'

def setup_inputs(seed: int=0):
    np.random.seed(seed)
    _w = jnp.asarray

    def _L0_attn_setup():
        import jax, jax.numpy as jnp
        import numpy as np
        B, T, C = (8, 128, 256)

        def wkv(time_decay, time_first, k, v):
            w = -jnp.exp(time_decay)
            u = time_first
            b, t, c = k.shape
            k_t = jnp.transpose(k, (1, 0, 2))
            v_t = jnp.transpose(v, (1, 0, 2))

            def step(carry, kv):
                p, q, o = carry
                kt, vt = kv
                no = jnp.maximum(o, u + kt)
                A = jnp.exp(o - no)
                Bc = jnp.exp(u + kt - no)
                y = (A * p + Bc * vt) / (A * q + Bc)
                no2 = jnp.maximum(w + o, kt)
                A2 = jnp.exp(w + o - no2)
                B2 = jnp.exp(kt - no2)
                return ((A2 * p + B2 * vt, A2 * q + B2, no2), y)
            init = (jnp.zeros((b, c), k.dtype), jnp.zeros((b, c), k.dtype), jnp.full((b, c), -1e+38, k.dtype))
            _, y = jax.lax.scan(step, init, (k_t, v_t))
            return jnp.transpose(y, (1, 0, 2))
        key = jax.random.key(seed)
        k1, k2, k3, k4, k5 = jax.random.split(key, 5)
        x = jax.random.normal(k1, (B, T, C), dtype=jnp.float32)
        W_rvk = jax.random.normal(k2, (3 * C, C), dtype=jnp.float32) / np.sqrt(C).astype(np.float32)
        W_out = jax.random.normal(k3, (C, C), dtype=jnp.float32) / np.sqrt(C).astype(np.float32)
        time_decay = jax.random.normal(k4, (C,), dtype=jnp.float32) * 0.1
        time_first = jax.random.normal(k5, (C,), dtype=jnp.float32) * 0.1
        return {'x': x, 'W_rvk': W_rvk, 'W_out': W_out, 'time_decay': time_decay, 'time_first': time_first}
    _L0_attn_in = _L0_attn_setup()

    def _L0_ffn_setup():
        import jax, jax.numpy as jnp
        import numpy as np
        H = 256
        M = 176
        E = 32
        TOPK = 6
        G = 8
        TOPK_G = 4
        SH = 2
        B, S = (1, 128)
        key = jax.random.key(seed)
        ks = jax.random.split(key, 9)
        sc = 0.02
        return {'x': jax.random.normal(ks[0], (B, S, H), dtype=jnp.float32), 'w_router': jax.random.normal(ks[1], (H, E), dtype=jnp.float32) * sc, 'corr_bias': jax.random.normal(ks[2], (E,), dtype=jnp.float32) * 0.1, 'gate_w': jax.random.normal(ks[3], (E, H, M), dtype=jnp.float32) * sc, 'up_w': jax.random.normal(ks[4], (E, H, M), dtype=jnp.float32) * sc, 'down_w': jax.random.normal(ks[5], (E, M, H), dtype=jnp.float32) * sc, 'sh_gate_w': jax.random.normal(ks[6], (H, M * SH), dtype=jnp.float32) * sc, 'sh_up_w': jax.random.normal(ks[7], (H, M * SH), dtype=jnp.float32) * sc, 'sh_down_w': jax.random.normal(ks[8], (M * SH, H), dtype=jnp.float32) * sc}
    _L0_ffn_in = _L0_ffn_setup()
    _L0_c = _w((lambda *s: np.random.randn(*s).astype(np.float32) * 0.05)(2, 256))
    _L0_wmod = _w((lambda *s: np.random.randn(*s).astype(np.float32) * 0.05)(256, 6 * 256) * 256 ** (-0.5))

    def _L1_attn_setup():
        import jax, jax.numpy as jnp
        import numpy as np
        C_RGLRU = 8.0

        def _rg_lru(x, wa, ba, wx, bx, lam):
            r = jax.nn.sigmoid(jnp.einsum('bld,ed->ble', x, wa) + ba)
            i = jax.nn.sigmoid(jnp.einsum('bld,ed->ble', x, wx) + bx)
            log_a = -C_RGLRU * r * jax.nn.softplus(lam)
            a = jnp.exp(log_a)
            mult = jnp.sqrt(jnp.maximum(1.0 - jnp.exp(2.0 * log_a), 0.0))
            b = mult * (i * x)

            def combine(c1, c2):
                a1, b1 = c1
                a2, b2 = c2
                return (a1 * a2, a2 * b1 + b2)
            _, h = jax.lax.associative_scan(combine, (a, b), axis=1)
            return h
        key = jax.random.key(seed)
        ks = jax.random.split(key, 12)
        B, L, D, R = (4, 256, 256, 320)
        s_d = 1.0 / np.sqrt(D)
        s_r = 1.0 / np.sqrt(R)
        s_c = 1.0 / np.sqrt(R * 4)
        return {'x': jax.random.normal(ks[0], (B, L, D), jnp.float32), 'w1': jax.random.normal(ks[1], (R, D), jnp.float32) * s_d, 'b1': jnp.zeros((R,), jnp.float32), 'conv_w': jax.random.normal(ks[2], (R, R, 4), jnp.float32) * s_c, 'conv_b': jnp.zeros((R,), jnp.float32), 'wa': jax.random.normal(ks[3], (R, R), jnp.float32) * s_r, 'ba': jnp.zeros((R,), jnp.float32), 'wx': jax.random.normal(ks[4], (R, R), jnp.float32) * s_r, 'bx': jnp.zeros((R,), jnp.float32), 'lam': jax.random.uniform(ks[5], (R,), jnp.float32, 0.5, 2.0), 'w2': jax.random.normal(ks[6], (D, R), jnp.float32) * s_r, 'b2': jnp.zeros((D,), jnp.float32)}
    _L1_attn_in = _L1_attn_setup()

    def _L1_ffn_setup():
        import jax, jax.numpy as jnp
        import numpy as np
        B, S, D, H = (4, 256, 256, 1024)

        def fwht(x):
            orig_shape = x.shape
            n = orig_shape[-1]
            x = x.reshape(-1, n)
            h = 1
            while h < n:
                xb = x.reshape(-1, n // (2 * h), 2, h)
                a = xb[:, :, 0, :]
                b = xb[:, :, 1, :]
                x = jnp.stack([a + b, a - b], axis=2).reshape(-1, n)
                h *= 2
            scale = jnp.asarray(1.0 / np.sqrt(n), dtype=x.dtype)
            return (x * scale).reshape(orig_shape)
        key = jax.random.key(seed)
        kx, k1, k2, k3 = jax.random.split(key, 4)
        x = jax.random.normal(kx, (B, S, D), dtype=jnp.float32)
        W1 = jax.random.normal(k1, (H, D), dtype=jnp.float32) * (1.0 / np.sqrt(D))
        W2 = jax.random.normal(k2, (D, H), dtype=jnp.float32) * (1.0 / np.sqrt(H))
        W3 = jax.random.normal(k3, (H, D), dtype=jnp.float32) * (1.0 / np.sqrt(D))
        return {'x': x, 'W1': W1, 'W2': W2, 'W3': W3}
    _L1_ffn_in = _L1_ffn_setup()
    _L1_c = _w((lambda *s: np.random.randn(*s).astype(np.float32) * 0.05)(2, 256))
    _L1_wmod = _w((lambda *s: np.random.randn(*s).astype(np.float32) * 0.05)(256, 6 * 256) * 256 ** (-0.5))
    _d = {'L0_attn_x': _L0_attn_in['x'], 'L0_attn_W_rvk': _L0_attn_in['W_rvk'], 'L0_attn_W_out': _L0_attn_in['W_out'], 'L0_attn_time_decay': _L0_attn_in['time_decay'], 'L0_attn_time_first': _L0_attn_in['time_first'], 'L0_ffn_w_router': _L0_ffn_in['w_router'], 'L0_ffn_corr_bias': _L0_ffn_in['corr_bias'], 'L0_ffn_gate_w': _L0_ffn_in['gate_w'], 'L0_ffn_up_w': _L0_ffn_in['up_w'], 'L0_ffn_down_w': _L0_ffn_in['down_w'], 'L0_ffn_sh_gate_w': _L0_ffn_in['sh_gate_w'], 'L0_ffn_sh_up_w': _L0_ffn_in['sh_up_w'], 'L0_ffn_sh_down_w': _L0_ffn_in['sh_down_w'], 'L0_c': _L0_c, 'L0_wmod': _L0_wmod, 'L1_attn_w1': _L1_attn_in['w1'], 'L1_attn_b1': _L1_attn_in['b1'], 'L1_attn_conv_w': _L1_attn_in['conv_w'], 'L1_attn_conv_b': _L1_attn_in['conv_b'], 'L1_attn_wa': _L1_attn_in['wa'], 'L1_attn_ba': _L1_attn_in['ba'], 'L1_attn_wx': _L1_attn_in['wx'], 'L1_attn_bx': _L1_attn_in['bx'], 'L1_attn_lam': _L1_attn_in['lam'], 'L1_attn_w2': _L1_attn_in['w2'], 'L1_attn_b2': _L1_attn_in['b2'], 'L1_ffn_W1': _L1_ffn_in['W1'], 'L1_ffn_W2': _L1_ffn_in['W2'], 'L1_ffn_W3': _L1_ffn_in['W3'], 'L1_c': _L1_c, 'L1_wmod': _L1_wmod}
    _x0 = _d['L0_attn_x']
    _d['L0_attn_x'] = jax.random.normal(jax.random.fold_in(jax.random.key(seed), 1), (2, 512, 256), dtype=_x0.dtype)
    del _x0
    return _d

def reference(L0_attn_x, L0_attn_W_rvk, L0_attn_W_out, L0_attn_time_decay, L0_attn_time_first, L0_ffn_w_router, L0_ffn_corr_bias, L0_ffn_gate_w, L0_ffn_up_w, L0_ffn_down_w, L0_ffn_sh_gate_w, L0_ffn_sh_up_w, L0_ffn_sh_down_w, L0_c, L0_wmod, L1_attn_w1, L1_attn_b1, L1_attn_conv_w, L1_attn_conv_b, L1_attn_wa, L1_attn_ba, L1_attn_wx, L1_attn_bx, L1_attn_lam, L1_attn_w2, L1_attn_b2, L1_ffn_W1, L1_ffn_W2, L1_ffn_W3, L1_c, L1_wmod):

    def _L0_attn_ref(x, W_rvk, W_out, time_decay, time_first):
        import jax, jax.numpy as jnp
        import numpy as np
        B, T, C = (8, 128, 256)

        def wkv(time_decay, time_first, k, v):
            w = -jnp.exp(time_decay)
            u = time_first
            b, t, c = k.shape
            k_t = jnp.transpose(k, (1, 0, 2))
            v_t = jnp.transpose(v, (1, 0, 2))

            def step(carry, kv):
                p, q, o = carry
                kt, vt = kv
                no = jnp.maximum(o, u + kt)
                A = jnp.exp(o - no)
                Bc = jnp.exp(u + kt - no)
                y = (A * p + Bc * vt) / (A * q + Bc)
                no2 = jnp.maximum(w + o, kt)
                A2 = jnp.exp(w + o - no2)
                B2 = jnp.exp(kt - no2)
                return ((A2 * p + B2 * vt, A2 * q + B2, no2), y)
            init = (jnp.zeros((b, c), k.dtype), jnp.zeros((b, c), k.dtype), jnp.full((b, c), -1e+38, k.dtype))
            _, y = jax.lax.scan(step, init, (k_t, v_t))
            return jnp.transpose(y, (1, 0, 2))
        rvk = jnp.einsum('btc,dc->btd', x, W_rvk)
        r, v, k = jnp.split(rvk, 3, axis=-1)
        y = jax.nn.sigmoid(r) * wkv(time_decay, time_first, k, v)
        return jnp.einsum('btc,dc->btd', y, W_out)

    def _L0_ffn_ref(x, w_router, corr_bias, gate_w, up_w, down_w, sh_gate_w, sh_up_w, sh_down_w):
        import jax, jax.numpy as jnp
        import numpy as np
        H = 256
        M = 176
        E = 32
        TOPK = 6
        G = 8
        TOPK_G = 4
        SH = 2
        B, S = (1, 128)
        b, s, h = x.shape
        xf = x.reshape(-1, h)
        T = xf.shape[0]
        logits = xf @ w_router
        scores = jax.nn.sigmoid(logits)
        sfc = scores + corr_bias
        grp = sfc.reshape(T, G, E // G)
        top2, _ = jax.lax.top_k(grp, 2)
        group_scores = top2.sum(-1)
        _, gidx = jax.lax.top_k(group_scores, TOPK_G)
        group_mask = jax.nn.one_hot(gidx, G, dtype=jnp.float32).sum(axis=1) > 0
        score_mask = jnp.repeat(group_mask, E // G, axis=1)
        masked = jnp.where(score_mask, sfc, -jnp.inf)
        _, topk_idx = jax.lax.top_k(masked, TOPK)
        topk_w = jnp.take_along_axis(scores, topk_idx, axis=1)
        combine = jnp.zeros((T, E), dtype=x.dtype).at[jnp.arange(T)[:, None], topk_idx].add(topk_w)
        g = jnp.einsum('th,ehm->etm', xf, gate_w)
        u = jnp.einsum('th,ehm->etm', xf, up_w)
        eo = jnp.einsum('etm,emh->eth', jax.nn.silu(g) * u, down_w)
        routed = jnp.einsum('te,eth->th', combine, eo)
        shared = jax.nn.silu(xf @ sh_gate_w) * (xf @ sh_up_w) @ sh_down_w
        return (routed + shared).reshape(b, s, h)

    def _L1_attn_ref(x, w1, b1, conv_w, conv_b, wa, ba, wx, bx, lam, w2, b2):
        import jax, jax.numpy as jnp
        import numpy as np
        C_RGLRU = 8.0

        def _rg_lru(x, wa, ba, wx, bx, lam):
            r = jax.nn.sigmoid(jnp.einsum('bld,ed->ble', x, wa) + ba)
            i = jax.nn.sigmoid(jnp.einsum('bld,ed->ble', x, wx) + bx)
            log_a = -C_RGLRU * r * jax.nn.softplus(lam)
            a = jnp.exp(log_a)
            mult = jnp.sqrt(jnp.maximum(1.0 - jnp.exp(2.0 * log_a), 0.0))
            b = mult * (i * x)

            def combine(c1, c2):
                a1, b1 = c1
                a2, b2 = c2
                return (a1 * a2, a2 * b1 + b2)
            _, h = jax.lax.associative_scan(combine, (a, b), axis=1)
            return h
        h = jax.nn.silu(jnp.einsum('bld,rd->blr', x, w1) + b1)
        hc = h.transpose(0, 2, 1)
        hc = jax.lax.conv_general_dilated(hc, conv_w, window_strides=(1,), padding=[(3, 3)], rhs_dilation=(2,), dimension_numbers=('NCH', 'OIH', 'NCH'))
        hc = hc + conv_b[None, :, None]
        h = hc.transpose(0, 2, 1)
        h = _rg_lru(h, wa, ba, wx, bx, lam)
        return jnp.einsum('blr,dr->bld', h, w2) + b2

    def _L1_ffn_ref(x, W1, W2, W3):
        import jax, jax.numpy as jnp
        import numpy as np
        B, S, D, H = (4, 256, 256, 1024)

        def fwht(x):
            orig_shape = x.shape
            n = orig_shape[-1]
            x = x.reshape(-1, n)
            h = 1
            while h < n:
                xb = x.reshape(-1, n // (2 * h), 2, h)
                a = xb[:, :, 0, :]
                b = xb[:, :, 1, :]
                x = jnp.stack([a + b, a - b], axis=2).reshape(-1, n)
                h *= 2
            scale = jnp.asarray(1.0 / np.sqrt(n), dtype=x.dtype)
            return (x * scale).reshape(orig_shape)
        up_gate = jnp.einsum('bsd,hd->bsh', x, W1)
        up_lin = jnp.einsum('bsd,hd->bsh', x, W3)
        hidden = jax.nn.silu(up_gate) * up_lin
        hidden = fwht(hidden)
        out = jnp.einsum('bsh,dh->bsd', hidden, W2)
        return out
    x = L0_attn_x
    mod = (_silu(L0_c) @ L0_wmod).reshape(L0_c.shape[0], 6, 1, -1)
    sa, ca, ga, sb, cb, gb = (mod[:, 0], mod[:, 1], mod[:, 2], mod[:, 3], mod[:, 4], mod[:, 5])
    ga = (2 * (ga >= 0) - 1) * jnp.maximum(jnp.abs(ga), 0.25)
    gb = (2 * (gb >= 0) - 1) * jnp.maximum(jnp.abs(gb), 0.25)
    h = _layernorm(x, axis=-1) * (1 + ca) + sa
    x = x + ga * _L0_attn_ref(h, L0_attn_W_rvk, L0_attn_W_out, L0_attn_time_decay, L0_attn_time_first)
    h = _layernorm(x, axis=-1) * (1 + cb) + sb
    x = x + gb * _L0_ffn_ref(h, L0_ffn_w_router, L0_ffn_corr_bias, L0_ffn_gate_w, L0_ffn_up_w, L0_ffn_down_w, L0_ffn_sh_gate_w, L0_ffn_sh_up_w, L0_ffn_sh_down_w)
    mod = (_silu(L1_c) @ L1_wmod).reshape(L1_c.shape[0], 6, 1, -1)
    sa, ca, ga, sb, cb, gb = (mod[:, 0], mod[:, 1], mod[:, 2], mod[:, 3], mod[:, 4], mod[:, 5])
    ga = (2 * (ga >= 0) - 1) * jnp.maximum(jnp.abs(ga), 0.25)
    gb = (2 * (gb >= 0) - 1) * jnp.maximum(jnp.abs(gb), 0.25)
    h = _layernorm(x, axis=-1) * (1 + ca) + sa
    x = x + ga * _L1_attn_ref(h, L1_attn_w1, L1_attn_b1, L1_attn_conv_w, L1_attn_conv_b, L1_attn_wa, L1_attn_ba, L1_attn_wx, L1_attn_bx, L1_attn_lam, L1_attn_w2, L1_attn_b2)
    h = _layernorm(x, axis=-1) * (1 + cb) + sb
    x = x + gb * _L1_ffn_ref(h, L1_ffn_W1, L1_ffn_W2, L1_ffn_W3)
    return x

_drawn_inputs = setup_inputs


def setup_inputs(seed=0):
    import zlib

    import numpy as np

    out = dict(_drawn_inputs(seed))
    spreads = {'L1_attn_b1': (0.0, 2.0),
     'L1_attn_conv_b': (0.0, 2.0),
     'L1_attn_ba': (0.0, 2.0),
     'L1_attn_bx': (0.0, 2.0),
     'L1_attn_b2': (0.0, 1.755)}
    factors = {'L0_attn_time_decay': 8.0,
     'L0_attn_time_first': 8.0,
     'L0_ffn_w_router': 8.0,
     'L0_ffn_corr_bias': 8.0,
     'L0_ffn_gate_w': 8.0,
     'L0_ffn_up_w': 8.0,
     'L0_ffn_down_w': 8.0,
     'L0_ffn_sh_gate_w': 8.0,
     'L0_ffn_sh_up_w': 8.0,
     'L0_ffn_sh_down_w': 8.0,
     'L1_attn_wa': 37.569,
     'L1_attn_lam': 64.0,
     'L1_attn_w1': 3.303,
     'L1_attn_wx': 5.756}
    for name, (base, spread) in spreads.items():
        noise = np.random.default_rng([zlib.crc32(name.encode()), seed]).standard_normal(out[name].shape)
        drawn = base * np.exp(spread * noise) if base else spread * noise
        out[name] = jnp.asarray(drawn.astype(out[name].dtype))
    for name, factor in factors.items():
        out[name] = (out[name] * factor).astype(out[name].dtype)
    return out
```

```python
from contextlib import ExitStack

import numpy as np

import concourse.bass as bass
from concourse import mybir

F32 = mybir.dt.float32
F16 = mybir.dt.float16
BF16 = mybir.dt.bfloat16
I32 = mybir.dt.int32
U32 = mybir.dt.uint32
ALU = mybir.AluOpType
ACT = mybir.ActivationFunctionType
AX = mybir.AxisListType

P = 128
B = 2
S = 512
C = 256
CT = C // P
NT = B * S // P
TB = S // P
E = 32
G = 8
EG = E // G
TOPG = 4
TOPK = 6
M = 176
MH = M // 2
SHM = 2 * M
SHT = 3
SH_ROWS = [P, P, SHM - 2 * P]
SLOT_TILES = 80
R = 320
RT = 3
R_ROWS = [P, P, R - 2 * P]
TAPS = 4
PAD = 3
H = 1024
HT = H // P
EPS = 1e-5
BIG = 3.0e38
NONE = -1.0e30
START = -1.0e38

(P_TD, P_TF, P_B1, P_CB, P_BA, P_BX, P_LAM, P_C0, P_C1, P_TOK, P_J, P_ZERO) = (
    0, 2, 4, 7, 10, 13, 17, 20, 24, 28, 36, 37)
P_COLS = 40
K_ID, K_TRI, K_HAD, K_IOTA, K_THR = 0, P, 2 * P, 3 * P, 4 * P
K_COLS = 4 * P + G
SA, CA, GA, SB, CB, GB = range(6)


def two_layers(nc, x_in, small, consts, wmod0, wmod1, w_rvk, w_out, w_router, corr_bias,
               w_gu, w_dn, w_shgu, w_shdn, w_1, w_conv, w_gates, w_2, w_f13, w_f2, out):
    mod_dram = [nc.dram_tensor(f"mod_dram{i}", (B, 6 * C), F32, kind="Internal").ap() for i in range(2)]
    h2_dram = nc.dram_tensor("h2_dram", (B * S, C), F32, kind="Internal").ap()
    x1_dram = nc.dram_tensor("x1_dram", (P, NT * C), F32, kind="Internal").ap()
    y_dram = nc.dram_tensor("y_dram", (SLOT_TILES * P, C), F32, kind="Internal").ap()

    with ExitStack() as ctx:
        def sb(name, shape, dt=F32):
            return ctx.enter_context(nc.sbuf_tensor(name, shape, dt))

        def sem(name):
            return ctx.enter_context(nc.semaphore(name))

        bank = [ctx.enter_context(nc.psum_tensor(f"bank{i}", [P, 512], F32)) for i in range(8)]

        GUW, DNW = 4 * M, 2 * C
        DN0 = E * GUW
        arena = sb("arena", [P, E * (GUW + DNW)])
        gu = arena[:, 0:DN0]
        dn = arena[0:MH, DN0:DN0 + E * DNW]

        def carve(limit, start):
            top = [start]

            def take(n):
                top[0] += n
                assert top[0] <= limit, (top[0], limit)
                return arena[:, top[0] - n:top[0]]
            return take, top

        par = sb("par", [P, P_COLS])
        con = sb("con", [P, K_COLS])
        ident = con[:, K_ID:K_ID + P]
        norm = sb("norm", [P, NT, C])
        shared_y = norm
        actT_all = sb("hT", [P, CT, B * S])
        hT = actT_all
        stats = sb("stats", [P, NT, 6])
        mv = sb("mv", [P, NT, 2])
        ve = sb("ve", [P, NT])
        rstd = sb("rstd", [P, NT])
        mhalf = sb("mhalf", [P, NT])
        silc = sb("silc", [P, 8])
        modcol = sb("modcol", [P, 2, 6 * CT, B])
        wneg = sb("wneg", [P, CT])
        gb0 = sb("gb0", [P, B, C])
        shgu = sb("shgu", [P, CT, 2 * SHM])
        shdn = sb("shdn", [P, SHT, C])
        router = sb("router", [P, CT, E])
        cbias = sb("cbias", [P, E])

        TW = 4 * C + 2 * C + 2 * 2 * M + 2 * C + 2 * C
        tile_mem = sb("tile_mem", [P, TW])
        o = 0
        xg = [tile_mem[:, o + i * C:o + (i + 1) * C] for i in range(4)]; o += 4 * C
        xgT = [tile_mem[:, o + i * C:o + (i + 1) * C] for i in range(2)]; o += 2 * C
        sil = [tile_mem[:, o + i * M:o + (i + 1) * M] for i in range(2)]; o += 2 * M
        hid = [tile_mem[:, o + i * M:o + (i + 1) * M] for i in range(2)]; o += 2 * M
        hidT = [tile_mem[0:MH, o + i * 2 * P:o + (i + 1) * 2 * P] for i in range(2)]; o += 2 * C
        yt = [tile_mem[:, o + i * C:o + (i + 1) * C] for i in range(2)]; o += 2 * C
        modrow0 = tile_mem[0:B, 0:6 * C]
        modB0 = tile_mem[:, 6 * C:6 * C + B * 3 * C].rearrange("p (b n) -> p b n", b=B)
        sh_hid = tile_mem[:, 0:SHT * S].rearrange("p (m n) -> p m n", m=SHT)
        sh_sil = tile_mem[:, SHT * S:(SHT + 1) * S]

        scores = sb("scores", [P, NT, E])
        o = (SHT + 1) * S

        def temp(*shape):
            nonlocal o
            n = NT * int(np.prod(shape))
            o += n
            assert o <= TW
            names = "abc"[:len(shape)]
            return tile_mem[:, o - n:o].rearrange(f"p (t {' '.join(names)}) -> p t {' '.join(names)}",
                                                  t=NT, **dict(zip(names, shape)))
        sfc = temp(E)
        hi2, lo2 = temp(G, 2), temp(G, 2)
        m1, m2, m3 = temp(G), temp(G), temp(G)
        gsx, gtop, grep = temp(G + 8 - TOPG), temp(8), temp(G + 8 - TOPG)
        gmask, gpen = temp(G), temp(G)
        sfx = sb("sfx", [P, NT, E + 8 - TOPK])
        stop8 = sb("stop8", [P, NT, 8])
        srep = sb("srep", [P, NT, E + 8 - TOPK])
        mask = sb("mask", [P, NT, E])
        mask16 = sb("mask16", [P, NT, E], BF16)
        tri16 = sb("tri16", [P, P], BF16)
        ones16 = sb("ones16", [P, P], BF16)
        iota16 = sb("iota16", [P, P], F16)
        cmp8 = sb("cmp8", [P, E, G])
        ntile = sb("ntile", [P, E])
        incl = sb("incl", [P, E])
        onesE = sb("onesE", [P, E])
        base = sb("base", [P, E])
        pos = sb("pos", [P, NT, E])
        ptop = sb("ptop", [P, NT, 8])
        pidx = sb("pidx", [P, NT, 8], I32)
        pint = sb("pint", [P, 2, NT, 8], I32)
        pflt = sb("pflt", [P, 2, NT, 8])
        wk = sb("wk", [P, NT, TOPK])
        onehot_s = sb("onehot_s", [P, 4, P], F16)
        onehot_j = sb("onehot_j", [P, 4, SLOT_TILES], F16)
        ejcmp = sb("ejcmp", [SLOT_TILES, E])
        ej = sb("ej", [SLOT_TILES, 1])
        eoff = sb("eoff", [1, SLOT_TILES], I32)
        gidx = sb("gidx", [P, SLOT_TILES], U32)
        tile_idx = [sb(f"tile_idx{i}", [P, 1], U32) for i in range(4)]

        EARLY = 14
        take, _ = carve(DN0, EARLY * GUW)
        X = take(NT * C).rearrange("p (t c) -> p t c", t=NT)
        rvk = take(CT * 3 * C).rearrange("p (k n) -> p k n", k=CT)
        wout = take(CT * C).rearrange("p (k n) -> p k n", k=CT)
        kS = [take(S) for _ in range(2)]
        vS = [take(S) for _ in range(2)]
        er = [take(S) for _ in range(2)]
        _, here = carve(DN0, EARLY * GUW)
        O = take(S + 1)
        Q = take(S + 1)
        PP = take(S + 1)
        z, t1, t2, rz, mz, Bv = [take(S) for _ in range(6)]
        wm0 = arena[:, DN0 - 6 * C * CT:DN0].rearrange("p (k n) -> p k n", k=CT)

        take1, _ = carve(E * (GUW + DNW), 0)
        X2 = take1(NT * C).rearrange("p (t c) -> p t c", t=NT)
        yg = [take1(TOPK * C).rearrange("p (k c) -> p k c", k=TOPK) for _ in range(2)]
        wm1_mem = take1(CT * 6 * C + 6 * C)
        wm1 = wm1_mem[:, 0:CT * 6 * C].rearrange("p (k n) -> p k n", k=CT)
        modrow1 = wm1_mem[0:B, CT * 6 * C:]
        fhid = wm1_mem[:, 0:HT * S].rearrange("p (h n) -> p h n", h=HT)
        modB1 = take1(B * 2 * C).rearrange("p (b n) -> p b n", b=B)
        w1 = take1(CT * R).rearrange("p (k n) -> p k n", k=CT)
        wconv = take1(RT * TAPS * R).rearrange("p (i k n) -> p i k n", i=RT, k=TAPS)
        wgate = take1(RT * 2 * R).rearrange("p (i n) -> p i n", i=RT)
        w2 = take1(RT * C).rearrange("p (i n) -> p i n", i=RT)
        f13 = take1(CT * 2 * H).rearrange("p (k n) -> p k n", k=CT)
        f2 = take1(HT * C).rearrange("p (h n) -> p h n", h=HT)
        f2a = take1(HT * C).rearrange("p (h n) -> p h n", h=HT)
        f2b = f2
        h1 = take1(RT * (S + 2 * PAD)).rearrange("p (i n) -> p i n", i=RT)
        hc = take1(RT * S).rearrange("p (i n) -> p i n", i=RT)
        rS = take1(RT * S).rearrange("p (i n) -> p i n", i=RT)
        iS = take1(RT * S).rearrange("p (i n) -> p i n", i=RT)
        aS = take1(RT * S).rearrange("p (i n) -> p i n", i=RT)
        a2 = take1(RT * S).rearrange("p (i n) -> p i n", i=RT)
        hs = take1(RT * S).rearrange("p (i n) -> p i n", i=RT)
        fsil = [tile_mem[:, i * S:(i + 1) * S] for i in range(2)]
        sp = sb("sp", [P, 6, RT])

        par_in, wm0_in, rvk_in, wout_in, route_in, sh_in = [sem(n) for n in (
            "par_in", "wm0_in", "rvk_in", "wout_in", "route_in", "sh_in")]
        x_in_s = [sem(f"x_in{b}") for b in range(B)]
        gu_early, gu_late, dn_in = sem("gu_early"), sem("gu_late"), sem("dn_in")
        mod_out = [sem(f"mod_out{i}") for i in range(2)]
        modB_in = [sem(f"modB_in{i}") for i in range(2)]
        h2_out, x1_out, x1_in = sem("h2_out"), sem("x1_out"), sem("x1_in")
        xg_in = [sem(f"xg_in{i}") for i in range(4)]
        y_out = [sem(f"y_out{i}") for i in range(2)]
        yg_in = [sem(f"yg_in{i}") for i in range(2)]
        wm1_in, w1_in, conv_in, gate_in, w2_in, f13_in, f2_in, out_out = [sem(n) for n in (
            "wm1_in", "w1_in", "conv_in", "gate_in", "w2_in", "f13_in", "f2_in", "out_out")]
        act_step, dve_step, pool_step = sem("act_step"), sem("dve_step"), sem("pool_step")
        silc_ready = sem("silc_ready")
        modps_done = sem("modps_done")
        modrow_ready = sem("modrow_ready")
        modT_done = sem("modT_done")
        modcol_ready = sem("modcol_ready")
        modB_ready = sem("modB_ready")
        ve_ready, rstd_ready = sem("ve_ready"), sem("rstd_ready")
        norm_ready = sem("norm_ready")
        normT_done = sem("normT_done")
        hT_ready = sem("hT_ready")
        rvk_done = sem("rvk_done")
        kvr_ready = sem("kvr_ready")
        exparg_ready = sem("exparg_ready")
        exp_ready = sem("exp_ready")
        yT_ready = sem("yT_ready")
        proj_done = sem("proj_done")
        x_done = sem("x_done")
        logit_done, score_ready = sem("logit_done"), sem("score_ready")
        mask_ready, rank_done = sem("mask_ready"), sem("rank_done")
        ej_ready, ejT_done, eoff_ready = sem("ej_ready"), sem("ejT_done"), sem("eoff_ready")
        onehot_ready, onehot_used = sem("onehot_ready"), sem("onehot_used")
        gidx_ready = sem("gidx_ready")
        shps_done, shsil_ready, shhid_ready = sem("shps_done"), sem("shsil_ready"), sem("shhid_ready")
        shy_done, shy_ready = sem("shy_done"), sem("shy_ready")
        tx_done, xgT_ready, gu_done, sil_ready, hid_ready, th_done, hidT_ready, dn_done, y_ready = [
            sem(n) for n in ("tx_done", "xgT_ready", "gu_done", "sil_ready", "hid_ready", "th_done",
                             "hidT_ready", "dn_done", "y_ready")]
        tile_idx_ready, gathers_begun = sem("tile_idx_ready"), sem("gathers_begun")
        comb_done = sem("comb_done")
        w1_done, h1_ready, conv_done, hc_ready = [sem(n) for n in (
            "w1_done", "h1_ready", "conv_done", "hc_ready")]
        gates_done, gates_ready, a_ready, a2_ready, mult_ready, hs_ready = [sem(n) for n in (
            "gates_done", "gates_ready", "a_ready", "a2_ready", "mult_ready", "hs_ready")]
        had_done, had_ready, f2_ready = sem("had_done"), sem("had_ready"), sem("f2_ready")
        mhalf_ready, sp_ready, pads_ready, ix_ready, a2min_ready = [sem(n) for n in (
            "mhalf_ready", "sp_ready", "pads_ready", "ix_ready", "a2min_ready")]
        fps_done, fsil_ready, fhid_ready = sem("fps_done"), sem("fsil_ready"), sem("fhid_ready")

        def counter(eng, s):
            n = [0]

            def step(ins):
                ins.then_inc(s, 1)
                n[0] += 1
                return n[0]

            def settle(k=None):
                eng.wait_ge(s, n[0] if k is None else k)
            return step, settle

        block = ctx.enter_context(nc.Block())

        @block.sync
        def _(sp_):
            sp_.dma_start(par[:, :], small).then_inc(par_in, 16)
            sp_.dma_start(con[:, :], consts).then_inc(par_in, 16)
            xv = x_in.rearrange("(t p) c -> p t c", p=P)
            sp_.dma_start(X[:, 0:TB, :], xv[:, 0:TB, :]).then_inc(x_in_s[0], 16)
            sp_.dma_start(wm0, wmod0).then_inc(wm0_in, 16)
            sp_.dma_start(X[:, TB:NT, :], xv[:, TB:NT, :]).then_inc(x_in_s[1], 16)
            sp_.dma_start(rvk, w_rvk).then_inc(rvk_in, 16)
            sp_.dma_start(wout, w_out).then_inc(wout_in, 16)
            sp_.dma_start(router[:, :, :], w_router).then_inc(route_in, 16)
            sp_.dma_start(cbias[:, :], corr_bias).then_inc(route_in, 16)
            sp_.dma_start(shgu[:, :, :], w_shgu).then_inc(sh_in, 16)
            sp_.dma_start(shdn[:, :, :], w_shdn).then_inc(sh_in, 16)

            sp_.wait_ge(modrow_ready, 3)
            sp_.dma_start(mod_dram[0], modrow0).then_inc(mod_out[0], 16)
            sp_.wait_ge(mod_out[0], 16)
            for b in range(B):
                for dst, chunk in ((modB0[:, b, 0:C], GA), (modB0[:, b, C:3 * C], SB), (gb0[:, b, :], GB)):
                    n = dst.shape[-1]
                    src = mod_dram[0][b:b + 1, chunk * C:chunk * C + n].to_broadcast([P, n])
                    sp_.dma_start(dst, src).then_inc(modB_in[0], 16)

            guv = w_gu.rearrange("p (e n) -> p e n", e=E)
            step_e = 7
            for e in range(0, EARLY, step_e):
                sp_.dma_start(gu[:, e * GUW:(e + step_e) * GUW], guv[:, e:e + step_e, :].rearrange("p e n -> p (e n)")).then_inc(gu_early, 16)
            for e in range(0, E, 8):
                sp_.dma_start(dn[:, e * DNW:(e + 8) * DNW], w_dn[:, e * DNW:(e + 8) * DNW]).then_inc(dn_in, 16)

            h2v = h2_dram.rearrange("(t p) c -> p t c", p=P)
            for b in range(B):
                sp_.wait_ge(x_done, b + 1)
                sp_.dma_start(x1_dram[:, b * TB * C:(b + 1) * TB * C],
                              X[:, b * TB:(b + 1) * TB, :].rearrange("p t c -> p (t c)")).then_inc(x1_out, 16)
                sp_.wait_ge(norm_ready, B + b + 1)
                sp_.dma_start(h2v[:, b * TB:(b + 1) * TB, :], norm[:, b * TB:(b + 1) * TB, :]).then_inc(h2_out, 16)
            sp_.wait_ge(x1_out, 16 * B)
            for e in range(EARLY, E, 6):
                sp_.dma_start(gu[:, e * GUW:(e + 6) * GUW], w_gu[:, e * GUW:(e + 6) * GUW]).then_inc(gu_late, 16)

            def store(j, r):
                sp_.wait_ge(y_ready, j + 1)
                dst = y_dram.rearrange("(j p) c -> j p c", p=P)[bass.ds(j, 1), :, :]
                sp_.dma_start(dst.rearrange("a p c -> p (a c)"), yt[r % 2]).then_inc(y_out[r % 2], 16)

            with sp_.Fori(0, SLOT_TILES // 4) as q:
                for r in range(4):
                    store(4 * q + r, r)

            sp_.wait_ge(dn_done, SLOT_TILES)
            sp_.dma_start(X2.rearrange("p t c -> p (t c)"), x1_dram).then_inc(x1_in, 16)
            sp_.dma_start(wm1, wmod1).then_inc(wm1_in, 16)
            sp_.dma_start(w1, w_1).then_inc(w1_in, 16)
            sp_.dma_start(wconv.rearrange("p i k n -> p (i k n)"), w_conv).then_inc(conv_in, 16)
            sp_.dma_start(wgate, w_gates).then_inc(gate_in, 16)
            sp_.dma_start(w2, w_2).then_inc(w2_in, 16)
            sp_.dma_start(f2, w_f2).then_inc(f2_in, 16)
            sp_.dma_start(f13, w_f13).then_inc(f13_in, 16)
            sp_.wait_ge(modrow_ready, 6)
            sp_.dma_start(mod_dram[1], modrow1).then_inc(mod_out[1], 16)
            sp_.wait_ge(mod_out[1], 16)
            for b in range(B):
                for i, chunk in enumerate((GA, GB)):
                    src = mod_dram[1][b:b + 1, chunk * C:(chunk + 1) * C].to_broadcast([P, C])
                    sp_.dma_start(modB1[:, b, i * C:(i + 1) * C], src).then_inc(modB_in[1], 16)

            ov = out.rearrange("(t p) c -> p t c", p=P)
            for b in range(B):
                sp_.wait_ge(x_done, 2 * B + b + 1)
                sp_.dma_start(ov[:, b * TB:(b + 1) * TB, :], X2[:, b * TB:(b + 1) * TB, :]).then_inc(out_out, 16)
            sp_.wait_ge(out_out, 16 * B)

        @block.tensor
        def _(pe):
            def mod_rows(layer):
                pe.wait_ge(silc_ready, 1)
                pe.wait_ge((wm0_in, wm1_in)[layer], 16)
                wm = (wm0, wm1)[layer]
                for n in range(3):
                    for k in range(CT):
                        mm = pe.matmul(bank[2 + n][0:B, :], silc[:, 4 * layer + B * k:4 * layer + B * (k + 1)],
                                       wm[:, k, n * 512:(n + 1) * 512], start=(k == 0), stop=(k == CT - 1))
                    mm.then_inc(modps_done, 1)

            def mod_cols(layer, chunks, row):
                pe.wait_ge(modrow_ready, 3 * layer + 3)
                for n in chunks:
                    for h in range(CT):
                        j = CT * n + h
                        mm = pe.transpose(bank[5][:, B * j:B * (j + 1)], row[:, j * P:(j + 1) * P], ident[0:B, 0:B])
                mm.then_inc(modT_done, 1)

            def transposes(n, b, wait_free):
                pe.wait_ge(norm_ready, n + 1)
                if wait_free is not None:
                    pe.wait_ge(*wait_free)
                for c in range(CT):
                    for t in range(TB):
                        mm = pe.transpose(bank[c][:, t * P:(t + 1) * P], norm[:, b * TB + t, c * P:(c + 1) * P], ident)
                    mm.then_inc(normT_done, 1)

            def project(src, w, ks, b, rows):
                for t in range(TB):
                    for k in range(ks):
                        mm = pe.matmul(bank[t // 2][:, (t % 2) * C:(t % 2 + 1) * C], src(k, t), w[0:rows[k], k, :],
                                       start=(k == 0), stop=(k == ks - 1))
                mm.then_inc(proj_done, 1)

            pe.wait_ge(par_in, 32)
            mod_rows(0)
            mod_cols(0, (SA, CA), modrow0)

            for b in range(B):
                transposes(b, b, (hT_ready, CT * b) if b else None)
                pe.wait_ge(hT_ready, CT * (b + 1))
                if b == 0:
                    pe.wait_ge(rvk_in, 16)
                    pe.wait_ge(modrow_ready, 3)
                    pe.wait_ge(modcol_ready, 1)
                for c in range(CT):
                    for i, part in enumerate((2, 1, 0)):
                        m0 = part * C + c * P
                        if b:
                            pe.wait_ge(kvr_ready, 3 * c + i + 1)
                        for k in range(CT):
                            mm = pe.matmul(bank[2 + 3 * c + i][:, :], rvk[:, k, m0:m0 + P],
                                           hT[:, k, b * S:(b + 1) * S], start=(k == 0), stop=(k == CT - 1))
                        mm.then_inc(rvk_done, 1)
            pe.wait_ge(wout_in, 16)
            for b in range(B):
                pe.wait_ge(hT_ready, CT * (B + b))
                pe.wait_ge(yT_ready, CT * (b + 1))
                project(lambda k, t: hT[:, k, b * S + t * P:b * S + (t + 1) * P], wout, CT, b, [P] * CT)
                transposes(B + b, b, (x_done, b + 1))

            pe.wait_ge(route_in, 32)
            pe.wait_ge(hT_ready, CT * 2 * B)
            for t in range(NT):
                for k in range(CT):
                    mm = pe.matmul(bank[0][:, t * E:(t + 1) * E], hT[:, k, t * P:(t + 1) * P], router[:, k, :],
                                   start=(k == 0), stop=(k == CT - 1))
            mm.then_inc(logit_done, 1)

            def shared_in(b):
                if b == 0:
                    pe.wait_ge(sh_in, 32)
                    pe.wait_ge(kvr_ready, 3 * CT * B)
                for m in range(SHT):
                    if b:
                        pe.wait_ge(shhid_ready, m + 1)
                    for h in range(2):
                        c0 = h * SHM + m * P
                        for k in range(CT):
                            mm = pe.matmul(bank[2 + 2 * m + h][0:SH_ROWS[m], :], shgu[:, k, c0:c0 + SH_ROWS[m]],
                                           hT[:, k, b * S:(b + 1) * S], start=(k == 0), stop=(k == CT - 1))
                        mm.then_inc(shps_done, 1)

            def shared_out(b, banks):
                pe.wait_ge(shhid_ready, SHT * (b + 1))
                for t in range(TB):
                    for k in range(SHT):
                        mm = pe.matmul(bank[banks[t // 2]][:, (t % 2) * C:(t % 2 + 1) * C],
                                       sh_hid[0:SH_ROWS[k], k, t * P:(t + 1) * P], shdn[0:SH_ROWS[k], k, :],
                                       start=(k == 0), stop=(k == SHT - 1))
                mm.then_inc(shy_done, 1)

            shared_in(0)
            pe.wait_ge(mask_ready, 1)
            pe.wait_ge(score_ready, 1)
            m16 = mask16[:, :, :].rearrange("p t e -> p (t e)")
            pe.matmul(bank[0][:, 0:NT * E], tri16[:, :], m16, start=True, stop=False, skip_group_check=True)
            for d in range(1, NT):
                pe.matmul(bank[0][:, d * E:NT * E], ones16[:, :], m16[:, 0:(NT - d) * E], start=False,
                          stop=(d == NT - 1), skip_group_check=True)
            for t in range(NT):
                mm = pe.matmul(bank[1][:, 0:E], ones16[:, :], m16[:, t * E:(t + 1) * E], start=(t == 0), stop=(t == NT - 1))
            mm.then_inc(rank_done, 1)
            shared_out(0, (2, 3))
            pe.wait_ge(shy_ready, 1)
            shared_in(1)
            pe.wait_ge(ej_ready, 1)
            pe.transpose(bank[1][0:1, 64:64 + SLOT_TILES], ej[:, :], ident[0:SLOT_TILES, 0:SLOT_TILES]).then_inc(ejT_done, 1)
            pe.wait_ge(eoff_ready, 1)
            for n in range(NT * TOPK):
                pe.wait_ge(onehot_ready, n + 1)
                pe.matmul(bank[1][:, 128:128 + SLOT_TILES], onehot_s[:, n % 4, :], onehot_j[:, n % 4, :],
                          start=(n == 0), stop=(n == NT * TOPK - 1)).then_inc(onehot_used, 1)
            shared_out(1, (2, 3))

            def tx(q, r):
                pe.wait_ge(xg_in[r], 16 * (q + 1))
                if not early(q, r, 2):
                    pe.wait_ge(xgT_ready, 4 * q + (r - 1))
                for c in range(CT):
                    mm = pe.transpose(bank[r % 2][:, c * P:(c + 1) * P], xg[r][:, c * P:(c + 1) * P], ident)
                mm.then_inc(tx_done, 1)

            def gate_up(q, r, e):
                pe.wait_ge(xgT_ready, 4 * q + (r + 1))
                if not early(q, r, 2):
                    pe.wait_ge(hid_ready, 4 * q + (r - 1))
                for k in range(CT):
                    mm = pe.matmul(bank[2 + r % 2][:, 0:2 * M], xgT[r % 2][:, k * P:(k + 1) * P],
                                   gu[:, bass.ds(e * GUW + k * 2 * M, 2 * M)], start=(k == 0), stop=(k == CT - 1))
                mm.then_inc(gu_done, 1)

            def th(q, r):
                pe.wait_ge(hid_ready, 4 * q + (r + 1))
                if not early(q, r, 2):
                    pe.wait_ge(hidT_ready, 4 * q + (r - 1))
                for k in range(2):
                    mm = pe.transpose(bank[4 + r % 2][0:MH, k * P:(k + 1) * P], hid[r % 2][:, k * MH:(k + 1) * MH], ident)
                mm.then_inc(th_done, 1)

            def down(q, r, e):
                pe.wait_ge(hidT_ready, 4 * q + (r + 1))
                if not early(q, r, 2):
                    pe.wait_ge(y_ready, 4 * q + (r - 1))
                for k in range(2):
                    mm = pe.matmul(bank[6 + r % 2][:, 0:C], hidT[r % 2][:, k * P:(k + 1) * P],
                                   dn[:, bass.ds(e * DNW + k * C, C)], start=(k == 0), stop=(k == 1))
                mm.then_inc(dn_done, 1)

            def expert(q, r):
                return pe.value_load(eoff[0:1, bass.ds(4 * q + r, 1)], min_val=0, max_val=E - 1)

            def tile_step(q, r, first=False, last=False):
                e_now = expert(q, r)
                if not last:
                    tx(*near(q, r, 1))
                if not first:
                    e_prev = expert(*near(q, r, -1))
                    th(*near(q, r, -1))
                gate_up(q, r, e_now)
                if not first:
                    down(*near(q, r, -1), e_prev)

            pe.wait_ge(gidx_ready, 1)
            pe.wait_ge(shy_ready, 2)
            pe.wait_ge(gu_early, 16 * 2)
            pe.wait_ge(gu_late, 16 * 3)
            pe.wait_ge(dn_in, 16 * 4)
            tx(0, 0)
            for r in range(4):
                tile_step(0, r, first=(r == 0))
            with pe.Fori(1, SLOT_TILES // 4 - 1) as q:
                for r in range(4):
                    tile_step(q, r)
            q = SLOT_TILES // 4 - 1
            for r in range(4):
                tile_step(q, r, last=(r == 3))
            th(q, 3)
            down(q, 3, expert(q, 3))

            pe.wait_ge(y_ready, SLOT_TILES)
            mod_rows(1)
            mod_cols(1, (SA, CA, SB, CB), modrow1)
            pe.wait_ge(f2_in, 16)
            pe.wait_ge(modrow_ready, 6)
            for h in range(HT):
                mm = pe.matmul(bank[(6, 7, 2, 3)[h // 2]][:, (h % 2) * C:(h % 2 + 1) * C],
                               con[:, K_HAD:K_HAD + P], f2[:, h, :], start=True, stop=True)
                if h % 2:
                    mm.then_inc(had_done, 1)

            def hidden1(b):
                pe.wait_ge(w1_in, 16)
                pe.wait_ge(had_ready, 4)
                pe.wait_ge(modcol_ready, 2)
                pe.wait_ge(hT_ready, CT * (5 + b))
                for m in range(RT):
                    if b:
                        pe.wait_ge(gates_ready, 2 * RT)
                    for k in range(CT):
                        mm = pe.matmul(bank[2 + m][0:R_ROWS[m], :], w1[:, k, m * P:m * P + R_ROWS[m]],
                                       hT[:, k, b * S:(b + 1) * S], start=(k == 0), stop=(k == CT - 1))
                    mm.then_inc(w1_done, 1)

            def conv(b):
                pe.wait_ge(conv_in, 16)
                pe.wait_ge(h1_ready, RT * (b + 1))
                if b:
                    pe.wait_ge(gates_ready, 2 * RT)
                for m in range(RT):
                    n = 0
                    for i in range(RT):
                        for k in range(TAPS):
                            mm = pe.matmul(bank[5 + m][0:R_ROWS[m], :], wconv[0:R_ROWS[i], i, k, m * P:m * P + R_ROWS[m]],
                                           h1[0:R_ROWS[i], i, 2 * k:2 * k + S], start=(n == 0), stop=(n == RT * TAPS - 1))
                            n += 1
                    mm.then_inc(conv_done, 1)

            def gates(b):
                pe.wait_ge(gate_in, 16)
                pe.wait_ge(hc_ready, RT * (b + 1))
                for m in range(5):
                    for i in range(RT):
                        mm = pe.matmul(bank[2 + m][:, :], wgate[0:R_ROWS[i], i, m * P:(m + 1) * P],
                                       hc[0:R_ROWS[i], i, :], start=(i == 0), stop=(i == RT - 1))
                    mm.then_inc(gates_done, 1)

            def recur_out(b):
                pe.wait_ge(w2_in, 16)
                pe.wait_ge(hs_ready, RT * (b + 1))
                project(lambda k, t: hs[0:(P, P, R_ROWS[2] + 1)[k], k, t * P:(t + 1) * P], w2, RT, b,
                        (P, P, R_ROWS[2] + 1))

            def ffn_in(b):
                pe.wait_ge(f13_in, 16)
                pe.wait_ge(hT_ready, CT * (7 + b))
                pe.wait_ge(gates_ready, 2 * RT * B)
                for h in range(HT):
                    n = HT * b + h
                    if n >= 3:
                        pe.wait_ge(fhid_ready, n - 2)
                    for up in range(2):
                        for k in range(CT):
                            mm = pe.matmul(bank[2 + 2 * (n % 3) + up][:, :], f13[:, k, up * H + h * P:up * H + (h + 1) * P],
                                           hT[:, k, b * S:(b + 1) * S], start=(k == 0), stop=(k == CT - 1))
                        mm.then_inc(fps_done, 1)

            def ffn_out(b):
                pe.wait_ge(fhid_ready, HT * (b + 1))
                pe.wait_ge(f2_ready, 1)
                project(lambda k, t: fhid[:, k, t * P:(t + 1) * P], f2b, HT, b, [P] * HT)

            transposes(4, 0, None)
            hidden1(0)
            conv(0)
            gates(0)
            transposes(5, 1, (hT_ready, CT * 5))
            hidden1(1)
            conv(1)
            pe.wait_ge(hT_ready, CT * 6)
            recur_out(0)
            transposes(6, 0, (x_done, 3))
            gates(1)
            ffn_in(0)
            pe.wait_ge(hT_ready, CT * 7)
            ffn_out(0)
            pe.wait_ge(x_done, 4)
            recur_out(1)
            transposes(7, 1, (x_done, 5))
            ffn_in(1)
            pe.wait_ge(hT_ready, CT * 8)
            ffn_out(1)

        @block.scalar
        def _(act):
            step, settle = counter(act, act_step)
            act.wait_ge(par_in, 32)
            act.activation(silc[:, :], par[:, P_C0:P_C0 + 8], ACT.Silu).then_inc(silc_ready, 1)
            step(act.activation(wneg[:, :], par[:, P_TD:P_TD + CT], ACT.Exp))
            settle()
            step(act.activation(wneg[:, :], wneg[:, :], ACT.Copy, scale=-1.0))

            def modulated(n, b, layer, sh, sc):
                if n in (0, 4):
                    act.wait_ge(modcol_ready, layer + 1)
                for c in range(CT):
                    act.wait_ge(normT_done, CT * n + c + 1)
                    dst = hT[:, c, b * S:(b + 1) * S]
                    if sh is None:
                        act.activation(dst, bank[c][:, :], ACT.Copy).then_inc(hT_ready, 1)
                    else:
                        act.activation(dst, bank[c][:, :], ACT.Identity, bias=modcol[:, layer, CT * sh + c, b:b + 1],
                                       scale=modcol[:, layer, CT * sc + c, b:b + 1]).then_inc(hT_ready, 1)

            def kvr(u):
                if u >= 2:
                    act.wait_ge(yT_ready, u - 1)
                for i, dst in enumerate((kS[u % 2], vS[u % 2], er[u % 2])):
                    act.wait_ge(rvk_done, 3 * u + i + 1)
                    act.activation(dst, bank[2 + 3 * (u % 2) + i][:, :], ACT.Exp if i == 2 else ACT.Copy,
                                   scale=-1.0 if i == 2 else 1.0).then_inc(kvr_ready, 1)

            def exps(u):
                for i, (v, scale, bias) in enumerate(((t1, 1.0, wneg[:, u % 2:u % 2 + 1]), (t2, 1.0, 0.0),
                                                      (rz, -1.0, 0.0), (mz, 1.0, 0.0))):
                    act.wait_ge(exparg_ready, 4 * u + i + 1)
                    act.activation(v, v, ACT.Exp, bias=bias, scale=scale).then_inc(exp_ready, 1)

            modulated(0, 0, 0, SA, CA)
            settle()
            kvr(0)
            kvr(1)
            modulated(1, 1, 0, SA, CA)
            exps(0)
            kvr(2)
            exps(1)
            kvr(3)
            exps(2)
            modulated(2, 0, 0, None, None)
            exps(3)
            modulated(3, 1, 0, None, None)
            act.wait_ge(logit_done, 1)
            act.activation(scores[:, :, :].rearrange("p t e -> p (t e)"), bank[0][:, 0:NT * E], ACT.Sigmoid)\
               .then_inc(score_ready, 1)

            def shared_silu(b):
                for m in range(SHT):
                    n = SHT * b + m
                    act.wait_ge(shps_done, 2 * n + 1)
                    if n:
                        act.wait_ge(shhid_ready, n)
                    act.activation(sh_sil[0:SH_ROWS[m], :], bank[2 + 2 * m][0:SH_ROWS[m], :], ACT.Silu)\
                       .then_inc(shsil_ready, 1)

            def shared_copy(b):
                act.wait_ge(shy_done, b + 1)
                if b == 0:
                    act.wait_ge(h2_out, 16 * B)
                for h in range(2):
                    dst = shared_y[:, b * TB + 2 * h:b * TB + 2 * h + 2, :].rearrange("p t c -> p (t c)")
                    ins = act.activation(dst, bank[2 + h][:, :], ACT.Copy)
                ins.then_inc(shy_ready, 1)

            shared_silu(0)
            shared_copy(0)
            shared_silu(1)
            shared_copy(1)

            def copy_x(q, r):
                act.wait_ge(tx_done, 4 * q + (r + 1))
                if not early(q, r, 2):
                    act.wait_ge(gu_done, 4 * q + (r - 1))
                act.activation(xgT[r % 2], bank[r % 2][:, 0:C], ACT.Copy).then_inc(xgT_ready, 1)

            def tile_silu(q, r):
                act.wait_ge(gu_done, 4 * q + (r + 1))
                if not early(q, r, 2):
                    act.wait_ge(hid_ready, 4 * q + (r - 1))
                act.activation(sil[r % 2], bank[2 + r % 2][:, 0:M], ACT.Silu).then_inc(sil_ready, 1)

            def tile_step(q, r, last=False):
                if not last:
                    copy_x(*near(q, r, 1))
                tile_silu(q, r)

            copy_x(0, 0)
            for r in range(4):
                tile_step(0, r)
            with act.Fori(1, SLOT_TILES // 4 - 1) as q:
                for r in range(4):
                    tile_step(q, r)
            for r in range(4):
                tile_step(SLOT_TILES // 4 - 1, r, last=(r == 3))

            lam = par[:, P_LAM:P_LAM + RT]
            step(act.activation(sp[:, 0, :], lam, ACT.Abs))
            step(act.activation(sp[:, 1, :], lam, ACT.Relu))
            settle()
            step(act.activation(sp[:, 2, :], sp[:, 0, :], ACT.Exp, scale=-1.0))
            settle()
            step(act.activation(sp[:, 3, :], sp[:, 2, :], ACT.Ln, bias=1.0))
            for i, k in enumerate((6, 7, 2, 3)):
                act.wait_ge(had_done, i + 1)
                act.activation(f2a[:, 2 * i:2 * i + 2, :].rearrange("p h c -> p (h c)"), bank[k][:, :], ACT.Copy)\
                   .then_inc(had_ready, 1)

            def recur_hidden(b):
                for m in range(RT):
                    n = R_ROWS[m]
                    act.wait_ge(w1_done, RT * b + m + 1)
                    if b:
                        act.wait_ge(conv_done, RT)
                    act.activation(h1[0:n, m, PAD:PAD + S], bank[2 + m][0:n, :], ACT.Silu,
                                   bias=par[0:n, P_B1 + m:P_B1 + m + 1]).then_inc(h1_ready, 1)

            def conv_out(b):
                for m in range(RT):
                    n = R_ROWS[m]
                    act.wait_ge(conv_done, RT * b + m + 1)
                    if b:
                        act.wait_ge(ix_ready, b)
                    act.activation(hc[0:n, m, :], bank[5 + m][0:n, :], ACT.Identity,
                                   bias=par[0:n, P_CB + m:P_CB + m + 1]).then_inc(hc_ready, 1)

            def gate_sigmoids(b):
                if b:
                    act.wait_ge(hs_ready, RT * b)
                for i, (dst, m, k, p0) in enumerate((
                        (rS[:, 0, :], 0, P_BA, 0), (rS[:, 1, :], 1, P_BA + 1, 0),
                        (iS[:, 0, :], 2, P_BX, 0), (iS[:, 1, :], 3, P_BX + 1, 0),
                        (rS[0:64, 2, :], 4, P_BA + 2, 0), (iS[0:64, 2, :], 4, P_BX + 2, 64))):
                    act.wait_ge(gates_done, 5 * b + m + 1)
                    n = dst.shape[0]
                    act.activation(dst, bank[2 + m][p0:p0 + n, :], ACT.Sigmoid, bias=par[p0:p0 + n, k:k + 1])\
                       .then_inc(gates_ready, 1)

            def decays(b):
                act.wait_ge(gates_ready, 2 * RT * (b + 1))
                act.wait_ge(sp_ready, 1)
                for dst, row, done in ((a2, 5, a2_ready), (aS, 4, a_ready)):
                    for m in range(RT):
                        n = R_ROWS[m]
                        act.activation(dst[0:n, m, :], rS[0:n, m, :], ACT.Exp, scale=sp[0:n, row, m:m + 1]).then_inc(done, 1)

            def roots(b):
                act.wait_ge(a2min_ready, 2 * (b + 1))
                for v in (a2[:, 0:2, :], a2[0:64, 2, :]):
                    act.activation(v, v, ACT.Sqrt, bias=1.0, scale=-1.0).then_inc(mult_ready, 1)

            def ffn_silu(b):
                for h in range(HT):
                    n = HT * b + h
                    act.wait_ge(fps_done, 2 * n + 1)
                    if n >= 2:
                        act.wait_ge(fhid_ready, n - 1)
                    act.activation(fsil[n % 2], bank[2 + 2 * (n % 3)][:, :], ACT.Silu).then_inc(fsil_ready, 1)

            modulated(4, 0, 1, SA, CA)
            act.wait_ge(pads_ready, 1)
            recur_hidden(0)
            conv_out(0)
            gate_sigmoids(0)
            decays(0)
            roots(0)
            modulated(5, 1, 1, SA, CA)
            recur_hidden(1)
            conv_out(1)
            modulated(6, 0, 1, SB, CB)
            gate_sigmoids(1)
            decays(1)
            roots(1)
            ffn_silu(0)
            modulated(7, 1, 1, SB, CB)
            ffn_silu(1)

        @block.gpsimd
        def _(pool):
            def inverse_root(n):
                ts = slice((n % B) * TB, (n % B + 1) * TB)
                pool.wait_ge(ve_ready, n + 1)
                if n == 0:
                    pool.wait_ge(mhalf_ready, 1)
                pool.tensor_tensor(rstd[:, ts], ve[:, ts], mhalf[:, ts], ALU.pow).then_inc(rstd_ready, 1)

            for n in range(4):
                inverse_root(n)

            def gather(q, r):
                if not early(q, r, 4):
                    pool.wait_ge(tx_done, 4 * q + (r - 3))
                pool.tensor_copy(tile_idx[r][:, :], gidx[:, bass.ds(4 * q + r, 1)]).then_inc(tile_idx_ready, 1)
                pool.wait_ge(tile_idx_ready, 4 * q + (r + 1))
                pool.sem_inc(gathers_begun, 1)
                pool.indirect_dma_start(out=xg[r], out_offset=None, in_=h2_dram,
                                        in_offset=bass.IndirectOffsetOnAxis(ap=tile_idx[r][:, :], axis=0))\
                    .then_inc(xg_in[r], 16)

            pool.wait_ge(gidx_ready, 1)
            pool.wait_ge(h2_out, 16 * B)
            pool.wait_ge(shy_done, 2)
            for r in range(4):
                gather(0, r)
            with pool.Fori(1, SLOT_TILES // 4) as q:
                for r in range(4):
                    gather(q, r)

            pool.wait_ge(dn_done, SLOT_TILES)
            pool.memset(h1[:, :, 0:PAD], 0.0)
            pool.memset(h1[:, :, PAD + S:PAD + S + PAD], 0.0).then_inc(pool_step, 1)
            pool.wait_ge(pool_step, 1)
            pool.memset(hs[64:65, 2, :], 1.0).then_inc(pads_ready, 1)

            pool.wait_ge(pads_ready, 1)
            for i in range(2):
                pool.wait_ge(y_out[i], 16 * SLOT_TILES // 2)

            def pick(t):
                if t >= 2:
                    pool.wait_ge(comb_done, t - 1)
                for k in range(TOPK):
                    pool.indirect_dma_start(out=yg[t % 2][:, k, :], out_offset=None, in_=y_dram,
                                            in_offset=bass.IndirectOffsetOnAxis(ap=pidx[:, t, k:k + 1].bitcast(U32), axis=0))\
                        .then_inc(yg_in[t % 2], 16)

            for t in range(TB + 2):
                pick(t)
            inverse_root(4)
            for t in range(TB + 2, NT):
                pick(t)
            for n in range(5, 8):
                inverse_root(n)

        @block.vector
        def _(dve):
            step, settle = counter(dve, dve_step)
            tt, ts_, stt = dve.tensor_tensor, dve.tensor_scalar, dve.scalar_tensor_tensor

            dve.memset(mhalf[:, :], -0.5).then_inc(mhalf_ready, 1)
            dve.memset(ones16[:, :], 1.0)
            dve.memset(onesE[:, :], 1.0)
            dve.memset(O[:, 0:1], START)
            dve.memset(Q[:, 0:1], 0.0)
            step(dve.memset(PP[:, 0:1], 0.0))
            dve.wait_ge(par_in, 32)
            dve.tensor_copy(tri16[:, :], con[:, K_TRI:K_TRI + P])
            step(dve.tensor_copy(iota16[:, :], con[:, K_IOTA:K_IOTA + P]))

            def mod_rows(layer, row):
                for n in range(3):
                    dve.wait_ge(modps_done, 3 * layer + n + 1)
                    dve.tensor_copy(row[:, n * 512:(n + 1) * 512], bank[2 + n][0:B, :]).then_inc(modrow_ready, 1)

            def mod_cols(layer, pairs):
                dve.wait_ge(modT_done, layer + 1)
                for sh, sc in pairs:
                    w = CT * B
                    dst = modcol[:, layer, :, :].rearrange("p j b -> p (j b)")
                    dve.tensor_copy(dst[:, w * sh:w * (sh + 1)], bank[5][:, w * sh:w * (sh + 1)])
                    ins = ts_(dst[:, w * sc:w * (sc + 1)], bank[5][:, w * sc:w * (sc + 1)], 1.0, None, ALU.add)
                ins.then_inc(modcol_ready, 1)

            def gate_floor(g, sign, size):
                step(stt(size, g, -1.0, g, ALU.mult, ALU.max))
                settle()
                ts_(sign, g, 0.0, 2.0, ALU.is_ge, ALU.mult)
                step(ts_(size, size, 0.25, None, ALU.max))
                settle()
                return step(stt(g, sign, -1.0, size, ALU.add, ALU.mult))

            def layer_norm(n, src, modulate=False):
                b = n % B
                tiles = range(b * TB, (b + 1) * TB)
                for t in tiles:
                    last = step(dve.bn_stats(out=stats[:, t, :], in_=src[:, t, :]))
                settle()
                for t in tiles:
                    last = step(dve.bn_aggr(out=mv[:, t, :], in_=stats[:, t, :]))
                settle()
                ts_(ve[:, b * TB:(b + 1) * TB], mv[:, b * TB:(b + 1) * TB, 1], EPS, None, ALU.add).then_inc(ve_ready, 1)
                if n >= B:
                    dve.wait_ge(normT_done, CT * (n - B + 1))
                dve.wait_ge(rstd_ready, n + 1)
                for t in tiles:
                    ins = ts_(norm[:, t, :], src[:, t, :], mv[:, t, 0:1], rstd[:, t:t + 1], ALU.subtract, ALU.mult)
                if modulate:
                    step(ins)
                    settle()
                    v = norm[:, b * TB:(b + 1) * TB, :]
                    sh, sc = [modB0[:, b, i * C:(i + 1) * C].unsqueeze(1).to_broadcast([P, TB, C]) for i in (1, 2)]
                    step(tt(v, v, sc, ALU.mult))
                    settle()
                    ins = tt(v, v, sh, ALU.add)
                ins.then_inc(norm_ready, 1)

            def residual(x, b, gate, done, free, tmp):
                if free <= B:
                    dve.wait_ge(yT_ready, 2 * free + (free < B))
                dve.wait_ge(proj_done, done)
                g = gate.unsqueeze(1).to_broadcast([P, 2, C])
                for h in range(2):
                    step(tt(tmp[h].rearrange("p (t c) -> p t c", t=2), bank[h][:, :].rearrange("p (t c) -> p t c", t=2),
                            g, ALU.mult))
                settle()
                for h in range(2):
                    v = x[:, b * TB + 2 * h:b * TB + 2 * h + 2, :]
                    ins = tt(v, v, tmp[h].rearrange("p (t c) -> p t c", t=2), ALU.add)
                ins.then_inc(x_done, 1)
                dve.wait_ge(x_done, free)

            for b in range(B):
                dve.wait_ge(x_in_s[b], 16)
                if b == 0:
                    layer_norm(0, X)
                    mod_rows(0, modrow0)
                    mod_cols(0, ((SA, CA),))
                else:
                    layer_norm(1, X)
            dve.wait_ge(modB_in[0], 16 * 3 * B)
            z3, t3 = z.rearrange("p (b c) -> p b c", b=B), t1.rearrange("p (b c) -> p b c", b=B)
            gate_floor(modB0[:, :, 0:C], z3, t3)
            settle()
            gate_floor(gb0[:, :, :], z3, t3)
            step(ts_(modB0[:, :, 2 * C:3 * C], modB0[:, :, 2 * C:3 * C], 1.0, None, ALU.add))
            settle()

            def wkv(u):
                b, c = divmod(u, CT)
                k, v, e = kS[u % 2], vS[u % 2], er[u % 2]
                dve.wait_ge(kvr_ready, 3 * u + 1)
                if u == 0:
                    dve.wait_ge(act_step, 2)
                step(dve.tensor_tensor_scan(O[:, 1:S + 1], wneg[:, c:c + 1].to_broadcast([P, S]), k, START,
                                            ALU.add, ALU.max))
                settle()
                stt(z, k, par[:, P_TF + c:P_TF + c + 1], O[:, 0:S], ALU.add, ALU.subtract)
                zs = step(tt(t1, O[:, 0:S], O[:, 1:S + 1], ALU.subtract))
                tt(t2, k, O[:, 1:S + 1], ALU.subtract).then_inc(exparg_ready, 2)
                settle(zs)
                ts_(rz, z, 0.0, None, ALU.max).then_inc(exparg_ready, 1)
                ts_(mz, z, 0.0, None, ALU.min).then_inc(exparg_ready, 1)
                dve.wait_ge(kvr_ready, 3 * u + 2)
                dve.wait_ge(exp_ready, 4 * u + 2)
                step(tt(Bv, t2, v, ALU.mult))
                dve.tensor_tensor_scan(Q[:, 1:S + 1], t1, t2, 0.0, ALU.mult, ALU.add)
                settle()
                step(dve.tensor_tensor_scan(PP[:, 1:S + 1], t1, Bv, 0.0, ALU.mult, ALU.add))
                dve.wait_ge(exp_ready, 4 * u + 4)
                settle()
                tt(z, rz, PP[:, 0:S], ALU.mult)
                step(tt(Bv, mz, v, ALU.mult))
                step(tt(rz, rz, Q[:, 0:S], ALU.mult))
                settle()
                tt(z, z, Bv, ALU.add)
                step(tt(rz, rz, mz, ALU.add))
                settle()
                dve.wait_ge(kvr_ready, 3 * u + 3)
                step(stt(rz, e, 1.0, rz, ALU.add, ALU.mult))
                settle()
                step(dve.reciprocal(t2, rz))
                settle()
                dve.wait_ge(rvk_done, 3 * CT * (b + 1))
                tt(hT[:, c, b * S:(b + 1) * S], z, t2, ALU.mult).then_inc(yT_ready, 1)

            tmp0 = [z, t1]
            wkv(0)
            wkv(1)
            wkv(2)
            residual(X, 0, modB0[:, 0, 0:C], 1, 1, tmp0)
            layer_norm(2, X, modulate=True)
            wkv(3)
            residual(X, 1, modB0[:, 1, 0:C], 2, 2, tmp0)
            layer_norm(3, X, modulate=True)

            dve.wait_ge(route_in, 32)
            dve.wait_ge(norm_ready, 4)
            dve.memset(gsx[:, :, G:], BIG)
            dve.memset(sfx[:, :, E:], BIG)
            dve.wait_ge(score_ready, 1)
            step(tt(sfc, scores[:, :, :], cbias[:, :].unsqueeze(1).to_broadcast([P, NT, E]), ALU.add))
            settle()
            f4 = sfc.rearrange("p t (g a b) -> p (t g a) b", g=G, a=2)
            fl = lambda v: v.rearrange("p t g a -> p (t g a)")
            tt(fl(hi2), f4[:, :, 0], f4[:, :, 1], ALU.max)
            step(tt(fl(lo2), f4[:, :, 0], f4[:, :, 1], ALU.min))
            settle()
            tt(m1, hi2[:, :, :, 0], hi2[:, :, :, 1], ALU.max)
            tt(m2, hi2[:, :, :, 0], hi2[:, :, :, 1], ALU.min)
            step(tt(m3, lo2[:, :, :, 0], lo2[:, :, :, 1], ALU.max))
            settle()
            step(tt(m2, m2, m3, ALU.max))
            settle()
            step(tt(gsx[:, :, 0:G], m1, m2, ALU.add))
            settle()
            for t in range(NT):
                step(dve.max(gtop[:, t, :], gsx[:, t, :]))
            settle()
            for t in range(NT):
                step(dve.match_replace(grep[:, t, :], gtop[:, t, :], gsx[:, t, :], -BIG))
            settle()
            step(ts_(gmask, grep[:, :, 0:G], -0.5 * BIG, None, ALU.is_lt))
            settle()
            step(ts_(gpen, gmask, -1.0, -NONE, ALU.add, ALU.mult))
            f3 = sfc.rearrange("p t (g a) -> p t g a", g=G)
            bc = lambda v: v.unsqueeze(3).to_broadcast([P, NT, G, EG])
            x3 = sfx[:, :, 0:E].rearrange("p t (g a) -> p t g a", g=G)
            step(tt(x3, f3, bc(gmask), ALU.mult))
            settle()
            step(tt(x3, x3, bc(gpen), ALU.add))
            settle()
            for t in range(NT):
                step(dve.max(stop8[:, t, :], sfx[:, t, :]))
            settle()
            for t in range(NT):
                step(dve.match_replace(srep[:, t, :], stop8[:, t, :], sfx[:, t, :], -BIG))
            settle()
            step(ts_(mask[:, :, :], srep[:, :, 0:E], -0.5 * BIG, None, ALU.is_lt))
            settle()
            dve.tensor_copy(mask16[:, :, :], mask[:, :, :]).then_inc(mask_ready, 1)

            def shared_hidden(b):
                for m in range(SHT):
                    n = SHT * b + m
                    dve.wait_ge(shsil_ready, n + 1)
                    dve.wait_ge(shps_done, 2 * n + 2)
                    if b:
                        dve.wait_ge(shy_done, b)
                    k = SH_ROWS[m]
                    tt(sh_hid[0:k, m, :], sh_sil[0:k, :], bank[3 + 2 * m][0:k, :], ALU.mult).then_inc(shhid_ready, 1)

            shared_hidden(0)

            dve.wait_ge(rank_done, 1)
            step(tt(cmp8[:, :, :], bank[1][:, 0:E].unsqueeze(2).to_broadcast([P, E, G]),
                    con[:, K_THR:K_THR + G].unsqueeze(1).to_broadcast([P, E, G]), ALU.is_gt))
            settle()
            step(dve.tensor_reduce(ntile[:, :], cmp8[:, :, :], AX.X, ALU.add))
            settle()
            step(dve.tensor_tensor_scan(incl[:, :], onesE[:, :], ntile[:, :], 0.0, ALU.mult, ALU.add))
            settle()
            step(tt(base[:, :], incl[:, :], ntile[:, :], ALU.subtract))
            step(ts_(ejcmp[:, :], incl[0:SLOT_TILES, :], par[0:SLOT_TILES, P_J:P_J + 1], None, ALU.is_le))
            settle()
            step(ts_(base[:, :], base[:, :], float(P), 1.0, ALU.mult, ALU.add))
            dve.tensor_reduce(ej[:, :], ejcmp[:, :], AX.X, ALU.add).then_inc(ej_ready, 1)
            settle()
            step(tt(pos[:, :, :], bank[0][:, 0:NT * E].rearrange("p (t e) -> p t e", t=NT),
                    base[:, :].unsqueeze(1).to_broadcast([P, NT, E]), ALU.add))
            settle()
            step(tt(pos[:, :, :], pos[:, :, :], mask[:, :, :], ALU.mult))
            settle()
            for t in range(NT):
                step(dve.max(ptop[:, t, :], pos[:, t, :]))
            settle()
            step(ts_(pidx[:, :, :], ptop[:, :, :], -1.0, 0.0, ALU.add, ALU.max))
            settle()
            ts_(pint[:, 0, :, :], pidx[:, :, :], 7, None, ALU.arith_shift_right)
            step(ts_(pint[:, 1, :, :], pidx[:, :, :], P - 1, None, ALU.bitwise_and))
            settle()
            step(dve.tensor_copy(pflt[:, :, :, :], pint[:, :, :, :]))
            dve.wait_ge(ejT_done, 1)
            ts_(eoff[:, :], bank[1][0:1, 64:64 + SLOT_TILES], float(E - 1), None, ALU.min).then_inc(eoff_ready, 1)
            settle()
            n = 0
            for t in range(NT):
                for k in range(TOPK):
                    if n >= 4:
                        dve.wait_ge(onehot_used, n - 3)
                    ts_(onehot_s[:, n % 4, :], iota16[:, :], pflt[:, 1, t, k:k + 1], None, ALU.is_equal)
                    ts_(onehot_j[:, n % 4, :], iota16[:, 0:SLOT_TILES], pflt[:, 0, t, k:k + 1],
                        par[:, P_TOK + t:P_TOK + t + 1], ALU.is_equal, ALU.mult).then_inc(onehot_ready, 1)
                    n += 1
                if t == 3:
                    shared_hidden(1)
            dve.wait_ge(onehot_used, n)
            dve.tensor_copy(gidx[:, :], bank[1][:, 128:128 + SLOT_TILES]).then_inc(gidx_ready, 1)
            eq, eqs = srep[:, :, 0:E], sfx[:, :, 0:E]
            for k in range(TOPK):
                step(tt(eq, pos[:, :, :], ptop[:, :, k:k + 1].to_broadcast([P, NT, E]), ALU.is_equal))
                settle()
                step(tt(eqs, eq, scores[:, :, :], ALU.mult))
                settle()
                step(dve.tensor_reduce(wk[:, :, k], eqs, AX.X, ALU.add))
                settle()

            def copy_h(q, r):
                dve.wait_ge(th_done, 4 * q + (r + 1))
                if not early(q, r, 2):
                    dve.wait_ge(dn_done, 4 * q + (r - 1))
                dve.tensor_copy(hidT[r % 2], bank[4 + r % 2][0:MH, 0:2 * P]).then_inc(hidT_ready, 1)

            def tile_hidden(q, r):
                dve.wait_ge(sil_ready, 4 * q + (r + 1))
                if not early(q, r, 2):
                    dve.wait_ge(th_done, 4 * q + (r - 1))
                tt(hid[r % 2], sil[r % 2], bank[2 + r % 2][:, M:2 * M], ALU.mult).then_inc(hid_ready, 1)

            def copy_y(q, r):
                dve.wait_ge(dn_done, 4 * q + (r + 1))
                if not early(q, r, 2):
                    dve.wait_ge(y_out[r % 2], 16 * (2 * q + r // 2))
                dve.tensor_copy(yt[r % 2], bank[6 + r % 2][:, 0:C]).then_inc(y_ready, 1)

            def tile_step(q, r, first=False):
                if not first:
                    copy_h(*near(q, r, -1))
                tile_hidden(q, r)
                if not first:
                    copy_y(*near(q, r, -1))

            for r in range(4):
                tile_step(0, r, first=(r == 0))
            with dve.Fori(1, SLOT_TILES // 4) as q:
                for r in range(4):
                    tile_step(q, r)
            copy_h(SLOT_TILES // 4 - 1, 3)
            copy_y(SLOT_TILES // 4 - 1, 3)

            mod_rows(1, modrow1)
            mod_cols(1, ((SA, CA), (SB, CB)))
            dve.wait_ge(act_step, 6)
            step(tt(sp[:, 3, :], sp[:, 3, :], sp[:, 1, :], ALU.add))
            settle()
            ts_(sp[:, 4, :], sp[:, 3, :], -8.0, None, ALU.mult)
            ts_(sp[:, 5, :], sp[:, 3, :], -16.0, None, ALU.mult).then_inc(sp_ready, 1)
            dve.wait_ge(had_ready, 4)
            src, dst = f2a, f2b
            for w in (1, 2, 4):
                s5 = src.rearrange("p (i a j) c -> p i a (j c)", a=2, j=w)
                d5 = dst.rearrange("p (i a j) c -> p i a (j c)", a=2, j=w)
                ins = [tt(d5[:, :, 0, :], s5[:, :, 0, :], s5[:, :, 1, :], ALU.add),
                       tt(d5[:, :, 1, :], s5[:, :, 0, :], s5[:, :, 1, :], ALU.subtract)]
                if w < 4:
                    step(ins[1])
                    settle()
                else:
                    ins[1].then_inc(f2_ready, 1)
                src, dst = dst, src
            dve.wait_ge(modB_in[1], 16 * 2 * B)
            g4 = modB1.rearrange("p b n -> p (b n)")
            gate_floor(g4, fhid[:, 0:2, :].rearrange("p h n -> p (h n)"), fhid[:, 2:4, :].rearrange("p h n -> p (h n)"))
            settle()

            def combine(t):
                dve.wait_ge(yg_in[t % 2], 16 * TOPK * (t // 2 + 1))
                acc = shared_y[:, t, :]
                for k in range(TOPK):
                    step(stt(acc, yg[t % 2][:, k, :], wk[:, t, k:k + 1], acc, ALU.mult, ALU.add))
                    settle()
                step(tt(acc, acc, gb0[:, t // TB, :], ALU.mult))
                settle()
                tt(X2[:, t, :], X2[:, t, :], acc, ALU.add).then_inc(comb_done, 1)
                dve.wait_ge(comb_done, t + 1)

            def recurrence(b):
                for m in range(RT):
                    pass
                dve.wait_ge(a2_ready, RT * (b + 1))
                for v in (a2[:, 0:2, :], a2[0:64, 2, :]):
                    ts_(v, v, 1.0, None, ALU.min).then_inc(a2min_ready, 1)
                dve.wait_ge(gates_ready, 2 * RT * (b + 1))
                for rows, ms in ((P, slice(0, 2)), (64, slice(2, 3))):
                    ins = tt(iS[0:rows, ms, :], iS[0:rows, ms, :], hc[0:rows, ms, :], ALU.mult)
                ins.then_inc(ix_ready, 1)
                dve.wait_ge(ix_ready, b + 1)
                dve.wait_ge(mult_ready, 2 * (b + 1))
                for rows, ms in ((P, slice(0, 2)), (64, slice(2, 3))):
                    last = step(tt(iS[0:rows, ms, :], iS[0:rows, ms, :], a2[0:rows, ms, :], ALU.mult))
                settle()
                if b:
                    dve.wait_ge(proj_done, 3)
                dve.wait_ge(a_ready, RT * (b + 1))
                for m in range(RT):
                    n = R_ROWS[m]
                    dve.tensor_tensor_scan(hs[0:n, m, :], aS[0:n, m, :], iS[0:n, m, :], 0.0, ALU.mult, ALU.add)\
                       .then_inc(hs_ready, 1)

            def ffn_hidden(b):
                for h in range(HT):
                    n = HT * b + h
                    dve.wait_ge(fsil_ready, n + 1)
                    dve.wait_ge(fps_done, 2 * n + 2)
                    if b and h == 0:
                        dve.wait_ge(proj_done, 4)
                    tt(fhid[:, h, :], fsil[n % 2], bank[3 + 2 * (n % 3)][:, :], ALU.mult).then_inc(fhid_ready, 1)

            dve.wait_ge(x1_in, 16)
            tmp1 = [yg[0].rearrange("p k c -> p (k c)")[:, i * S:(i + 1) * S] for i in range(2)]
            for b in range(B):
                for t in range(b * TB, (b + 1) * TB):
                    combine(t)
                layer_norm(4 + b, X2)
            ga1 = lambda b: modB1[:, b, 0:C]
            gb1 = lambda b: modB1[:, b, C:2 * C]
            recurrence(0)
            residual(X2, 0, ga1(0), 3, 3, tmp1)
            layer_norm(6, X2)
            recurrence(1)
            ffn_hidden(0)
            residual(X2, 0, gb1(0), 4, 4, tmp1)
            residual(X2, 1, ga1(1), 5, 5, tmp1)
            layer_norm(7, X2)
            ffn_hidden(1)
            residual(X2, 1, gb1(1), 6, 6, tmp1)


def early(q, r, n):
    return isinstance(q, int) and 4 * q + r < n


def near(q, r, d):
    return q + (r + d) // 4, (r + d) % 4


def _cols(a, rows=P):
    n = -(-a.shape[0] // rows) * rows
    padded = np.zeros((n,) + a.shape[1:], a.dtype)
    padded[:a.shape[0]] = a
    return np.ascontiguousarray(np.moveaxis(padded.reshape((n // rows, rows) + a.shape[1:]), 0, 1))


def _flat(a):
    return np.ascontiguousarray(a.reshape(a.shape[0], -1))


def _hadamard(n):
    h = np.ones((1, 1), np.float32)
    while h.shape[0] < n:
        h = np.block([[h, h], [h, -h]])
    return h


def _lay_out(i):
    f = np.float32
    small = np.zeros((P, P_COLS), f)
    for col, a in ((P_TD, i["L0_attn_time_decay"]), (P_TF, i["L0_attn_time_first"]), (P_B1, i["L1_attn_b1"]),
                   (P_CB, i["L1_attn_conv_b"]), (P_BA, i["L1_attn_ba"]), (P_LAM, i["L1_attn_lam"])):
        c = _cols(a)
        small[:, col:col + c.shape[1]] = c
    bx = i["L1_attn_bx"]
    small[:, P_BX:P_BX + 2] = _cols(bx[:2 * P])
    small[64:128, P_BX + 2] = bx[2 * P:]
    for col, c in ((P_C0, i["L0_c"]), (P_C1, i["L1_c"])):
        small[:, col:col + CT * B] = _flat(_cols(np.ascontiguousarray(c.T)))
    small[:, P_TOK:P_TOK + NT] = np.arange(NT * P, dtype=f).reshape(NT, P).T
    small[:, P_J] = np.arange(P, dtype=f)
    consts = np.zeros((P, K_COLS), f)
    consts[:, K_ID:K_ID + P] = np.eye(P)
    consts[:, K_TRI:K_TRI + P] = np.triu(np.ones((P, P)), 1)
    consts[:, K_HAD:K_HAD + P] = _hadamard(P) / 32.0
    consts[:, K_IOTA:K_IOTA + P] = np.arange(P)
    consts[:, K_THR:K_THR + G] = np.arange(G) * P
    gate, up, down = i["L0_ffn_gate_w"], i["L0_ffn_up_w"], i["L0_ffn_down_w"]
    gu = np.concatenate([gate, up], axis=2)
    gu = np.ascontiguousarray(gu.reshape(E, CT, P, 2 * M).transpose(2, 0, 1, 3)).reshape(P, -1)
    dn = np.ascontiguousarray(down.reshape(E, 2, MH, C).transpose(2, 0, 1, 3)).reshape(MH, -1)
    wa, wx = i["L1_attn_wa"].T, i["L1_attn_wx"].T
    gates = np.concatenate([wa[:, :2 * P], wx[:, :2 * P], wa[:, 2 * P:], wx[:, 2 * P:]], axis=1)
    w2 = np.concatenate([i["L1_attn_w2"].T, i["L1_attn_b2"][None]], axis=0)
    return {
        "x": i["L0_attn_x"].reshape(B * S, C),
        "small": small, "consts": consts,
        "wmod0": _cols(i["L0_wmod"]), "wmod1": _cols(i["L1_wmod"]),
        "w_rvk": _cols(i["L0_attn_W_rvk"].T), "w_out": _cols(i["L0_attn_W_out"].T),
        "w_router": _cols(i["L0_ffn_w_router"]),
        "corr_bias": np.ascontiguousarray(np.broadcast_to(i["L0_ffn_corr_bias"], (P, E))),
        "w_gu": gu, "w_dn": dn,
        "w_shgu": _cols(np.concatenate([i["L0_ffn_sh_gate_w"], i["L0_ffn_sh_up_w"]], axis=1)),
        "w_shdn": _cols(i["L0_ffn_sh_down_w"]),
        "w_1": _cols(i["L1_attn_w1"].T),
        "w_conv": _flat(_cols(i["L1_attn_conv_w"].transpose(1, 2, 0))),
        "w_gates": _cols(gates), "w_2": _cols(w2),
        "w_f13": _cols(np.concatenate([i["L1_ffn_W1"].T, i["L1_ffn_W3"].T], axis=1)),
        "w_f2": _cols(i["L1_ffn_W2"].T),
    }


def kernel(**inputs):
    import concourse.bacc as bacc
    from concourse.bass_utils import run_bass_kernel_spmd

    arrays = {n: np.ascontiguousarray(a) for n, a in _lay_out({k: np.asarray(v) for k, v in inputs.items()}).items()}
    nc = bacc.Bacc("TRN2", target_bir_lowering=False, num_devices=1)
    args = [nc.dram_tensor(n, a.shape, mybir.dt.from_np(a.dtype), kind="ExternalInput").ap() for n, a in arrays.items()]
    out = nc.dram_tensor("out", (B * S, C), F32, kind="ExternalOutput").ap()
    two_layers(nc, *args, out)
    r = run_bass_kernel_spmd(nc, [arrays], core_ids=[0])
    return r.results[0]["out"].reshape(B, S, C)
```

```python
from contextlib import ExitStack

import numpy as np

import concourse.bass as bass
from concourse import mybir

F32 = mybir.dt.float32
F16 = mybir.dt.float16
BF16 = mybir.dt.bfloat16
I32 = mybir.dt.int32
U32 = mybir.dt.uint32
ALU = mybir.AluOpType
ACT = mybir.ActivationFunctionType
AX = mybir.AxisListType

P = 128
B = 2
S = 512
C = 256
CT = C // P
NT = B * S // P
TB = S // P
E = 32
G = 8
EG = E // G
TOPG = 4
TOPK = 6
M = 176
MH = M // 2
SHM = 2 * M
SHT = 3
SH_ROWS = [P, P, SHM - 2 * P]
SLOT_TILES = 80
QUADS = SLOT_TILES // 4
SURE_QUADS = B * S * TOPK // (4 * P)
R = 320
RT = 3
R_ROWS = [P, P, R - 2 * P]
TAPS = 4
PAD = 3
H = 1024
HT = H // P
EPS = 1e-5
BIG = 3.0e38
NONE = -1.0e30
START = -1.0e38

(P_TD, P_TF, P_B1, P_CB, P_BA, P_BX, P_LAM, P_C0, P_C1, P_TOK, P_J, P_ZERO) = (
    0, 2, 4, 7, 10, 13, 17, 20, 24, 28, 36, 37)
P_COLS = 40
K_ID, K_TRI, K_HAD, K_IOTA, K_THR = 0, P, 2 * P, 3 * P, 4 * P
K_COLS = 4 * P + G
SA, CA, GA, SB, CB, GB = range(6)


def two_layers(nc, x_in, small, consts, wmod0, wmod1, w_rvk, w_out, w_router, corr_bias,
               w_gu, w_dn, w_shgu, w_shdn, w_1, w_conv, w_gates, w_2, w_f13, w_f2, out):
    mod_dram = [nc.dram_tensor(f"mod_dram{i}", (B, 6 * C), F32, kind="Internal").ap() for i in range(2)]
    h2_dram = nc.dram_tensor("h2_dram", (B * S, C), F32, kind="Internal").ap()
    x1_dram = nc.dram_tensor("x1_dram", (P, NT * C), F32, kind="Internal").ap()
    y_dram = nc.dram_tensor("y_dram", (SLOT_TILES * P, C), F32, kind="Internal").ap()

    with ExitStack() as ctx:
        def sb(name, shape, dt=F32):
            return ctx.enter_context(nc.sbuf_tensor(name, shape, dt))

        def sem(name):
            return ctx.enter_context(nc.semaphore(name))

        bank = [ctx.enter_context(nc.psum_tensor(f"bank{i}", [P, 512], F32)) for i in range(8)]

        GUW, DNW = 4 * M, 2 * C
        DN0 = E * GUW
        arena = sb("arena", [P, E * (GUW + DNW)])
        gu = arena[:, 0:DN0]
        dn = arena[0:MH, DN0:DN0 + E * DNW]

        def carve(limit, start):
            top = [start]

            def take(n):
                top[0] += n
                assert top[0] <= limit, (top[0], limit)
                return arena[:, top[0] - n:top[0]]
            return take

        par = sb("par", [P, P_COLS])
        con = sb("con", [P, K_COLS])
        ident = con[:, K_ID:K_ID + P]
        norm = sb("norm", [P, NT, C])
        shared_y = norm
        actT_all = sb("hT", [P, CT, B * S])
        hT = actT_all
        stats = sb("stats", [P, NT, 6])
        mv = sb("mv", [P, NT, 2])
        ve = sb("ve", [P, NT])
        rstd = sb("rstd", [P, NT])
        mhalf = sb("mhalf", [P, NT])
        silc = sb("silc", [P, 8])
        modcol = sb("modcol", [P, 2, 6 * CT, B])
        wneg = sb("wneg", [P, CT])
        gb0 = sb("gb0", [P, B, C])
        shgu = sb("shgu", [P, CT, 2 * SHM])
        shdn = sb("shdn", [P, SHT, C])
        router = sb("router", [P, CT, E])
        cbias = sb("cbias", [P, E])

        TW = 4 * C + 2 * C + 2 * 2 * M + 2 * C + 2 * C
        tile_mem = sb("tile_mem", [P, TW])
        o = 0
        xg = [tile_mem[:, o + i * C:o + (i + 1) * C] for i in range(4)]; o += 4 * C
        xgT = [tile_mem[:, o + i * C:o + (i + 1) * C] for i in range(2)]; o += 2 * C
        sil = [tile_mem[:, o + i * M:o + (i + 1) * M] for i in range(2)]; o += 2 * M
        hid = [tile_mem[:, o + i * M:o + (i + 1) * M] for i in range(2)]; o += 2 * M
        hidT = [tile_mem[0:MH, o + i * 2 * P:o + (i + 1) * 2 * P] for i in range(2)]; o += 2 * C
        yt = [tile_mem[:, o + i * C:o + (i + 1) * C] for i in range(2)]; o += 2 * C
        modrow0 = tile_mem[0:B, 0:6 * C]
        modB0 = tile_mem[:, 6 * C:6 * C + B * 3 * C].rearrange("p (b n) -> p b n", b=B)
        sh_hid = tile_mem[:, 0:SHT * S].rearrange("p (m n) -> p m n", m=SHT)
        sh_sil = tile_mem[:, SHT * S:(SHT + 1) * S]

        scores = sb("scores", [P, NT, E])
        o = (SHT + 1) * S

        def temp(*shape):
            nonlocal o
            n = NT * int(np.prod(shape))
            o += n
            assert o <= TW
            names = "abc"[:len(shape)]
            return tile_mem[:, o - n:o].rearrange(f"p (t {' '.join(names)}) -> p t {' '.join(names)}",
                                                  t=NT, **dict(zip(names, shape)))
        sfc = temp(E)
        hi2, lo2 = temp(G, 2), temp(G, 2)
        m1, m2, m3 = temp(G), temp(G), temp(G)
        gsx, gtop, grep = temp(G + 8 - TOPG), temp(8), temp(G + 8 - TOPG)
        gmask, gpen = temp(G), temp(G)
        sfx = sb("sfx", [P, NT, E + 8 - TOPK])
        stop8 = sb("stop8", [P, NT, 8])
        srep = sb("srep", [P, NT, E + 8 - TOPK])
        mask = sb("mask", [P, NT, E])
        mask16 = sb("mask16", [P, NT, E], BF16)
        tri16 = sb("tri16", [P, P], BF16)
        ones16 = sb("ones16", [P, P], BF16)
        iota16 = sb("iota16", [P, P], F16)
        cmp8 = sb("cmp8", [P, E, G])
        ntile = sb("ntile", [P, E])
        incl = sb("incl", [P, E])
        onesE = sb("onesE", [P, E])
        base = sb("base", [P, E])
        pos = sb("pos", [P, NT, E])
        ptop = sb("ptop", [P, NT, 8])
        pidx = sb("pidx", [P, NT, 8], I32)
        pint = sb("pint", [P, 2, NT, 8], I32)
        pflt = sb("pflt", [P, 2, NT, 8])
        wk = sb("wk", [P, NT, TOPK])
        onehot_s = sb("onehot_s", [P, 4, P], F16)
        onehot_j = sb("onehot_j", [P, 4, SLOT_TILES + 1], F16)
        ejcmp = sb("ejcmp", [SLOT_TILES, E])
        ej = sb("ej", [SLOT_TILES, 1])
        eoff = sb("eoff", [1, SLOT_TILES + 8], I32)
        gidx = sb("gidx", [P, SLOT_TILES + 1], U32)
        last_quad = sb("last_quad", [1, 1], I32)
        tile_idx = [sb(f"tile_idx{i}", [P, 1], U32) for i in range(4)]

        EARLY = 14
        take = carve(DN0, EARLY * GUW)
        X = take(NT * C).rearrange("p (t c) -> p t c", t=NT)
        rvk = take(CT * 3 * C).rearrange("p (k n) -> p k n", k=CT)
        wout = take(CT * C).rearrange("p (k n) -> p k n", k=CT)
        kS = [take(S) for _ in range(2)]
        vS = [take(S) for _ in range(2)]
        er = [take(S) for _ in range(2)]
        O = take(S + 1)
        Q = take(S + 1)
        PP = take(S + 1)
        z, t1, t2, rz, mz, Bv = [take(S) for _ in range(6)]
        wm0 = arena[:, DN0 - 6 * C * CT:DN0].rearrange("p (k n) -> p k n", k=CT)

        take1 = carve(E * (GUW + DNW), 0)
        X2 = take1(NT * C).rearrange("p (t c) -> p t c", t=NT)
        YG = 4
        w1 = take1(CT * R).rearrange("p (k n) -> p k n", k=CT)
        w2 = take1(RT * C).rearrange("p (i n) -> p i n", i=RT)
        assert NT * C + CT * R + RT * C <= SURE_QUADS // 2 * GUW
        yg_mem = [take1(TOPK * C) for _ in range(YG)]
        yg = [m.rearrange("p (k c) -> p k c", k=TOPK) for m in yg_mem]
        wm1_mem = take1(CT * 6 * C + 6 * C)
        wm1 = wm1_mem[:, 0:CT * 6 * C].rearrange("p (k n) -> p k n", k=CT)
        modrow1 = wm1_mem[0:B, CT * 6 * C:]
        fhid = wm1_mem[:, 0:HT * S].rearrange("p (h n) -> p h n", h=HT)
        modB1 = take1(B * 2 * C).rearrange("p (b n) -> p b n", b=B)
        wconv = take1(RT * TAPS * R).rearrange("p (i k n) -> p i k n", i=RT, k=TAPS)
        wgate = take1(RT * 2 * R).rearrange("p (i n) -> p i n", i=RT)
        f13 = take1(CT * 2 * H).rearrange("p (k n) -> p k n", k=CT)
        f2 = take1(HT * C).rearrange("p (h n) -> p h n", h=HT)
        f2a = take1(HT * C).rearrange("p (h n) -> p h n", h=HT)
        f2b = f2
        h1 = take1(RT * (S + 2 * PAD)).rearrange("p (i n) -> p i n", i=RT)
        hc = take1(RT * S).rearrange("p (i n) -> p i n", i=RT)
        rS = take1(RT * S).rearrange("p (i n) -> p i n", i=RT)
        iS = take1(RT * S).rearrange("p (i n) -> p i n", i=RT)
        aS, a2 = [m[:, 0:RT * S].rearrange("p (i n) -> p i n", i=RT) for m in yg_mem[2:4]]
        hs = take1(RT * S).rearrange("p (i n) -> p i n", i=RT)
        fsil = [tile_mem[:, i * S:(i + 1) * S] for i in range(2)]
        sp = sb("sp", [P, 6, RT])

        par_in, wm0_in, rvk_in, wout_in, route_in, sh_in = [sem(n) for n in (
            "par_in", "wm0_in", "rvk_in", "wout_in", "route_in", "sh_in")]
        x_in_s = [sem(f"x_in{b}") for b in range(B)]
        gu_early, gu_late, dn_in = sem("gu_early"), sem("gu_late"), sem("dn_in")
        y_filled = sem("y_filled")
        quads_ready = sem("quads_ready")
        mod_out = [sem(f"mod_out{i}") for i in range(2)]
        modB_in = [sem(f"modB_in{i}") for i in range(2)]
        h2_out, x1_out, x1_in = sem("h2_out"), sem("x1_out"), sem("x1_in")
        xg_in = [sem(f"xg_in{i}") for i in range(4)]
        y_out = [sem(f"y_out{i}") for i in range(2)]
        yg_in = [sem(f"yg_in{i}") for i in range(YG)]
        wm1_in, w1_in, conv_in, gate_in, w2_in, f13_in, f2_in, out_out = [sem(n) for n in (
            "wm1_in", "w1_in", "conv_in", "gate_in", "w2_in", "f13_in", "f2_in", "out_out")]
        act_step, dve_step, pool_step = sem("act_step"), sem("dve_step"), sem("pool_step")
        silc_ready = sem("silc_ready")
        modps_done = sem("modps_done")
        modrow_ready = sem("modrow_ready")
        modT_done = sem("modT_done")
        modcol_ready = sem("modcol_ready")
        modB_ready = sem("modB_ready")
        ve_ready, rstd_ready = sem("ve_ready"), sem("rstd_ready")
        norm_ready = sem("norm_ready")
        normT_done = sem("normT_done")
        hT_ready = sem("hT_ready")
        rvk_done = sem("rvk_done")
        kvr_ready = sem("kvr_ready")
        exparg_ready = sem("exparg_ready")
        exp_ready = sem("exp_ready")
        yT_ready = sem("yT_ready")
        proj_done = sem("proj_done")
        x_done = sem("x_done")
        logit_done, score_ready = sem("logit_done"), sem("score_ready")
        mask_ready, rank_done = sem("mask_ready"), sem("rank_done")
        ej_ready, ejT_done, eoff_ready = sem("ej_ready"), sem("ejT_done"), sem("eoff_ready")
        onehot_ready, onehot_used = sem("onehot_ready"), sem("onehot_used")
        gidx_ready = sem("gidx_ready")
        shps_done, shsil_ready, shhid_ready = sem("shps_done"), sem("shsil_ready"), sem("shhid_ready")
        shy_done, shy_ready = sem("shy_done"), sem("shy_ready")
        tx_done, xgT_ready, gu_done, sil_ready, hid_ready, th_done, hidT_ready, dn_done, y_ready = [
            sem(n) for n in ("tx_done", "xgT_ready", "gu_done", "sil_ready", "hid_ready", "th_done",
                             "hidT_ready", "dn_done", "y_ready")]
        tile_idx_ready, gathers_begun = sem("tile_idx_ready"), sem("gathers_begun")
        comb_done = sem("comb_done")
        w1_done, h1_ready, conv_done, hc_ready = [sem(n) for n in (
            "w1_done", "h1_ready", "conv_done", "hc_ready")]
        gates_done, gates_ready, a_ready, a2_ready, mult_ready, hs_ready = [sem(n) for n in (
            "gates_done", "gates_ready", "a_ready", "a2_ready", "mult_ready", "hs_ready")]
        had_done, had_ready, f2_ready = sem("had_done"), sem("had_ready"), sem("f2_ready")
        mhalf_ready, sp_ready, pads_ready, ix_ready, a2min_ready = [sem(n) for n in (
            "mhalf_ready", "sp_ready", "pads_ready", "ix_ready", "a2min_ready")]
        fps_done, fsil_ready, fhid_ready = sem("fps_done"), sem("fsil_ready"), sem("fhid_ready")

        def counter(eng, s):
            n = [0]

            def step(ins):
                ins.then_inc(s, 1)
                n[0] += 1
                return n[0]

            def settle(k=None):
                eng.wait_ge(s, n[0] if k is None else k)
            return step, settle

        def load_last(eng):
            eng.wait_ge(quads_ready, 1)
            return eng.value_load(last_quad[0:1, 0:1], min_val=SURE_QUADS - 1, max_val=QUADS - 1)

        block = ctx.enter_context(nc.Block())

        @block.sync
        def _(sp_):
            sp_.dma_start(par[:, :], small).then_inc(par_in, 16)
            sp_.dma_start(con[:, :], consts).then_inc(par_in, 16)
            xv = x_in.rearrange("(t p) c -> p t c", p=P)
            sp_.dma_start(X[:, 0:TB, :], xv[:, 0:TB, :]).then_inc(x_in_s[0], 16)
            sp_.dma_start(wm0, wmod0).then_inc(wm0_in, 16)
            sp_.dma_start(X[:, TB:NT, :], xv[:, TB:NT, :]).then_inc(x_in_s[1], 16)
            sp_.dma_start(rvk, w_rvk).then_inc(rvk_in, 16)
            sp_.dma_start(wout, w_out).then_inc(wout_in, 16)
            sp_.dma_start(router[:, :, :], w_router).then_inc(route_in, 16)
            sp_.dma_start(cbias[:, :], corr_bias).then_inc(route_in, 16)
            sp_.dma_start(shgu[:, :, :], w_shgu).then_inc(sh_in, 16)
            sp_.dma_start(shdn[:, :, :], w_shdn).then_inc(sh_in, 16)

            sp_.wait_ge(modrow_ready, 3)
            sp_.dma_start(mod_dram[0], modrow0).then_inc(mod_out[0], 16)
            sp_.wait_ge(mod_out[0], 16)
            for b in range(B):
                for dst, chunk in ((modB0[:, b, 0:C], GA), (modB0[:, b, C:3 * C], SB), (gb0[:, b, :], GB)):
                    n = dst.shape[-1]
                    src = mod_dram[0][b:b + 1, chunk * C:chunk * C + n].to_broadcast([P, n])
                    sp_.dma_start(dst, src).then_inc(modB_in[0], 16)

            guv = w_gu.rearrange("p (e n) -> p e n", e=E)
            step_e = 7
            for e in range(0, EARLY, step_e):
                sp_.dma_start(gu[:, e * GUW:(e + step_e) * GUW], guv[:, e:e + step_e, :].rearrange("p e n -> p (e n)")).then_inc(gu_early, 16)
            for e in range(0, E, 8):
                sp_.dma_start(dn[:, e * DNW:(e + 8) * DNW], w_dn[:, e * DNW:(e + 8) * DNW]).then_inc(dn_in, 16)

            h2v = h2_dram.rearrange("(t p) c -> p t c", p=P)
            for b in range(B):
                sp_.wait_ge(x_done, b + 1)
                sp_.dma_start(x1_dram[:, b * TB * C:(b + 1) * TB * C],
                              X[:, b * TB:(b + 1) * TB, :].rearrange("p t c -> p (t c)")).then_inc(x1_out, 16)
                sp_.wait_ge(norm_ready, B + b + 1)
                sp_.dma_start(h2v[:, b * TB:(b + 1) * TB, :], norm[:, b * TB:(b + 1) * TB, :]).then_inc(h2_out, 16)
            sp_.wait_ge(x1_out, 16 * B)
            for e in range(EARLY, E, 6):
                sp_.dma_start(gu[:, e * GUW:(e + 6) * GUW], w_gu[:, e * GUW:(e + 6) * GUW]).then_inc(gu_late, 16)

            def store(j, r):
                sp_.wait_ge(y_ready, j + 1)
                dst = y_dram.rearrange("(j p) c -> j p c", p=P)[bass.ds(j, 1), :, :]
                sp_.dma_start(dst.rearrange("a p c -> p (a c)"), yt[r % 2]).then_inc(y_out[r % 2], 16)

            last_q = load_last(sp_)
            with sp_.Fori(SURE_QUADS, QUADS) as q:
                with sp_.If(q <= last_q):
                    sp_.sem_inc(y_filled, 16)
                with sp_.Else():
                    dst = y_dram.rearrange("(q r p) c -> q p r c", r=4, p=P)[bass.ds(q, 1), :, :, :]
                    sp_.dma_start(dst.rearrange("a p r c -> p (a r) c"),
                                  con[:, 0:C].unsqueeze(1).to_broadcast([P, 4, C])).then_inc(y_filled, 16)
            with sp_.Fori(0, SURE_QUADS) as q:
                for r in range(4):
                    store(4 * q + r, r)
            sp_.wait_ge(dn_done, 4 * SURE_QUADS)
            sp_.dma_start(X2.rearrange("p t c -> p (t c)"), x1_dram).then_inc(x1_in, 16)
            sp_.dma_start(w1, w_1).then_inc(w1_in, 16)
            sp_.dma_start(w2, w_2).then_inc(w2_in, 16)
            with sp_.Fori(SURE_QUADS, QUADS) as q:
                with sp_.If(q <= last_q):
                    for r in range(4):
                        store(4 * q + r, r)

            sp_.wait_ge(dn_done, 4 * last_q + 4)
            for k in range(CT):
                sp_.dma_start(wm1[:, k, :], wmod1[:, k, :]).then_inc(wm1_in, 16)
            sp_.dma_start(f2[:, 0:4, :], w_f2[:, 0:4, :]).then_inc(f2_in, 16)
            sp_.dma_start(f2[:, 4:8, :], w_f2[:, 4:8, :]).then_inc(f2_in, 16)
            for i in range(RT):
                sp_.dma_start(wconv[:, i, :, :], w_conv[:, i, :, :]).then_inc(conv_in, 16)
            sp_.wait_ge(modrow_ready, 6)
            sp_.dma_start(mod_dram[1], modrow1).then_inc(mod_out[1], 16)
            sp_.wait_ge(mod_out[1], 16)
            for b in range(B):
                for i, chunk in enumerate((GA, GB)):
                    src = mod_dram[1][b:b + 1, chunk * C:(chunk + 1) * C].to_broadcast([P, C])
                    sp_.dma_start(modB1[:, b, i * C:(i + 1) * C], src).then_inc(modB_in[1], 16)
            for i in range(RT):
                sp_.dma_start(wgate[:, i, :], w_gates[:, i, :]).then_inc(gate_in, 16)
            sp_.wait_ge(comb_done, NT)
            sp_.dma_start(f13, w_f13).then_inc(f13_in, 16)

            ov = out.rearrange("(t p) c -> p t c", p=P)
            for b in range(B):
                sp_.wait_ge(x_done, 2 * B + b + 1)
                sp_.dma_start(ov[:, b * TB:(b + 1) * TB, :], X2[:, b * TB:(b + 1) * TB, :]).then_inc(out_out, 16)
            sp_.wait_ge(out_out, 16 * B)

        @block.tensor
        def _(pe):
            def mod_rows(layer):
                pe.wait_ge(silc_ready, 1)
                pe.wait_ge((wm0_in, wm1_in)[layer], (16, 16 * CT)[layer])
                wm = (wm0, wm1)[layer]
                for n in range(3):
                    for k in range(CT):
                        mm = pe.matmul(bank[2 + n][0:B, :], silc[:, 4 * layer + B * k:4 * layer + B * (k + 1)],
                                       wm[:, k, n * 512:(n + 1) * 512], start=(k == 0), stop=(k == CT - 1))
                    mm.then_inc(modps_done, 1)

            def mod_cols(layer, chunks, row):
                pe.wait_ge(modrow_ready, 3 * layer + 3)
                for n in chunks:
                    for h in range(CT):
                        j = CT * n + h
                        mm = pe.transpose(bank[5][:, B * j:B * (j + 1)], row[:, j * P:(j + 1) * P], ident[0:B, 0:B])
                mm.then_inc(modT_done, 1)

            def transposes(n, b, wait_free):
                pe.wait_ge(norm_ready, n + 1)
                if wait_free is not None:
                    pe.wait_ge(*wait_free)
                for c in range(CT):
                    for t in range(TB):
                        mm = pe.transpose(bank[c][:, t * P:(t + 1) * P], norm[:, b * TB + t, c * P:(c + 1) * P], ident)
                    mm.then_inc(normT_done, 1)

            def project(src, w, ks, b, rows):
                for t in range(TB):
                    for k in range(ks):
                        mm = pe.matmul(bank[t // 2][:, (t % 2) * C:(t % 2 + 1) * C], src(k, t), w[0:rows[k], k, :],
                                       start=(k == 0), stop=(k == ks - 1))
                mm.then_inc(proj_done, 1)

            pe.wait_ge(par_in, 32)
            mod_rows(0)
            mod_cols(0, (SA, CA), modrow0)

            for b in range(B):
                transposes(b, b, (hT_ready, CT * b) if b else None)
                pe.wait_ge(hT_ready, CT * (b + 1))
                if b == 0:
                    pe.wait_ge(rvk_in, 16)
                    pe.wait_ge(modrow_ready, 3)
                    pe.wait_ge(modcol_ready, 1)
                for c in range(CT):
                    for i, part in enumerate((2, 1, 0)):
                        m0 = part * C + c * P
                        if b:
                            pe.wait_ge(kvr_ready, 3 * c + i + 1)
                        for k in range(CT):
                            mm = pe.matmul(bank[2 + 3 * c + i][:, :], rvk[:, k, m0:m0 + P],
                                           hT[:, k, b * S:(b + 1) * S], start=(k == 0), stop=(k == CT - 1))
                        mm.then_inc(rvk_done, 1)
            pe.wait_ge(wout_in, 16)
            for b in range(B):
                pe.wait_ge(hT_ready, CT * (B + b))
                pe.wait_ge(yT_ready, CT * (b + 1))
                project(lambda k, t: hT[:, k, b * S + t * P:b * S + (t + 1) * P], wout, CT, b, [P] * CT)
                transposes(B + b, b, (x_done, b + 1))

            pe.wait_ge(route_in, 32)
            pe.wait_ge(hT_ready, CT * 2 * B)
            for t in range(NT):
                for k in range(CT):
                    mm = pe.matmul(bank[0][:, t * E:(t + 1) * E], hT[:, k, t * P:(t + 1) * P], router[:, k, :],
                                   start=(k == 0), stop=(k == CT - 1))
            mm.then_inc(logit_done, 1)

            def shared_in(b):
                if b == 0:
                    pe.wait_ge(sh_in, 32)
                    pe.wait_ge(kvr_ready, 3 * CT * B)
                for m in range(SHT):
                    for h in range(2):
                        c0 = h * SHM + m * P
                        for k in range(CT):
                            mm = pe.matmul(bank[2 + 2 * m + h][0:SH_ROWS[m], :], shgu[:, k, c0:c0 + SH_ROWS[m]],
                                           hT[:, k, b * S:(b + 1) * S], start=(k == 0), stop=(k == CT - 1))
                        mm.then_inc(shps_done, 1)

            def shared_out(b, banks):
                pe.wait_ge(shhid_ready, SHT * (b + 1))
                for t in range(TB):
                    for k in range(SHT):
                        mm = pe.matmul(bank[banks[t // 2]][:, (t % 2) * C:(t % 2 + 1) * C],
                                       sh_hid[0:SH_ROWS[k], k, t * P:(t + 1) * P], shdn[0:SH_ROWS[k], k, :],
                                       start=(k == 0), stop=(k == SHT - 1))
                mm.then_inc(shy_done, 1)

            shared_in(0)
            pe.wait_ge(mask_ready, 1)
            pe.wait_ge(score_ready, 1)
            m16 = mask16[:, :, :].rearrange("p t e -> p (t e)")
            pe.matmul(bank[0][:, 0:NT * E], tri16[:, :], m16, start=True, stop=False, skip_group_check=True)
            for d in range(1, NT):
                pe.matmul(bank[0][:, d * E:NT * E], ones16[:, :], m16[:, 0:(NT - d) * E], start=False,
                          stop=(d == NT - 1), skip_group_check=True)
            for t in range(NT):
                mm = pe.matmul(bank[1][:, 0:E], ones16[:, :], m16[:, t * E:(t + 1) * E], start=(t == 0), stop=(t == NT - 1))
            mm.then_inc(rank_done, 1)
            shared_out(0, (2, 3))
            pe.wait_ge(ej_ready, 1)
            pe.transpose(bank[1][0:1, 256:256 + SLOT_TILES], ej[:, :], ident[0:SLOT_TILES, 0:SLOT_TILES]).then_inc(ejT_done, 1)
            for n in range(NT * TOPK):
                pe.wait_ge(onehot_ready, n + 1)
                pe.matmul(bank[1][:, 128:128 + SLOT_TILES + 1], onehot_s[:, n % 4, :], onehot_j[:, n % 4, :],
                          start=(n == 0), stop=(n == NT * TOPK - 1)).then_inc(onehot_used, 1)

            def tx(q, r):
                pe.wait_ge(xg_in[r], 16 * (q + 1))
                for c in range(CT):
                    mm = pe.transpose(bank[r % 2][:, c * P:(c + 1) * P], xg[r][:, c * P:(c + 1) * P], ident)
                mm.then_inc(tx_done, 1)

            def gate_up(q, r, e):
                pe.wait_ge(xgT_ready, 4 * q + (r + 1))
                for k in range(CT):
                    mm = pe.matmul(bank[2 + r % 2][:, 0:2 * M], xgT[r % 2][:, k * P:(k + 1) * P],
                                   gu[:, bass.ds(e[k], 2 * M)], start=(k == 0), stop=(k == CT - 1))
                mm.then_inc(gu_done, 1)

            def th(q, r):
                pe.wait_ge(hid_ready, 4 * q + (r + 1))
                for k in range(2):
                    mm = pe.transpose(bank[4 + r % 2][0:MH, k * P:(k + 1) * P], hid[r % 2][:, k * MH:(k + 1) * MH], ident)
                mm.then_inc(th_done, 1)

            def down(q, r, e):
                pe.wait_ge(hidT_ready, 4 * q + (r + 1))
                if not early(q, r, 2):
                    pe.wait_ge(y_ready, 4 * q + (r - 1))
                for k in range(2):
                    mm = pe.matmul(bank[6 + r % 2][:, 0:C], hidT[r % 2][:, k * P:(k + 1) * P],
                                   dn[:, bass.ds(e[2 + k], C)], start=(k == 0), stop=(k == 1))
                mm.then_inc(dn_done, 1)

            regs = [pe.alloc_register(f"expert{i}") for i in range(5)]

            def blocks(i):
                e = pe.snap(regs[i], min_val=0, max_val=E - 1)
                return [pe.snap(e * GUW + k * 2 * M) for k in range(CT)] + [pe.snap(e * DNW + k * C) for k in range(2)]

            def quad(q, first=False):
                pe.load(regs[0:4], eoff[0:1, bass.ds(4 * q, 4)])
                e_prev, e_next = blocks(0), blocks(1)
                for r in range(4):
                    e_now = e_next
                    if r == 1:
                        pe.load(regs[4], eoff[0:1, bass.ds(4 * q + 4, 1)])
                    tx(*near(q, r, 1))
                    if not (first and r == 0):
                        th(*near(q, r, -1))
                    gate_up(q, r, e_now)
                    if r < 3:
                        e_next = blocks(r + 2)
                    if not (first and r == 0):
                        down(*near(q, r, -1), e_prev)
                    e_prev = e_now

            pe.wait_ge(eoff_ready, 1)
            pe.wait_ge(gidx_ready, 1)
            pe.wait_ge(shy_ready, 1)
            pe.wait_ge(gu_early, 16 * 2)
            pe.wait_ge(gu_late, 16 * 3)
            pe.wait_ge(dn_in, 16 * 4)
            last_q = load_last(pe)
            tx(0, 0)
            quad(0, first=True)
            with pe.Fori(1, SURE_QUADS) as q:
                quad(q)
            with pe.Fori(SURE_QUADS, QUADS + 1) as q:
                with pe.If(q <= last_q + 1):
                    with pe.If(q <= last_q):
                        quad(q)
                    with pe.If(q == last_q + 1):
                        pe.load(regs[4], eoff[0:1, bass.ds(4 * q, 1)])
                        e = blocks(4)
                        th(*near(q, 0, -1))
                        down(*near(q, 0, -1), e)
                    pe.nop()

            pe.wait_ge(y_ready, 4 * last_q + 4)
            pe.wait_ge(xgT_ready, 4 * last_q + 5)
            shared_in(1)
            pe.wait_ge(shhid_ready, 2 * SHT)
            mod_rows(1)
            shared_out(1, (0, 1))
            mod_cols(1, (SA, CA, SB, CB), modrow1)
            pe.wait_ge(f2_in, 32)
            pe.wait_ge(modrow_ready, 6)
            for h in range(HT):
                mm = pe.matmul(bank[(6, 7, 2, 3)[h // 2]][:, (h % 2) * C:(h % 2 + 1) * C],
                               con[:, K_HAD:K_HAD + P], f2[:, h, :], start=True, stop=True)
                if h % 2:
                    mm.then_inc(had_done, 1)

            def hidden1(b):
                pe.wait_ge(w1_in, 16)
                pe.wait_ge(had_ready, 4)
                pe.wait_ge(modcol_ready, 2)
                pe.wait_ge(hT_ready, CT * (5 + b))
                for m in range(RT):
                    if b:
                        pe.wait_ge(gates_ready, 2 * RT)
                    for k in range(CT):
                        mm = pe.matmul(bank[2 + m][0:R_ROWS[m], :], w1[:, k, m * P:m * P + R_ROWS[m]],
                                       hT[:, k, b * S:(b + 1) * S], start=(k == 0), stop=(k == CT - 1))
                    mm.then_inc(w1_done, 1)

            def conv(b):
                pe.wait_ge(conv_in, 16 * RT)
                pe.wait_ge(h1_ready, RT * (b + 1))
                if b:
                    pe.wait_ge(gates_ready, 2 * RT)
                for m in range(RT):
                    n = 0
                    for i in range(RT):
                        for k in range(TAPS):
                            mm = pe.matmul(bank[5 + m][0:R_ROWS[m], :], wconv[0:R_ROWS[i], i, k, m * P:m * P + R_ROWS[m]],
                                           h1[0:R_ROWS[i], i, 2 * k:2 * k + S], start=(n == 0), stop=(n == RT * TAPS - 1))
                            n += 1
                    mm.then_inc(conv_done, 1)

            def gates(b):
                pe.wait_ge(gate_in, 16 * RT)
                pe.wait_ge(hc_ready, RT * (b + 1))
                for m in range(5):
                    for i in range(RT):
                        mm = pe.matmul(bank[2 + m][:, :], wgate[0:R_ROWS[i], i, m * P:(m + 1) * P],
                                       hc[0:R_ROWS[i], i, :], start=(i == 0), stop=(i == RT - 1))
                    mm.then_inc(gates_done, 1)

            def recur_out(b):
                pe.wait_ge(w2_in, 16)
                pe.wait_ge(hs_ready, RT * (b + 1))
                project(lambda k, t: hs[0:(P, P, R_ROWS[2] + 1)[k], k, t * P:(t + 1) * P], w2, RT, b,
                        (P, P, R_ROWS[2] + 1))

            def ffn_in(b):
                pe.wait_ge(f13_in, 16)
                pe.wait_ge(hT_ready, CT * (7 + b))
                pe.wait_ge(gates_ready, 2 * RT * B)
                for h in range(HT):
                    n = HT * b + h
                    if n >= 3:
                        pe.wait_ge(fhid_ready, n - 2)
                    for up in range(2):
                        for k in range(CT):
                            mm = pe.matmul(bank[2 + 2 * (n % 3) + up][:, :], f13[:, k, up * H + h * P:up * H + (h + 1) * P],
                                           hT[:, k, b * S:(b + 1) * S], start=(k == 0), stop=(k == CT - 1))
                        mm.then_inc(fps_done, 1)

            def ffn_out(b):
                pe.wait_ge(fhid_ready, HT * (b + 1))
                pe.wait_ge(f2_ready, 1)
                project(lambda k, t: fhid[:, k, t * P:(t + 1) * P], f2b, HT, b, [P] * HT)

            transposes(4, 0, (shy_ready, 2))
            hidden1(0)
            conv(0)
            gates(0)
            transposes(5, 1, (hT_ready, CT * 5))
            hidden1(1)
            conv(1)
            pe.wait_ge(hT_ready, CT * 6)
            recur_out(0)
            transposes(6, 0, (x_done, 3))
            gates(1)
            ffn_in(0)
            pe.wait_ge(hT_ready, CT * 7)
            ffn_out(0)
            pe.wait_ge(x_done, 4)
            recur_out(1)
            transposes(7, 1, (x_done, 5))
            ffn_in(1)
            pe.wait_ge(hT_ready, CT * 8)
            ffn_out(1)

        @block.scalar
        def _(act):
            step, settle = counter(act, act_step)
            act.wait_ge(par_in, 32)
            act.activation(silc[:, :], par[:, P_C0:P_C0 + 8], ACT.Silu).then_inc(silc_ready, 1)
            step(act.activation(wneg[:, :], par[:, P_TD:P_TD + CT], ACT.Exp))
            settle()
            step(act.activation(wneg[:, :], wneg[:, :], ACT.Copy, scale=-1.0))

            def modulated(n, b, layer, sh, sc):
                if n in (0, 4):
                    act.wait_ge(modcol_ready, layer + 1)
                for c in range(CT):
                    act.wait_ge(normT_done, CT * n + c + 1)
                    dst = hT[:, c, b * S:(b + 1) * S]
                    if sh is None:
                        act.activation(dst, bank[c][:, :], ACT.Copy).then_inc(hT_ready, 1)
                    else:
                        act.activation(dst, bank[c][:, :], ACT.Identity, bias=modcol[:, layer, CT * sh + c, b:b + 1],
                                       scale=modcol[:, layer, CT * sc + c, b:b + 1]).then_inc(hT_ready, 1)

            def kvr(u):
                if u >= 2:
                    act.wait_ge(yT_ready, u - 1)
                for i, dst in enumerate((kS[u % 2], vS[u % 2], er[u % 2])):
                    act.wait_ge(rvk_done, 3 * u + i + 1)
                    act.activation(dst, bank[2 + 3 * (u % 2) + i][:, :], ACT.Exp if i == 2 else ACT.Copy,
                                   scale=-1.0 if i == 2 else 1.0).then_inc(kvr_ready, 1)

            def exps(u):
                for i, (v, scale, bias) in enumerate(((t1, 1.0, wneg[:, u % 2:u % 2 + 1]), (t2, 1.0, 0.0),
                                                      (rz, -1.0, 0.0), (mz, 1.0, 0.0))):
                    act.wait_ge(exparg_ready, 4 * u + i + 1)
                    act.activation(v, v, ACT.Exp, bias=bias, scale=scale).then_inc(exp_ready, 1)

            modulated(0, 0, 0, SA, CA)
            settle()
            kvr(0)
            kvr(1)
            modulated(1, 1, 0, SA, CA)
            exps(0)
            kvr(2)
            exps(1)
            kvr(3)
            exps(2)
            modulated(2, 0, 0, None, None)
            exps(3)
            modulated(3, 1, 0, None, None)
            act.wait_ge(logit_done, 1)
            act.activation(scores[:, :, :].rearrange("p t e -> p (t e)"), bank[0][:, 0:NT * E], ACT.Sigmoid)\
               .then_inc(score_ready, 1)

            def shared_silu(b):
                for m in range(SHT):
                    n = SHT * b + m
                    act.wait_ge(shps_done, 2 * n + 1)
                    if n:
                        act.wait_ge(shhid_ready, n)
                    act.activation(sh_sil[0:SH_ROWS[m], :], bank[2 + 2 * m][0:SH_ROWS[m], :], ACT.Silu)\
                       .then_inc(shsil_ready, 1)

            def shared_copy(b, banks):
                act.wait_ge(shy_done, b + 1)
                if b == 0:
                    act.wait_ge(h2_out, 16 * B)
                for h in range(2):
                    dst = shared_y[:, b * TB + 2 * h:b * TB + 2 * h + 2, :].rearrange("p t c -> p (t c)")
                    ins = act.activation(dst, bank[banks[h]][:, :], ACT.Copy)
                ins.then_inc(shy_ready, 1)

            shared_silu(0)
            shared_copy(0, (2, 3))

            def copy_x(q, r):
                act.wait_ge(tx_done, 4 * q + (r + 1))
                act.activation(xgT[r % 2], bank[r % 2][:, 0:C], ACT.Copy).then_inc(xgT_ready, 1)

            def tile_silu(q, r):
                act.wait_ge(gu_done, 4 * q + (r + 1))
                act.activation(sil[r % 2], bank[2 + r % 2][:, 0:M], ACT.Silu).then_inc(sil_ready, 1)

            def quad(q):
                for r in range(4):
                    copy_x(*near(q, r, 1))
                    tile_silu(q, r)

            last_q = load_last(act)
            copy_x(0, 0)
            quad(0)
            with act.Fori(1, SURE_QUADS) as q:
                quad(q)
            with act.Fori(SURE_QUADS, QUADS) as q:
                with act.If(q <= last_q):
                    quad(q)

            act.wait_ge(th_done, 4 * last_q + 4)
            shared_silu(1)
            shared_copy(1, (0, 1))

            lam = par[:, P_LAM:P_LAM + RT]
            step(act.activation(sp[:, 0, :], lam, ACT.Abs))
            step(act.activation(sp[:, 1, :], lam, ACT.Relu))
            settle()
            step(act.activation(sp[:, 2, :], sp[:, 0, :], ACT.Exp, scale=-1.0))
            settle()
            step(act.activation(sp[:, 3, :], sp[:, 2, :], ACT.Ln, bias=1.0))
            for i, k in enumerate((6, 7, 2, 3)):
                act.wait_ge(had_done, i + 1)
                act.activation(f2a[:, 2 * i:2 * i + 2, :].rearrange("p h c -> p (h c)"), bank[k][:, :], ACT.Copy)\
                   .then_inc(had_ready, 1)

            def recur_hidden(b):
                for m in range(RT):
                    n = R_ROWS[m]
                    act.wait_ge(w1_done, RT * b + m + 1)
                    if b:
                        act.wait_ge(conv_done, RT)
                    act.activation(h1[0:n, m, PAD:PAD + S], bank[2 + m][0:n, :], ACT.Silu,
                                   bias=par[0:n, P_B1 + m:P_B1 + m + 1]).then_inc(h1_ready, 1)

            def conv_out(b):
                for m in range(RT):
                    n = R_ROWS[m]
                    act.wait_ge(conv_done, RT * b + m + 1)
                    if b:
                        act.wait_ge(ix_ready, b)
                    act.activation(hc[0:n, m, :], bank[5 + m][0:n, :], ACT.Identity,
                                   bias=par[0:n, P_CB + m:P_CB + m + 1]).then_inc(hc_ready, 1)

            def gate_sigmoids(b):
                if b:
                    act.wait_ge(hs_ready, RT * b)
                for i, (dst, m, k, p0) in enumerate((
                        (rS[:, 0, :], 0, P_BA, 0), (rS[:, 1, :], 1, P_BA + 1, 0),
                        (iS[:, 0, :], 2, P_BX, 0), (iS[:, 1, :], 3, P_BX + 1, 0),
                        (rS[0:64, 2, :], 4, P_BA + 2, 0), (iS[0:64, 2, :], 4, P_BX + 2, 64))):
                    act.wait_ge(gates_done, 5 * b + m + 1)
                    n = dst.shape[0]
                    act.activation(dst, bank[2 + m][p0:p0 + n, :], ACT.Sigmoid, bias=par[p0:p0 + n, k:k + 1])\
                       .then_inc(gates_ready, 1)

            def decays(b):
                act.wait_ge(gates_ready, 2 * RT * (b + 1))
                act.wait_ge(sp_ready, 1)
                act.wait_ge(comb_done, NT)
                for dst, row, done in ((a2, 5, a2_ready), (aS, 4, a_ready)):
                    for m in range(RT):
                        n = R_ROWS[m]
                        act.activation(dst[0:n, m, :], rS[0:n, m, :], ACT.Exp, scale=sp[0:n, row, m:m + 1]).then_inc(done, 1)

            def roots(b):
                act.wait_ge(a2min_ready, 2 * (b + 1))
                for v in (a2[:, 0:2, :], a2[0:64, 2, :]):
                    act.activation(v, v, ACT.Sqrt, bias=1.0, scale=-1.0).then_inc(mult_ready, 1)

            def ffn_silu(b):
                for h in range(HT):
                    n = HT * b + h
                    act.wait_ge(fps_done, 2 * n + 1)
                    if n >= 2:
                        act.wait_ge(fhid_ready, n - 1)
                    act.activation(fsil[n % 2], bank[2 + 2 * (n % 3)][:, :], ACT.Silu).then_inc(fsil_ready, 1)

            modulated(4, 0, 1, SA, CA)
            act.wait_ge(pads_ready, 1)
            recur_hidden(0)
            conv_out(0)
            gate_sigmoids(0)
            decays(0)
            roots(0)
            modulated(5, 1, 1, SA, CA)
            recur_hidden(1)
            conv_out(1)
            modulated(6, 0, 1, SB, CB)
            gate_sigmoids(1)
            decays(1)
            roots(1)
            ffn_silu(0)
            modulated(7, 1, 1, SB, CB)
            ffn_silu(1)

        @block.gpsimd
        def _(pool):
            def inverse_root(n):
                ts = slice((n % B) * TB, (n % B + 1) * TB)
                pool.wait_ge(ve_ready, n + 1)
                if n == 0:
                    pool.wait_ge(mhalf_ready, 1)
                pool.tensor_tensor(rstd[:, ts], ve[:, ts], mhalf[:, ts], ALU.pow).then_inc(rstd_ready, 1)

            for n in range(4):
                inverse_root(n)

            def gather(q, r):
                if not early(q, r, 4):
                    pool.wait_ge(tx_done, 4 * q + (r - 3))
                pool.tensor_copy(tile_idx[r][:, :], gidx[:, bass.ds(4 * q + r, 1)]).then_inc(tile_idx_ready, 1)
                pool.wait_ge(tile_idx_ready, 4 * q + (r + 1))
                pool.sem_inc(gathers_begun, 1)
                pool.indirect_dma_start(out=xg[r], out_offset=None, in_=h2_dram,
                                        in_offset=bass.IndirectOffsetOnAxis(ap=tile_idx[r][:, :], axis=0))\
                    .then_inc(xg_in[r], 16)

            pool.wait_ge(gidx_ready, 1)
            pool.wait_ge(h2_out, 16 * B)
            pool.wait_ge(shy_done, 1)
            for r in range(4):
                gather(0, r)
            last_q = load_last(pool)
            with pool.Fori(1, SURE_QUADS) as q:
                for r in range(4):
                    gather(q, r)
            with pool.Fori(SURE_QUADS, QUADS) as q:
                with pool.If(q <= last_q):
                    for r in range(4):
                        gather(q, r)
            gather(*near(last_q, 3, 1))

            for i in range(2):
                pool.wait_ge(y_out[i], 32 * last_q + 32)
            pool.sem_inc(gathers_begun, 1)
            pool.wait_ge(y_filled, 16 * (QUADS - SURE_QUADS))

            def pick(t):
                if t >= YG:
                    pool.wait_ge(comb_done, t - YG + 1)
                for k in range(TOPK):
                    pool.indirect_dma_start(out=yg[t % YG][:, k, :], out_offset=None, in_=y_dram,
                                            in_offset=bass.IndirectOffsetOnAxis(ap=pidx[:, t, k:k + 1].bitcast(U32), axis=0))\
                        .then_inc(yg_in[t % YG], 16)

            pick(0)
            pick(1)
            pool.memset(h1[:, :, 0:PAD], 0.0)
            pool.memset(h1[:, :, PAD + S:PAD + S + PAD], 0.0).then_inc(pool_step, 1)
            pool.wait_ge(pool_step, 1)
            pool.memset(hs[64:65, 2, :], 1.0).then_inc(pads_ready, 1)
            for t in range(2, TB + 1):
                pick(t)
            pool.wait_ge(pads_ready, 1)
            inverse_root(4)
            for t in range(TB + 1, NT):
                pick(t)
            for n in range(5, 8):
                inverse_root(n)

        @block.vector
        def _(dve):
            step, settle = counter(dve, dve_step)
            tt, ts_, stt = dve.tensor_tensor, dve.tensor_scalar, dve.scalar_tensor_tensor

            dve.memset(mhalf[:, :], -0.5).then_inc(mhalf_ready, 1)
            dve.memset(eoff[:, 0:1], 0)
            dve.memset(ones16[:, :], 1.0)
            dve.memset(onesE[:, :], 1.0)
            dve.memset(O[:, 0:1], START)
            dve.memset(Q[:, 0:1], 0.0)
            step(dve.memset(PP[:, 0:1], 0.0))
            dve.wait_ge(par_in, 32)
            dve.tensor_copy(tri16[:, :], con[:, K_TRI:K_TRI + P])
            step(dve.tensor_copy(iota16[:, :], con[:, K_IOTA:K_IOTA + P]))

            def mod_rows(layer, row):
                for n in range(3):
                    dve.wait_ge(modps_done, 3 * layer + n + 1)
                    dve.tensor_copy(row[:, n * 512:(n + 1) * 512], bank[2 + n][0:B, :]).then_inc(modrow_ready, 1)

            def mod_cols(layer, pairs):
                dve.wait_ge(modT_done, layer + 1)
                for sh, sc in pairs:
                    w = CT * B
                    dst = modcol[:, layer, :, :].rearrange("p j b -> p (j b)")
                    dve.tensor_copy(dst[:, w * sh:w * (sh + 1)], bank[5][:, w * sh:w * (sh + 1)])
                    ins = ts_(dst[:, w * sc:w * (sc + 1)], bank[5][:, w * sc:w * (sc + 1)], 1.0, None, ALU.add)
                ins.then_inc(modcol_ready, 1)

            def gate_floor(g, sign, size):
                step(stt(size, g, -1.0, g, ALU.mult, ALU.max))
                settle()
                ts_(sign, g, 0.0, 2.0, ALU.is_ge, ALU.mult)
                step(ts_(size, size, 0.25, None, ALU.max))
                settle()
                return step(stt(g, sign, -1.0, size, ALU.add, ALU.mult))

            def layer_norm(n, src, modulate=False):
                b = n % B
                tiles = range(b * TB, (b + 1) * TB)
                for t in tiles:
                    last = step(dve.bn_stats(out=stats[:, t, :], in_=src[:, t, :]))
                settle()
                for t in tiles:
                    last = step(dve.bn_aggr(out=mv[:, t, :], in_=stats[:, t, :]))
                settle()
                ts_(ve[:, b * TB:(b + 1) * TB], mv[:, b * TB:(b + 1) * TB, 1], EPS, None, ALU.add).then_inc(ve_ready, 1)
                if n >= B:
                    dve.wait_ge(normT_done, CT * (n - B + 1))
                dve.wait_ge(rstd_ready, n + 1)
                for t in tiles:
                    ins = ts_(norm[:, t, :], src[:, t, :], mv[:, t, 0:1], rstd[:, t:t + 1], ALU.subtract, ALU.mult)
                if modulate:
                    step(ins)
                    settle()
                    v = norm[:, b * TB:(b + 1) * TB, :]
                    sh, sc = [modB0[:, b, i * C:(i + 1) * C].unsqueeze(1).to_broadcast([P, TB, C]) for i in (1, 2)]
                    step(tt(v, v, sc, ALU.mult))
                    settle()
                    ins = tt(v, v, sh, ALU.add)
                ins.then_inc(norm_ready, 1)

            def residual(x, b, gate, done, free, tmp):
                if free <= B:
                    dve.wait_ge(yT_ready, 2 * free + (free < B))
                dve.wait_ge(proj_done, done)
                g = gate.unsqueeze(1).to_broadcast([P, 2, C])
                for h in range(2):
                    step(tt(tmp[h].rearrange("p (t c) -> p t c", t=2), bank[h][:, :].rearrange("p (t c) -> p t c", t=2),
                            g, ALU.mult))
                settle()
                for h in range(2):
                    v = x[:, b * TB + 2 * h:b * TB + 2 * h + 2, :]
                    ins = tt(v, v, tmp[h].rearrange("p (t c) -> p t c", t=2), ALU.add)
                ins.then_inc(x_done, 1)
                dve.wait_ge(x_done, free)

            for b in range(B):
                dve.wait_ge(x_in_s[b], 16)
                if b == 0:
                    layer_norm(0, X)
                    mod_rows(0, modrow0)
                    mod_cols(0, ((SA, CA),))
                else:
                    layer_norm(1, X)
            dve.wait_ge(modB_in[0], 16 * 3 * B)
            z3, t3 = z.rearrange("p (b c) -> p b c", b=B), t1.rearrange("p (b c) -> p b c", b=B)
            gate_floor(modB0[:, :, 0:C], z3, t3)
            settle()
            gate_floor(gb0[:, :, :], z3, t3)
            step(ts_(modB0[:, :, 2 * C:3 * C], modB0[:, :, 2 * C:3 * C], 1.0, None, ALU.add))
            settle()

            def wkv(u):
                b, c = divmod(u, CT)
                k, v, e = kS[u % 2], vS[u % 2], er[u % 2]
                dve.wait_ge(kvr_ready, 3 * u + 1)
                if u == 0:
                    dve.wait_ge(act_step, 2)
                step(dve.tensor_tensor_scan(O[:, 1:S + 1], wneg[:, c:c + 1].to_broadcast([P, S]), k, START,
                                            ALU.add, ALU.max))
                settle()
                stt(z, k, par[:, P_TF + c:P_TF + c + 1], O[:, 0:S], ALU.add, ALU.subtract)
                zs = step(tt(t1, O[:, 0:S], O[:, 1:S + 1], ALU.subtract))
                tt(t2, k, O[:, 1:S + 1], ALU.subtract).then_inc(exparg_ready, 2)
                settle(zs)
                ts_(rz, z, 0.0, None, ALU.max).then_inc(exparg_ready, 1)
                ts_(mz, z, 0.0, None, ALU.min).then_inc(exparg_ready, 1)
                dve.wait_ge(kvr_ready, 3 * u + 2)
                dve.wait_ge(exp_ready, 4 * u + 2)
                step(tt(Bv, t2, v, ALU.mult))
                dve.tensor_tensor_scan(Q[:, 1:S + 1], t1, t2, 0.0, ALU.mult, ALU.add)
                settle()
                step(dve.tensor_tensor_scan(PP[:, 1:S + 1], t1, Bv, 0.0, ALU.mult, ALU.add))
                dve.wait_ge(exp_ready, 4 * u + 4)
                settle()
                tt(z, rz, PP[:, 0:S], ALU.mult)
                step(tt(Bv, mz, v, ALU.mult))
                step(tt(rz, rz, Q[:, 0:S], ALU.mult))
                settle()
                tt(z, z, Bv, ALU.add)
                step(tt(rz, rz, mz, ALU.add))
                settle()
                dve.wait_ge(kvr_ready, 3 * u + 3)
                step(stt(rz, e, 1.0, rz, ALU.add, ALU.mult))
                settle()
                step(dve.reciprocal(t2, rz))
                settle()
                dve.wait_ge(rvk_done, 3 * CT * (b + 1))
                tt(hT[:, c, b * S:(b + 1) * S], z, t2, ALU.mult).then_inc(yT_ready, 1)

            tmp0 = [z, t1]
            wkv(0)
            wkv(1)
            wkv(2)
            residual(X, 0, modB0[:, 0, 0:C], 1, 1, tmp0)
            layer_norm(2, X, modulate=True)
            wkv(3)
            residual(X, 1, modB0[:, 1, 0:C], 2, 2, tmp0)
            layer_norm(3, X, modulate=True)

            dve.wait_ge(route_in, 32)
            dve.wait_ge(norm_ready, 4)
            dve.memset(gsx[:, :, G:], BIG)
            dve.memset(sfx[:, :, E:], BIG)
            dve.wait_ge(score_ready, 1)
            step(tt(sfc, scores[:, :, :], cbias[:, :].unsqueeze(1).to_broadcast([P, NT, E]), ALU.add))
            settle()
            f4 = sfc.rearrange("p t (g a b) -> p (t g a) b", g=G, a=2)
            fl = lambda v: v.rearrange("p t g a -> p (t g a)")
            tt(fl(hi2), f4[:, :, 0], f4[:, :, 1], ALU.max)
            step(tt(fl(lo2), f4[:, :, 0], f4[:, :, 1], ALU.min))
            settle()
            tt(m1, hi2[:, :, :, 0], hi2[:, :, :, 1], ALU.max)
            tt(m2, hi2[:, :, :, 0], hi2[:, :, :, 1], ALU.min)
            step(tt(m3, lo2[:, :, :, 0], lo2[:, :, :, 1], ALU.max))
            settle()
            step(tt(m2, m2, m3, ALU.max))
            settle()
            step(tt(gsx[:, :, 0:G], m1, m2, ALU.add))
            settle()
            for t in range(NT):
                step(dve.max(gtop[:, t, :], gsx[:, t, :]))
            settle()
            for t in range(NT):
                step(dve.match_replace(grep[:, t, :], gtop[:, t, :], gsx[:, t, :], -BIG))
            settle()
            step(ts_(gmask, grep[:, :, 0:G], -0.5 * BIG, None, ALU.is_lt))
            settle()
            step(ts_(gpen, gmask, -1.0, -NONE, ALU.add, ALU.mult))
            f3 = sfc.rearrange("p t (g a) -> p t g a", g=G)
            bc = lambda v: v.unsqueeze(3).to_broadcast([P, NT, G, EG])
            x3 = sfx[:, :, 0:E].rearrange("p t (g a) -> p t g a", g=G)
            step(tt(x3, f3, bc(gmask), ALU.mult))
            settle()
            step(tt(x3, x3, bc(gpen), ALU.add))
            settle()
            for t in range(NT):
                step(dve.max(stop8[:, t, :], sfx[:, t, :]))
            settle()
            for t in range(NT):
                step(dve.match_replace(srep[:, t, :], stop8[:, t, :], sfx[:, t, :], -BIG))
            settle()
            step(ts_(mask[:, :, :], srep[:, :, 0:E], -0.5 * BIG, None, ALU.is_lt))
            settle()
            dve.tensor_copy(mask16[:, :, :], mask[:, :, :]).then_inc(mask_ready, 1)

            def shared_hidden(b):
                for m in range(SHT):
                    n = SHT * b + m
                    dve.wait_ge(shsil_ready, n + 1)
                    dve.wait_ge(shps_done, 2 * n + 2)
                    k = SH_ROWS[m]
                    tt(sh_hid[0:k, m, :], sh_sil[0:k, :], bank[3 + 2 * m][0:k, :], ALU.mult).then_inc(shhid_ready, 1)

            shared_hidden(0)

            dve.wait_ge(rank_done, 1)
            step(tt(cmp8[:, :, :], bank[1][:, 0:E].unsqueeze(2).to_broadcast([P, E, G]),
                    con[:, K_THR:K_THR + G].unsqueeze(1).to_broadcast([P, E, G]), ALU.is_gt))
            settle()
            step(dve.tensor_reduce(ntile[:, :], cmp8[:, :, :], AX.X, ALU.add))
            settle()
            step(dve.tensor_tensor_scan(incl[:, :], onesE[:, :], ntile[:, :], 0.0, ALU.mult, ALU.add))
            settle()
            step(ts_(last_quad[:, :], incl[0:1, E - 1:E], -1.0, None, ALU.add))
            step(tt(base[:, :], incl[:, :], ntile[:, :], ALU.subtract))
            step(ts_(ejcmp[:, :], incl[0:SLOT_TILES, :], par[0:SLOT_TILES, P_J:P_J + 1], None, ALU.is_le))
            settle()
            ts_(last_quad[:, :], last_quad[:, :], 2, None, ALU.arith_shift_right).then_inc(quads_ready, 1)
            step(ts_(base[:, :], base[:, :], float(P), 1.0, ALU.mult, ALU.add))
            dve.tensor_reduce(ej[:, :], ejcmp[:, :], AX.X, ALU.add).then_inc(ej_ready, 1)
            settle()
            step(tt(pos[:, :, :], bank[0][:, 0:NT * E].rearrange("p (t e) -> p t e", t=NT),
                    base[:, :].unsqueeze(1).to_broadcast([P, NT, E]), ALU.add))
            settle()
            step(tt(pos[:, :, :], pos[:, :, :], mask[:, :, :], ALU.mult))
            settle()
            for t in range(NT):
                step(dve.max(ptop[:, t, :], pos[:, t, :]))
            settle()
            step(ts_(pidx[:, :, :], ptop[:, :, :], -1.0, 0.0, ALU.add, ALU.max))
            settle()
            ts_(pint[:, 0, :, :], pidx[:, :, :], 7, None, ALU.arith_shift_right)
            step(ts_(pint[:, 1, :, :], pidx[:, :, :], P - 1, None, ALU.bitwise_and))
            settle()
            step(dve.tensor_copy(pflt[:, :, :, :], pint[:, :, :, :]))
            settle()
            n = 0
            for t in range(NT):
                for k in range(TOPK):
                    if n >= 4:
                        dve.wait_ge(onehot_used, n - 3)
                    ts_(onehot_s[:, n % 4, :], iota16[:, :], pflt[:, 1, t, k:k + 1], None, ALU.is_equal)
                    ts_(onehot_j[:, n % 4, :], iota16[:, 0:SLOT_TILES + 1], pflt[:, 0, t, k:k + 1],
                        par[:, P_TOK + t:P_TOK + t + 1], ALU.is_equal, ALU.mult).then_inc(onehot_ready, 1)
                    n += 1
            dve.wait_ge(onehot_used, n)
            dve.tensor_copy(gidx[:, :], bank[1][:, 128:128 + SLOT_TILES + 1]).then_inc(gidx_ready, 1)
            dve.wait_ge(ejT_done, 1)
            ts_(eoff[:, 1:1 + SLOT_TILES], bank[1][0:1, 256:256 + SLOT_TILES], float(E - 1), None, ALU.min).then_inc(eoff_ready, 1)
            def copy_h(q, r):
                dve.wait_ge(th_done, 4 * q + (r + 1))
                dve.tensor_copy(hidT[r % 2], bank[4 + r % 2][0:MH, 0:2 * P]).then_inc(hidT_ready, 1)

            def tile_hidden(q, r):
                dve.wait_ge(sil_ready, 4 * q + (r + 1))
                tt(hid[r % 2], sil[r % 2], bank[2 + r % 2][:, M:2 * M], ALU.mult).then_inc(hid_ready, 1)

            def copy_y(q, r):
                dve.wait_ge(dn_done, 4 * q + (r + 1))
                if not early(q, r, 2):
                    dve.wait_ge(y_out[r % 2], 16 * (2 * q + r // 2))
                dve.tensor_copy(yt[r % 2], bank[6 + r % 2][:, 0:C]).then_inc(y_ready, 1)

            def quad(q, first=False):
                for r in range(4):
                    if not (first and r == 0):
                        copy_h(*near(q, r, -1))
                    tile_hidden(q, r)
                    if not (first and r == 0):
                        copy_y(*near(q, r, -1))

            last_q = load_last(dve)
            quad(0, first=True)
            with dve.Fori(1, SURE_QUADS) as q:
                quad(q)
            with dve.Fori(SURE_QUADS, QUADS + 1) as q:
                with dve.If(q <= last_q + 1):
                    with dve.If(q <= last_q):
                        quad(q)
                    with dve.If(q == last_q + 1):
                        copy_h(*near(q, 0, -1))
                        copy_y(*near(q, 0, -1))
                    dve.nop()
            eq, eqs = srep[:, :, 0:E], sfx[:, :, 0:E]
            for k in range(TOPK):
                step(tt(eq, pos[:, :, :], ptop[:, :, k:k + 1].to_broadcast([P, NT, E]), ALU.is_equal))
                settle()
                step(tt(eqs, eq, scores[:, :, :], ALU.mult))
                settle()
                step(dve.tensor_reduce(wk[:, :, k], eqs, AX.X, ALU.add))
                settle()

            dve.wait_ge(gu_done, 4 * last_q + 4)
            shared_hidden(1)

            def decay_rates():
                dve.wait_ge(act_step, 6)
                step(tt(sp[:, 3, :], sp[:, 3, :], sp[:, 1, :], ALU.add))
                settle()
                ts_(sp[:, 4, :], sp[:, 3, :], -8.0, None, ALU.mult)
                ts_(sp[:, 5, :], sp[:, 3, :], -16.0, None, ALU.mult).then_inc(sp_ready, 1)
            def combine(t):
                dve.wait_ge(shy_ready, t // TB + 1)
                dve.wait_ge(yg_in[t % YG], 16 * TOPK * (t // YG + 1))
                acc = shared_y[:, t, :]
                for k in range(TOPK):
                    step(stt(acc, yg[t % YG][:, k, :], wk[:, t, k:k + 1], acc, ALU.mult, ALU.add))
                    settle()
                step(tt(acc, acc, gb0[:, t // TB, :], ALU.mult))
                settle()
                tt(X2[:, t, :], X2[:, t, :], acc, ALU.add).then_inc(comb_done, 1)
                dve.wait_ge(comb_done, t + 1)

            def recurrence(b):
                dve.wait_ge(a2_ready, RT * (b + 1))
                for v in (a2[:, 0:2, :], a2[0:64, 2, :]):
                    ts_(v, v, 1.0, None, ALU.min).then_inc(a2min_ready, 1)
                dve.wait_ge(gates_ready, 2 * RT * (b + 1))
                for rows, ms in ((P, slice(0, 2)), (64, slice(2, 3))):
                    ins = tt(iS[0:rows, ms, :], iS[0:rows, ms, :], hc[0:rows, ms, :], ALU.mult)
                ins.then_inc(ix_ready, 1)
                dve.wait_ge(ix_ready, b + 1)
                dve.wait_ge(mult_ready, 2 * (b + 1))
                for rows, ms in ((P, slice(0, 2)), (64, slice(2, 3))):
                    last = step(tt(iS[0:rows, ms, :], iS[0:rows, ms, :], a2[0:rows, ms, :], ALU.mult))
                settle()
                if b:
                    dve.wait_ge(proj_done, 3)
                dve.wait_ge(a_ready, RT * (b + 1))
                for m in range(RT):
                    n = R_ROWS[m]
                    dve.tensor_tensor_scan(hs[0:n, m, :], aS[0:n, m, :], iS[0:n, m, :], 0.0, ALU.mult, ALU.add)\
                       .then_inc(hs_ready, 1)

            def ffn_hidden(b):
                for h in range(HT):
                    n = HT * b + h
                    dve.wait_ge(fsil_ready, n + 1)
                    dve.wait_ge(fps_done, 2 * n + 2)
                    if b and h == 0:
                        dve.wait_ge(proj_done, 4)
                    tt(fhid[:, h, :], fsil[n % 2], bank[3 + 2 * (n % 3)][:, :], ALU.mult).then_inc(fhid_ready, 1)

            def hadamard_adds():
                dve.wait_ge(had_ready, 4)
                src, dst = f2a, f2b
                for w in (1, 2, 4):
                    s5 = src.rearrange("p (i a j) c -> p i a (j c)", a=2, j=w)
                    d5 = dst.rearrange("p (i a j) c -> p i a (j c)", a=2, j=w)
                    ins = [tt(d5[:, :, 0, :], s5[:, :, 0, :], s5[:, :, 1, :], ALU.add),
                           tt(d5[:, :, 1, :], s5[:, :, 0, :], s5[:, :, 1, :], ALU.subtract)]
                    if w < 4:
                        step(ins[1])
                        settle()
                    else:
                        ins[1].then_inc(f2_ready, 1)
                    src, dst = dst, src

            def gate_floors():
                dve.wait_ge(modB_in[1], 16 * 2 * B)
                g4 = modB1.rearrange("p b n -> p (b n)")
                gate_floor(g4, fhid[:, 0:2, :].rearrange("p h n -> p (h n)"), fhid[:, 2:4, :].rearrange("p h n -> p (h n)"))
                settle()

            dve.wait_ge(x1_in, 16)
            tmp1 = [yg[0].rearrange("p k c -> p (k c)")[:, i * S:(i + 1) * S] for i in range(2)]
            combine(0)
            mod_rows(1, modrow1)
            combine(1)
            mod_cols(1, ((SA, CA), (SB, CB)))
            combine(2)
            combine(3)
            layer_norm(4, X2)
            decay_rates()
            gate_floors()
            for t in range(TB, NT):
                combine(t)
            layer_norm(5, X2)
            ga1 = lambda b: modB1[:, b, 0:C]
            gb1 = lambda b: modB1[:, b, C:2 * C]
            hadamard_adds()
            recurrence(0)
            residual(X2, 0, ga1(0), 3, 3, tmp1)
            layer_norm(6, X2)
            recurrence(1)
            ffn_hidden(0)
            residual(X2, 0, gb1(0), 4, 4, tmp1)
            residual(X2, 1, ga1(1), 5, 5, tmp1)
            layer_norm(7, X2)
            ffn_hidden(1)
            residual(X2, 1, gb1(1), 6, 6, tmp1)


def early(q, r, n):
    return isinstance(q, int) and 4 * q + r < n


def near(q, r, d):
    return q + (r + d) // 4, (r + d) % 4


def _cols(a, rows=P):
    n = -(-a.shape[0] // rows) * rows
    padded = np.zeros((n,) + a.shape[1:], a.dtype)
    padded[:a.shape[0]] = a
    return np.ascontiguousarray(np.moveaxis(padded.reshape((n // rows, rows) + a.shape[1:]), 0, 1))


def _flat(a):
    return np.ascontiguousarray(a.reshape(a.shape[0], -1))


def _hadamard(n):
    h = np.ones((1, 1), np.float32)
    while h.shape[0] < n:
        h = np.block([[h, h], [h, -h]])
    return h


def _lay_out(i):
    f = np.float32
    small = np.zeros((P, P_COLS), f)
    for col, a in ((P_TD, i["L0_attn_time_decay"]), (P_TF, i["L0_attn_time_first"]), (P_B1, i["L1_attn_b1"]),
                   (P_CB, i["L1_attn_conv_b"]), (P_BA, i["L1_attn_ba"]), (P_LAM, i["L1_attn_lam"])):
        c = _cols(a)
        small[:, col:col + c.shape[1]] = c
    bx = i["L1_attn_bx"]
    small[:, P_BX:P_BX + 2] = _cols(bx[:2 * P])
    small[64:128, P_BX + 2] = bx[2 * P:]
    for col, c in ((P_C0, i["L0_c"]), (P_C1, i["L1_c"])):
        small[:, col:col + CT * B] = _flat(_cols(np.ascontiguousarray(c.T)))
    small[:, P_TOK:P_TOK + NT] = np.arange(NT * P, dtype=f).reshape(NT, P).T
    small[:, P_J] = np.arange(P, dtype=f)
    consts = np.zeros((P, K_COLS), f)
    consts[:, K_ID:K_ID + P] = np.eye(P)
    consts[:, K_TRI:K_TRI + P] = np.triu(np.ones((P, P)), 1)
    consts[:, K_HAD:K_HAD + P] = _hadamard(P) / 32.0
    consts[:, K_IOTA:K_IOTA + P] = np.arange(P)
    consts[:, K_THR:K_THR + G] = np.arange(G) * P
    gate, up, down = i["L0_ffn_gate_w"], i["L0_ffn_up_w"], i["L0_ffn_down_w"]
    gu = np.concatenate([gate, up], axis=2)
    gu = np.ascontiguousarray(gu.reshape(E, CT, P, 2 * M).transpose(2, 0, 1, 3)).reshape(P, -1)
    dn = np.ascontiguousarray(down.reshape(E, 2, MH, C).transpose(2, 0, 1, 3)).reshape(MH, -1)
    wa, wx = i["L1_attn_wa"].T, i["L1_attn_wx"].T
    gates = np.concatenate([wa[:, :2 * P], wx[:, :2 * P], wa[:, 2 * P:], wx[:, 2 * P:]], axis=1)
    w2 = np.concatenate([i["L1_attn_w2"].T, i["L1_attn_b2"][None]], axis=0)
    return {
        "x": i["L0_attn_x"].reshape(B * S, C),
        "small": small, "consts": consts,
        "wmod0": _cols(i["L0_wmod"]), "wmod1": _cols(i["L1_wmod"]),
        "w_rvk": _cols(i["L0_attn_W_rvk"].T), "w_out": _cols(i["L0_attn_W_out"].T),
        "w_router": _cols(i["L0_ffn_w_router"]),
        "corr_bias": np.ascontiguousarray(np.broadcast_to(i["L0_ffn_corr_bias"], (P, E))),
        "w_gu": gu, "w_dn": dn,
        "w_shgu": _cols(np.concatenate([i["L0_ffn_sh_gate_w"], i["L0_ffn_sh_up_w"]], axis=1)),
        "w_shdn": _cols(i["L0_ffn_sh_down_w"]),
        "w_1": _cols(i["L1_attn_w1"].T),
        "w_conv": _cols(i["L1_attn_conv_w"].transpose(1, 2, 0)),
        "w_gates": _cols(gates), "w_2": _cols(w2),
        "w_f13": _cols(np.concatenate([i["L1_ffn_W1"].T, i["L1_ffn_W3"].T], axis=1)),
        "w_f2": _cols(i["L1_ffn_W2"].T),
    }


def kernel(**inputs):
    import concourse.bacc as bacc
    from concourse.bass_utils import run_bass_kernel_spmd

    arrays = {n: np.ascontiguousarray(a) for n, a in _lay_out({k: np.asarray(v) for k, v in inputs.items()}).items()}
    nc = bacc.Bacc("TRN2", target_bir_lowering=False, num_devices=1)
    args = [nc.dram_tensor(n, a.shape, mybir.dt.from_np(a.dtype), kind="ExternalInput").ap() for n, a in arrays.items()]
    out = nc.dram_tensor("out", (B * S, C), F32, kind="ExternalOutput").ap()
    two_layers(nc, *args, out)
    r = run_bass_kernel_spmd(nc, [arrays], core_ids=[0])
    return r.results[0]["out"].reshape(B, S, C)
```

```python
from contextlib import ExitStack

import numpy as np

import concourse.bass as bass
from concourse import mybir

F32 = mybir.dt.float32
F32R = mybir.dt.float32r
F16 = mybir.dt.float16
BF16 = mybir.dt.bfloat16
I32 = mybir.dt.int32
U32 = mybir.dt.uint32
ALU = mybir.AluOpType
ACT = mybir.ActivationFunctionType
AX = mybir.AxisListType

P = 128
B = 2
S = 512
C = 256
CT = C // P
NT = B * S // P
TB = S // P
E = 32
G = 8
EG = E // G
TOPG = 4
TOPK = 6
M = 176
MH = M // 2
SHM = 2 * M
SHT = 3
SH_ROWS = [P, P, SHM - 2 * P]
SLOT_TILES = 80
QUADS = SLOT_TILES // 4
TAIL = 3
SURE_QUADS = B * S * TOPK // (4 * P)
R = 320
RT = 3
R_ROWS = [P, P, R - 2 * P]
TAPS = 4
PAD = 3
SW = S + 2 * PAD
CONV_K = [(i, 2 * k) for i in range(2) for k in range(TAPS)] + [(2, 0), (2, 4)]
H = 1024
HT = H // P
GATE_ORDER = ((3, 4), (0, 1, 2)), ((0, 1, 2), (3, 4))
EPS = 1e-5
BIG = 3.0e38
NONE = -1.0e30
START = -1.0e38

(P_TD, P_TF, P_B1, P_CB, P_BA, P_BX, P_LAM, P_C0, P_C1, P_TOK, P_J, P_ZERO) = (
    0, 2, 4, 7, 10, 13, 17, 20, 24, 28, 36, 37)
P_COLS = 40
K_ID, K_TRI, K_HAD, K_IOTA, K_THR = 0, P, 2 * P, 3 * P, 4 * P
K_COLS = 4 * P + G
SA, CA, GA, SB, CB, GB = range(6)


def two_layers(nc, x_in, small, consts, wmod0, wmod1, w_rvk, w_out, w_router, corr_bias,
               w_gu, w_dn, w_shgu, w_shdn, w_1, w_conv, w_gates, w_2, w_f13, w_f2, out):
    mod_dram = [nc.dram_tensor(f"mod_dram{i}", (B, 6 * C), F32, kind="Internal").ap() for i in range(2)]
    h2_dram = nc.dram_tensor("h2_dram", (B * S, C), F32, kind="Internal").ap()
    x1_dram = nc.dram_tensor("x1_dram", (P, NT * C), F32, kind="Internal").ap()
    y_dram = nc.dram_tensor("y_dram", (SLOT_TILES * P, C), F32, kind="Internal").ap()

    with ExitStack() as ctx:
        def sb(name, shape, dt=F32):
            return ctx.enter_context(nc.sbuf_tensor(name, shape, dt))

        def sb_at(name, shape):
            at = -(-nc.sbuf_base // 32) * 32
            return sb(name, shape), at

        def rounded(name, at, *shape):
            return nc.alloc_sbuf_tensor_at(name, [P, *shape], F32R, offset=at)[(slice(None),) * (1 + len(shape))]

        def sem(name):
            return ctx.enter_context(nc.semaphore(name))

        bank = [ctx.enter_context(nc.psum_tensor(f"bank{i}", [P, 512], F32)) for i in range(8)]

        GUW, DNW = 4 * M, 2 * C
        DN0 = E * GUW
        arena, arena_at = sb_at("arena", [P, E * (GUW + DNW)])
        gu = arena[:, 0:DN0]
        dn = arena[0:MH, DN0:DN0 + E * DNW]

        def carve(limit, start):
            top = [start]

            def take(n, name=None):
                start = top[0]
                top[0] += n + -n % 8
                assert top[0] <= limit, (top[0], limit)
                whole = arena[:, start:start + n]
                return (whole, rounded(name, arena_at + 4 * start, n)) if name else whole
            return take

        par = sb("par", [P, P_COLS])
        con = sb("con", [P, K_COLS])
        ident = con[:, K_ID:K_ID + P]
        norm, norm_at = sb_at("norm", [P, NT, C])
        shared_y = norm
        hT, hT_at = sb_at("hT", [P, CT, B * S])
        stats = sb("stats", [P, NT, 6])
        mv = sb("mv", [P, NT, 2])
        ve = sb("ve", [P, NT])
        rstd = sb("rstd", [P, NT])
        mhalf = sb("mhalf", [P, NT])
        silc = sb("silc", [P, 8])
        modcol = sb("modcol", [P, 2, 6 * CT, B])
        wneg = sb("wneg", [P, CT])
        gb0 = sb("gb0", [P, B, C])
        sh_mem, sh_mem_at = sb_at("sh_mem", [P, CT * 2 * SHM + SHT * C])
        shgu = sh_mem[:, 0:CT * 2 * SHM].rearrange("p (k n) -> p k n", k=CT)
        shdn = sh_mem[:, CT * 2 * SHM:].rearrange("p (k n) -> p k n", k=SHT)
        router = sb("router", [P, CT, E])
        cbias = sb("cbias", [P, E])

        TW = 4 * C + 2 * C + 2 * 2 * M + 2 * C + 2 * C
        tile_mem, tile_mem_at = sb_at("tile_mem", [P, TW])
        o = 0
        xg = [tile_mem[:, o + i * C:o + (i + 1) * C] for i in range(4)]; o += 4 * C
        xgT = [tile_mem[:, o + i * C:o + (i + 1) * C] for i in range(2)]; o += 2 * C
        sil = [tile_mem[:, o + i * M:o + (i + 1) * M] for i in range(2)]; o += 2 * M
        hid = [tile_mem[:, o + i * M:o + (i + 1) * M] for i in range(2)]; o += 2 * M
        hidT = [tile_mem[0:MH, o + i * 2 * P:o + (i + 1) * 2 * P] for i in range(2)]; o += 2 * C
        yt = [tile_mem[:, o + i * C:o + (i + 1) * C] for i in range(2)]; o += 2 * C
        modrow0 = tile_mem[0:B, 0:6 * C]
        modB0 = tile_mem[:, 6 * C:6 * C + B * 3 * C].rearrange("p (b n) -> p b n", b=B)
        sh_hid = tile_mem[:, 0:SHT * S].rearrange("p (m n) -> p m n", m=SHT)
        sh_sil = tile_mem[:, SHT * S:(SHT + 1) * S]

        scores = sb("scores", [P, NT, E])
        o = (SHT + 1) * S

        def temp(*shape):
            nonlocal o
            n = NT * int(np.prod(shape))
            o += n
            assert o <= TW
            names = "abc"[:len(shape)]
            return tile_mem[:, o - n:o].rearrange(f"p (t {' '.join(names)}) -> p t {' '.join(names)}",
                                                  t=NT, **dict(zip(names, shape)))
        sfc = temp(E)
        hi2, lo2 = temp(G, 2), temp(G, 2)
        m1, m2, m3 = temp(G), temp(G), temp(G)
        gsx, gtop, grep = temp(G + 8 - TOPG), temp(8), temp(G + 8 - TOPG)
        gmask, gpen = temp(G), temp(G)
        sfx = sb("sfx", [P, NT, E + 8 - TOPK])
        stop8 = sb("stop8", [P, NT, 8])
        srep = sb("srep", [P, NT, E + 8 - TOPK])
        mask = sb("mask", [P, NT, E])
        mask16 = sb("mask16", [P, NT, E], BF16)
        tri16 = sb("tri16", [P, P], BF16)
        ones16 = sb("ones16", [P, P], BF16)
        iota16 = sb("iota16", [P, P], F16)
        cmp8 = sb("cmp8", [P, E, G])
        ntile = sb("ntile", [P, E])
        incl = sb("incl", [P, E])
        onesE = sb("onesE", [P, E])
        base = sb("base", [P, E])
        pos = sb("pos", [P, NT, E])
        ptop = sb("ptop", [P, NT, 8])
        pidx = sb("pidx", [P, NT, 8], I32)
        pint = sb("pint", [P, 2, NT, 8], I32)
        pflt = sb("pflt", [P, 2, NT, 8])
        wk = sb("wk", [P, NT, TOPK])
        OS = 8
        onehot_s = sb("onehot_s", [P, OS, P], F16)
        OJ = TB * TOPK
        onehot_j = nc.alloc_sbuf_tensor_at("onehot_j", [P, OJ, SLOT_TILES + 1], F16, offset=norm_at + 4 * TB * C)
        assert OJ * (SLOT_TILES + 1) <= 2 * TB * C
        ejcmp = sb("ejcmp", [SLOT_TILES, E])
        ej = sb("ej", [SLOT_TILES, 1])
        eoff = sb("eoff", [1, SLOT_TILES + 8], I32)
        gidx = sb("gidx", [P, SLOT_TILES + 1], U32)
        last_quad = sb("last_quad", [1, 1], I32)
        tile_idx = [sb(f"tile_idx{i}", [P, 1], U32) for i in range(4)]

        EARLY = 14
        take = carve(DN0, EARLY * GUW)
        X = take(NT * C).rearrange("p (t c) -> p t c", t=NT)
        rvk = take(CT * 3 * C).rearrange("p (k n) -> p k n", k=CT)
        wout = take(CT * C).rearrange("p (k n) -> p k n", k=CT)
        kS = [take(S) for _ in range(2)]
        vS = [take(S) for _ in range(2)]
        er = [take(S) for _ in range(2)]
        O = take(S + 1)
        Q = take(S + 1)
        PP = take(S + 1)
        z, t1, t2, rz, mz, Bv = [take(S) for _ in range(6)]
        sign0 = take(B * C).rearrange("p (b c) -> p b c", b=B)
        wm0 = arena[:, DN0 - 6 * C * CT:DN0].rearrange("p (k n) -> p k n", k=CT)

        take1 = carve(E * (GUW + DNW), 0)
        YG = 4
        tiles = lambda v, n: v.rearrange("p (i n) -> p i n", i=n)
        def parts(name, n, k):
            w, l = take1(n, name + "l")
            return [tiles(v, k) for v in (w, l, take1(n, name + "h")[1])]

        w1w, w1l = [tiles(v, CT) for v in take1(CT * R, "w1l")]
        o = len(CONV_K) * R
        conv_mem = take1(2 * o + (2 + RT) * SW, "conv_r")
        fhw, fhl = [tiles(v[:, 0:HT * S], HT) for v in conv_mem]
        fhh = tiles(conv_mem[1][:, HT * S:2 * HT * S], HT)
        convw, convl = [tiles(v[:, 0:o], len(CONV_K)) for v in conv_mem]
        convh = tiles(conv_mem[1][:, o:2 * o], len(CONV_K))
        h1_cols = lambda v, r: [v[:, 2 * o + i * SW:2 * o + (i + 1) * SW] for i in r]
        h1w, h1l = [h1_cols(v, range(2)) for v in conv_mem]
        h1h = h1_cols(conv_mem[1], range(2, 2 + RT))
        assert CT * R + len(CONV_K) * R <= SURE_QUADS // 2 * GUW
        X2 = take1(NT * C).rearrange("p (t c) -> p t c", t=NT)
        w2w, w2l, w2h = parts("w2", RT * C, RT)
        gatew, gatel, gateh = parts("gate", RT * 2 * R, RT)
        f2w, f2l = [tiles(v, HT) for v in take1(HT * C, "f2l")]
        f2t, f2h = [tiles(v, HT) for v in take1(HT * C, "f2h")]
        f13_mem = take1(2 * CT * 2 * H, "f13_r")
        f13w, f13l = [tiles(v[:, 0:CT * 2 * H], CT) for v in f13_mem]
        f13h = tiles(f13_mem[1][:, CT * 2 * H:], CT)
        wm1 = tiles(f13_mem[0][:, 0:CT * 6 * C], CT)
        modrow1 = f13_mem[0][0:B, CT * 6 * C:CT * 6 * C + 6 * C]
        hch, hcl = [tiles(take1(RT * S, n)[1], RT) for n in ("hch", "hcl")]
        yg_mem = [take1(TOPK * C, n) for n in ("hsh", "hsl", None, None)]
        yg_w = [m[0] if i < 2 else m for i, m in enumerate(yg_mem)]
        yg = [tiles(m, TOPK) for m in yg_w]
        rS, iS, aS, a2 = [tiles(m[:, 0:RT * S], RT) for m in yg_w]
        hsh, hsl = [tiles(m[1][:, 0:RT * S], RT) for m in yg_mem[0:2]]
        x_r = rounded("x_r", hT_at, CT, 2 * S)
        xh, xl, xw = x_r[:, :, 0:S], x_r[:, :, S:2 * S], hT[:, :, S:2 * S]
        hc = tiles(sh_mem[:, 0:RT * S], RT)
        h1w.append(sh_mem[:, RT * S:RT * S + SW])
        h1l.append(rounded("h1l2", sh_mem_at + 4 * RT * S, SW))
        fsil = [tile_mem[:, i * S:(i + 1) * S] for i in range(2)]
        tmp1 = [tile_mem[:, i * S:(i + 1) * S] for i in (2, 3)]
        w1h = rounded("w1h", tile_mem_at + 4 * 4 * S, CT, R)
        ga1 = tile_mem[:, 4 * S + CT * R:4 * S + CT * R + B * C].rearrange("p (b n) -> p b n", b=B)
        gb1 = gb0
        sp = sb("sp", [P, 6, RT])

        par_in, rvk_in, wout_in, route_in, sh_in = [sem(n) for n in (
            "par_in", "rvk_in", "wout_in", "route_in", "sh_in")]
        wm0_in = [sem(f"wm0_in{n}") for n in range(3)]
        x_in_s = [sem(f"x_in{b}") for b in range(B)]
        gu_early, gu_late, dn_in = sem("gu_early"), sem("gu_late"), sem("dn_in")
        y_filled = sem("y_filled")
        quads_ready = sem("quads_ready")
        mod_out = [sem(f"mod_out{i}") for i in range(2)]
        modB_in = [sem(f"modB_in{i}") for i in range(2)]
        h2_ready = sem("h2_ready")
        h2_out, x1_out, x1_in = sem("h2_out"), sem("x1_out"), sem("x1_in")
        xg_in = [sem(f"xg_in{i}") for i in range(4)]
        y_out = [sem(f"y_out{i}") for i in range(2)]
        yg_in = [[sem(f"yg_in{i}_{half}") for half in range(2)] for i in range(YG)]
        wm1_in, w1_in, conv_in, gate_in, w2_in, f13_in, f2_in, out_out = [sem(n) for n in (
            "wm1_in", "w1_in", "conv_in", "gate_in", "w2_in", "f13_in", "f2_in", "out_out")]
        act_step, dve_step, pool_step = sem("act_step"), sem("dve_step"), sem("pool_step")
        silc_ready = sem("silc_ready")
        modps_done = sem("modps_done")
        modrow_ready = sem("modrow_ready")
        modT_done = sem("modT_done")
        modcol_ready = sem("modcol_ready")
        modB_floored = sem("modB_floored")
        ve_ready, rstd_ready = sem("ve_ready"), sem("rstd_ready")
        norm_ready = sem("norm_ready")
        normT_done = sem("normT_done")
        hT_ready = sem("hT_ready")
        rvk_done = sem("rvk_done")
        kvr_ready = sem("kvr_ready")
        exparg_ready = sem("exparg_ready")
        tv_ready = sem("tv_ready")
        mzv_ready = sem("mzv_ready")
        exp_ready = sem("exp_ready")
        yT_ready = sem("yT_ready")
        proj_done = sem("proj_done")
        x_done = sem("x_done")
        logit_done, score_ready = sem("logit_done"), sem("score_ready")
        mask_ready, rank_done = sem("mask_ready"), sem("rank_done")
        ej_ready, ejT_done, eoff_ready = sem("ej_ready"), sem("ejT_done"), sem("eoff_ready")
        onehot_ready, onehot_used = sem("onehot_ready"), sem("onehot_used")
        onehot_j_ready = sem("onehot_j_ready")
        tile_token_ready = sem("tile_token_ready")
        gidx_ready = sem("gidx_ready")
        shps_done, shsil_ready, shhid_ready = sem("shps_done"), sem("shsil_ready"), sem("shhid_ready")
        shy_done, shy_ready = sem("shy_done"), sem("shy_ready")
        tx_done, xgT_ready, gu_done, sil_ready, hid_ready, th_done, hidT_ready, dn_done, y_ready = [
            sem(n) for n in ("tx_done", "xgT_ready", "gu_done", "sil_ready", "hid_ready", "th_done",
                             "hidT_ready", "dn_done", "y_ready")]
        tile_idx_ready, gathers_begun = sem("tile_idx_ready"), sem("gathers_begun")
        comb_done = sem("comb_done")
        w1_done, h1_ready, conv_done = sem("w1_done"), sem("h1_ready"), sem("conv_done")
        gates_done, gates_ready, a_ready, a2_ready, mult_ready, hs_ready = [sem(n) for n in (
            "gates_done", "gates_ready", "a_ready", "a2_ready", "mult_ready", "hs_ready")]
        had_done, had_ready, f2_ready = sem("had_done"), sem("had_ready"), sem("f2_ready")
        mhalf_ready, sp_ready, pads_ready, ix_ready, a2min_ready = [sem(n) for n in (
            "mhalf_ready", "sp_ready", "pads_ready", "ix_ready", "a2min_ready")]
        hT_whole, h1_whole, hc_whole = sem("hT_whole"), sem("h1_whole"), sem("hc_whole")
        (w1_high, w1_low, conv_high, conv_low, gate_high, gate_low, w2_high, w2_low, f13_high, f13_low,
         f2_high, f2_low, hT_low, h1_low, hc_high, hc_low, hs_high, hs_low, fhid_high, fhid_low) = [sem(n) for n in (
             "w1_high", "w1_low", "conv_high", "conv_low", "gate_high", "gate_low", "w2_high", "w2_low",
             "f13_high", "f13_low", "f2_high", "f2_low", "hT_low", "h1_low", "hc_high", "hc_low",
             "hs_high", "hs_low", "fhid_high", "fhid_low")]
        ones_ready = sem("ones_ready")
        fps_done, fsil_ready, fhid_ready = sem("fps_done"), sem("fsil_ready"), sem("fhid_ready")

        def counter(eng, s):
            n = [0]

            def step(ins):
                ins.then_inc(s, 1)
                n[0] += 1
                return n[0]

            def settle(k=None):
                eng.wait_ge(s, n[0] if k is None else k)
            return step, settle

        def load_last(eng):
            eng.wait_ge(quads_ready, 1)
            return eng.value_load(last_quad[0:1, 0:1], min_val=SURE_QUADS - 1, max_val=QUADS - 1)

        block = ctx.enter_context(nc.Block())

        @block.sync
        def _(sp_):
            sp_.dma_start(par[:, :], small).then_inc(par_in, 16)
            sp_.dma_start(con[:, :], consts).then_inc(par_in, 16)
            xv = x_in.rearrange("(t p) c -> p t c", p=P)
            sp_.dma_start(X[:, 0:TB, :], xv[:, 0:TB, :]).then_inc(x_in_s[0], 16)
            sp_.dma_start(wm0[:, :, 0:512], wmod0[:, :, 0:512]).then_inc(wm0_in[0], 16)
            sp_.dma_start(rvk, w_rvk).then_inc(rvk_in, 16)
            for n in range(1, 3):
                sp_.dma_start(wm0[:, :, n * 512:(n + 1) * 512], wmod0[:, :, n * 512:(n + 1) * 512]).then_inc(wm0_in[n], 16)
            sp_.dma_start(X[:, TB:NT, :], xv[:, TB:NT, :]).then_inc(x_in_s[1], 16)
            sp_.dma_start(wout, w_out).then_inc(wout_in, 16)
            sp_.dma_start(router[:, :, :], w_router).then_inc(route_in, 16)
            sp_.dma_start(cbias[:, :], corr_bias).then_inc(route_in, 16)
            sp_.dma_start(shgu[:, :, :], w_shgu).then_inc(sh_in, 16)
            sp_.dma_start(shdn[:, :, :], w_shdn).then_inc(sh_in, 16)

            sp_.wait_ge(modrow_ready, 3)
            sp_.dma_start(mod_dram[0], modrow0).then_inc(mod_out[0], 16)
            sp_.wait_ge(mod_out[0], 16)
            for b in range(B):
                for dst, chunk in ((modB0[:, b, 0:C], GA), (modB0[:, b, C:3 * C], SB), (gb0[:, b, :], GB)):
                    n = dst.shape[-1]
                    src = mod_dram[0][b:b + 1, chunk * C:chunk * C + n].to_broadcast([P, n])
                    sp_.dma_start(dst, src).then_inc(modB_in[0], 16)

            guv = w_gu.rearrange("p (e n) -> p e n", e=E)
            step_e = 7
            for e in range(0, EARLY, step_e):
                sp_.dma_start(gu[:, e * GUW:(e + step_e) * GUW], guv[:, e:e + step_e, :].rearrange("p e n -> p (e n)")).then_inc(gu_early, 16)
            for e in range(0, E, 8):
                sp_.dma_start(dn[:, e * DNW:(e + 8) * DNW], w_dn[:, e * DNW:(e + 8) * DNW]).then_inc(dn_in, 16)

            h2v = h2_dram.rearrange("(t p) c -> p t c", p=P)
            for b in range(B):
                sp_.wait_ge(x_done, b + 1)
                sp_.dma_start(x1_dram[:, b * TB * C:(b + 1) * TB * C],
                              X[:, b * TB:(b + 1) * TB, :].rearrange("p t c -> p (t c)")).then_inc(x1_out, 16)
                sp_.wait_ge(h2_ready, b + 1)
                sp_.dma_start(h2v[:, b * TB:(b + 1) * TB, :], norm[:, b * TB:(b + 1) * TB, :]).then_inc(h2_out, 16)
            sp_.wait_ge(x1_out, 16 * B)
            for e in range(EARLY, E, 6):
                sp_.dma_start(gu[:, e * GUW:(e + 6) * GUW], w_gu[:, e * GUW:(e + 6) * GUW]).then_inc(gu_late, 16)

            def store(j, r):
                sp_.wait_ge(y_ready, j + 1)
                dst = y_dram.rearrange("(j p) c -> j p c", p=P)[bass.ds(j, 1), :, :]
                sp_.dma_start(dst.rearrange("a p c -> p (a c)"), yt[r % 2]).then_inc(y_out[r % 2], 16)

            last_q = load_last(sp_)
            with sp_.Fori(SURE_QUADS, QUADS) as q:
                with sp_.If(q <= last_q):
                    sp_.sem_inc(y_filled, 16)
                with sp_.Else():
                    dst = y_dram.rearrange("(q r p) c -> q p r c", r=4, p=P)[bass.ds(q, 1), :, :, :]
                    sp_.dma_start(dst.rearrange("a p r c -> p (a r) c"),
                                  con[:, 0:C].unsqueeze(1).to_broadcast([P, 4, C])).then_inc(y_filled, 16)
            with sp_.Fori(0, SURE_QUADS) as q:
                for r in range(4):
                    store(4 * q + r, r)
            sp_.wait_ge(dn_done, 4 * SURE_QUADS)
            sp_.dma_start(w1w, w_1).then_inc(w1_in, 16)
            for k in range(0, len(CONV_K), 2):
                sp_.dma_start(convw[:, k:k + 2, :], w_conv[:, k:k + 2, :]).then_inc(conv_in, 16)
            with sp_.Fori(SURE_QUADS, QUADS) as q:
                with sp_.If(q <= last_q):
                    for r in range(4):
                        store(4 * q + r, r)

            sp_.wait_ge(dn_done, 4 * last_q + 4)
            for k in range(CT):
                sp_.dma_start(wm1[:, k, :], wmod1[:, k, :]).then_inc(wm1_in, 16)
            for b in range(B):
                half = slice(b * TB * C, (b + 1) * TB * C)
                sp_.dma_start(X2.rearrange("p t c -> p (t c)")[:, half], x1_dram[:, half]).then_inc(x1_in, 16)
            sp_.wait_ge(yg_in[0][1], 16 * TOPK // 2)
            for k in range(0, HT, 4):
                sp_.dma_start(f2w[:, k:k + 4, :], w_f2[:, k:k + 4, :]).then_inc(f2_in, 16)
            sp_.dma_start(w2w, w_2).then_inc(w2_in, 16)
            sp_.wait_ge(modrow_ready, 6)
            sp_.dma_start(mod_dram[1], modrow1).then_inc(mod_out[1], 16)
            sp_.wait_ge(mod_out[1], 16)
            for i in range(2):
                sp_.wait_ge(y_out[i], 32 * last_q + 32)
            for b in range(B):
                src = mod_dram[1][b:b + 1, GA * C:(GA + 1) * C].to_broadcast([P, C])
                sp_.dma_start(ga1[:, b, :], src).then_inc(modB_in[1], 16)
            for i in range(RT):
                sp_.dma_start(gatew[:, i, :], w_gates[:, i, :]).then_inc(gate_in, 16)
            sp_.wait_ge(comb_done, NT)
            for b in range(B):
                src = mod_dram[1][b:b + 1, GB * C:(GB + 1) * C].to_broadcast([P, C])
                sp_.dma_start(gb1[:, b, :], src).then_inc(modB_in[1], 16)
            for k in range(CT):
                for h in range(2):
                    sp_.dma_start(f13w[:, k, h * H:(h + 1) * H], w_f13[:, k, h * H:(h + 1) * H]).then_inc(f13_in, 16)

            ov = out.rearrange("(t p) c -> p t c", p=P)
            for b in range(B):
                sp_.wait_ge(x_done, 2 * B + b + 1)
                sp_.dma_start(ov[:, b * TB:(b + 1) * TB, :], X2[:, b * TB:(b + 1) * TB, :]).then_inc(out_out, 16)
            sp_.wait_ge(out_out, 16 * B)

        @block.tensor
        def _(pe):
            def mod_rows(layer, ns):
                wm = (wm0, wm1)[layer]
                for n in ns:
                    if layer == 0:
                        pe.wait_ge(wm0_in[n], 16)
                    elif n == 0:
                        pe.wait_ge(wm1_in, 16 * CT)
                    for k in range(CT):
                        mm = pe.matmul(bank[2 + n][0:B, :], silc[:, 4 * layer + B * k:4 * layer + B * (k + 1)],
                                       wm[:, k, n * 512:(n + 1) * 512], start=(k == 0), stop=(k == CT - 1))
                    mm.then_inc(modps_done, 1)

            def mod_cols(chunks, row, rows):
                pe.wait_ge(modrow_ready, rows)
                for n in chunks:
                    for h in range(CT):
                        j = CT * n + h
                        mm = pe.transpose(bank[5][:, B * j:B * (j + 1)], row[:, j * P:(j + 1) * P], ident[0:B, 0:B])
                mm.then_inc(modT_done, 1)

            def transposes(n, b, wait_free, banks=(0, 1)):
                pe.wait_ge(norm_ready, n + 1)
                if wait_free is not None:
                    pe.wait_ge(*wait_free)
                for c in range(CT):
                    for t in range(TB):
                        mm = pe.transpose(bank[banks[c]][:, t * P:(t + 1) * P], norm[:, b * TB + t, c * P:(c + 1) * P], ident)
                    mm.then_inc(normT_done, 1)

            def project(src, w, ks, b, rows, banks=(0, 1)):
                for t in range(TB):
                    for k in range(ks):
                        mm = pe.matmul(bank[banks[t // 2]][:, (t % 2) * C:(t % 2 + 1) * C], src(k, t), w[0:rows[k], k, :],
                                       start=(k == 0), stop=(k == ks - 1))
                mm.then_inc(proj_done, 1)

            pe.wait_ge(par_in, 32)
            pe.wait_ge(silc_ready, 1)
            mod_rows(0, range(1))
            mod_cols((SA, CA), modrow0, 1)

            for b in range(B):
                transposes(b, b, (hT_ready, CT * b) if b else None)
                if b == 0:
                    mod_rows(0, range(1, 3))
                pe.wait_ge(hT_ready, CT * (b + 1))
                if b == 0:
                    pe.wait_ge(rvk_in, 16)
                    pe.wait_ge(modrow_ready, 3)
                for c in range(CT):
                    if b == 0 and c == 1:
                        mod_cols((SB, CB), modrow0, 3)
                        pe.wait_ge(modcol_ready, 2)
                    for i, part in enumerate((2, 1, 0)):
                        m0 = part * C + c * P
                        if b:
                            pe.wait_ge(kvr_ready, 3 * c + i + 1)
                        for k in range(CT):
                            mm = pe.matmul(bank[2 + 3 * c + i][:, :], rvk[:, k, m0:m0 + P],
                                           hT[:, k, b * S:(b + 1) * S], start=(k == 0), stop=(k == CT - 1))
                        mm.then_inc(rvk_done, 1)
            pe.wait_ge(wout_in, 16)
            pe.wait_ge(hT_ready, CT * B)
            for b in range(B):
                pe.wait_ge(yT_ready, CT * (b + 1))
                project(lambda k, t: hT[:, k, b * S + t * P:b * S + (t + 1) * P], wout, CT, b, [P] * CT, ((0, 1), (2, 3))[b])
            pe.wait_ge(route_in, 32)
            for b in range(B):
                transposes(B + b, b, (x_done, b + 1))
                pe.wait_ge(hT_ready, CT * (B + b + 1))
                for t in range(b * TB, (b + 1) * TB):
                    for k in range(CT):
                        mm = pe.matmul(bank[6][:, t * E:(t + 1) * E], hT[:, k, t * P:(t + 1) * P], router[:, k, :],
                                       start=(k == 0), stop=(k == CT - 1))
            mm.then_inc(logit_done, 1)

            def shared_in(b, parts):
                for m, h in (divmod(i, 2) for i in parts):
                    c0 = h * SHM + m * P
                    for k in range(CT):
                        mm = pe.matmul(bank[2 + 2 * m + h][0:SH_ROWS[m], :], shgu[:, k, c0:c0 + SH_ROWS[m]],
                                       hT[:, k, b * S:(b + 1) * S], start=(k == 0), stop=(k == CT - 1))
                    mm.then_inc(shps_done, 1)

            def shared_out(b, banks, ts):
                for t in ts:
                    for k in range(SHT):
                        mm = pe.matmul(bank[banks[t // 2]][:, (t % 2) * C:(t % 2 + 1) * C],
                                       sh_hid[0:SH_ROWS[k], k, t * P:(t + 1) * P], shdn[0:SH_ROWS[k], k, :],
                                       start=(k == 0), stop=(k == SHT - 1))
                if ts[-1] == TB - 1:
                    mm.then_inc(shy_done, 1)

            pe.wait_ge(sh_in, 32)
            pe.wait_ge(kvr_ready, 3 * CT * B)
            shared_in(0, range(3))
            pe.wait_ge(mask_ready, 1)
            m16 = mask16[:, :, :].rearrange("p t e -> p (t e)")
            pe.matmul(bank[0][:, 0:NT * E], tri16[:, :], m16, start=True, stop=False, skip_group_check=True)
            for d in range(1, NT):
                pe.matmul(bank[0][:, d * E:NT * E], ones16[:, :], m16[:, 0:(NT - d) * E], start=False,
                          stop=(d == NT - 1), skip_group_check=True)
            for t in range(NT):
                mm = pe.matmul(bank[1][:, 0:E], ones16[:, :], m16[:, t * E:(t + 1) * E], start=(t == 0), stop=(t == NT - 1))
            mm.then_inc(rank_done, 1)
            pe.wait_ge(score_ready, 1)
            shared_in(0, range(3, 2 * SHT))
            pe.wait_ge(ej_ready, 1)
            pe.transpose(bank[1][0:1, 256:256 + SLOT_TILES], ej[:, :], ident[0:SLOT_TILES, 0:SLOT_TILES]).then_inc(ejT_done, 1)
            pe.wait_ge(shhid_ready, SHT)
            shared_out(0, (2, 3), range(1))
            for n in range(NT * TOPK):
                if n % TOPK == 0:
                    pe.wait_ge(tile_token_ready, n // TOPK + 1)
                pe.wait_ge(onehot_ready, n + 1)
                pe.matmul(bank[1][:, 128:128 + SLOT_TILES + 1], onehot_s[:, n % OS, :], onehot_j[:, n % OJ, :],
                          start=(n == 0), stop=(n == NT * TOPK - 1)).then_inc(onehot_used, 1)
                t, k = divmod(n, TOPK)
                if k == TOPK - 1 and 1 <= t < TB:
                    shared_out(0, (2, 3), range(t, t + 1))

            def tx(q, r):
                pe.wait_ge(xg_in[r], 16 * (q + 1))
                for c in range(CT):
                    mm = pe.transpose(bank[r % 2][:, c * P:(c + 1) * P], xg[r][:, c * P:(c + 1) * P], ident)
                mm.then_inc(tx_done, 1)

            def gate_up(q, r, e):
                pe.wait_ge(xgT_ready, 4 * q + (r + 1))
                for k in range(CT):
                    mm = pe.matmul(bank[2 + r % 2][:, 0:2 * M], xgT[r % 2][:, k * P:(k + 1) * P],
                                   gu[:, bass.ds(e[k], 2 * M)], start=(k == 0), stop=(k == CT - 1))
                mm.then_inc(gu_done, 1)

            def th(q, r):
                pe.wait_ge(hid_ready, 4 * q + (r + 1))
                for k in range(2):
                    mm = pe.transpose(bank[4 + r % 2][0:MH, k * P:(k + 1) * P], hid[r % 2][:, k * MH:(k + 1) * MH], ident)
                mm.then_inc(th_done, 1)

            def down(q, r, e):
                pe.wait_ge(hidT_ready, 4 * q + (r + 1))
                if not early(q, r, 2):
                    pe.wait_ge(y_ready, 4 * q + (r - 1))
                for k in range(2):
                    mm = pe.matmul(bank[6 + r % 2][:, 0:C], hidT[r % 2][:, k * P:(k + 1) * P],
                                   dn[:, bass.ds(e[2 + k], C)], start=(k == 0), stop=(k == 1))
                mm.then_inc(dn_done, 1)

            regs = [pe.alloc_register(f"expert{i}") for i in range(5)]

            def blocks(i):
                e = pe.snap(regs[i], min_val=0, max_val=E - 1)
                return [pe.snap(e * GUW + k * 2 * M) for k in range(CT)] + [pe.snap(e * DNW + k * C) for k in range(2)]

            def quad(q, first=False):
                pe.load(regs[0:4], eoff[0:1, bass.ds(4 * q, 4)])
                e_prev, e_next = blocks(0), blocks(1)
                for r in range(4):
                    e_now = e_next
                    if r == 1:
                        pe.load(regs[4], eoff[0:1, bass.ds(4 * q + 4, 1)])
                    tx(*near(q, r, 1))
                    if not (first and r == 0):
                        th(*near(q, r, -1))
                    gate_up(q, r, e_now)
                    if r < 3:
                        e_next = blocks(r + 2)
                    if not (first and r == 0):
                        down(*near(q, r, -1), e_prev)
                    e_prev = e_now

            pe.wait_ge(eoff_ready, 1)
            pe.wait_ge(gidx_ready, 1)
            pe.wait_ge(shy_ready, 1)
            pe.wait_ge(gu_early, 16 * 2)
            pe.wait_ge(gu_late, 16 * 3)
            pe.wait_ge(dn_in, 16 * 4)
            last_q = load_last(pe)
            tx(0, 0)
            quad(0, first=True)
            with pe.Fori(1, SURE_QUADS) as q:
                quad(q)
            with pe.Fori(0, (QUADS + 1 - SURE_QUADS) // TAIL) as g:
                with pe.If(TAIL * g + SURE_QUADS <= last_q + 1):
                    with pe.Fori(0, TAIL) as i:
                        q = TAIL * g + i + SURE_QUADS
                        with pe.If(q <= last_q):
                            quad(q)
                        with pe.If(q == last_q + 1):
                            pe.load(regs[4], eoff[0:1, bass.ds(4 * q, 1)])
                            e = blocks(4)
                            th(*near(q, 0, -1))
                            down(*near(q, 0, -1), e)
                    pe.nop()

            pe.wait_ge(y_ready, 4 * last_q + 4)
            pe.wait_ge(xgT_ready, 4 * last_q + 5)
            shared_in(1, range(2 * SHT))
            pe.wait_ge(shhid_ready, 2 * SHT)
            mod_rows(1, range(3))
            shared_out(1, (0, 1), range(TB))
            mod_cols((SA, CA, SB, CB), modrow1, 6)
            pe.wait_ge(f2_in, 32)
            pe.wait_ge(modrow_ready, 6)
            for h in range(HT):
                mm = pe.matmul(bank[(6, 7, 2, 3)[h // 2]][:, (h % 2) * C:(h % 2 + 1) * C],
                               con[:, K_HAD:K_HAD + P], f2w[:, h, :], start=True, stop=True)
                if h % 2:
                    mm.then_inc(had_done, 1)

            def products(*groups):
                for i, (wi, xi) in enumerate(((0, 0), (1, 0), (0, 1))):
                    for dst, w, x, w_first, waits, done in groups:
                        for k, pair in enumerate(zip(w[wi], x[xi])):
                            for at, signal, count in waits.get(i, ()):
                                if at == k:
                                    pe.wait_ge(signal, count)
                            lhs, rhs = pair if w_first else pair[::-1]
                            mm = pe.matmul(dst, lhs, rhs, start=(i == 0 and k == 0), stop=(i == 2 and k == len(w[0]) - 1),
                                           skip_group_check=len(groups) > 1)
                        if i == 2 and done is not None:
                            mm.then_inc(done, 1)

            def both(h, l, get):
                return get(h), get(l)

            def hidden1(b):
                pe.wait_ge(had_ready, 4)
                pe.wait_ge(w1_high, 1)
                if b:
                    pe.wait_ge(h1_whole, RT)
                waits = {0: [(k, hT_ready, CT * (4 + b) + k + 1) for k in range(CT)], 1: [(0, w1_low, 1)],
                         2: [(k, hT_low, CT * b + k + 1) for k in range(CT)]}
                products(*[(bank[2 + m][0:R_ROWS[m], :],
                            both(w1h, w1l, lambda v: [v[:, k, m * P:m * P + R_ROWS[m]] for k in range(CT)]),
                            both(xh, xl, lambda v: [v[:, k, :] for k in range(CT)]),
                            True, waits if m == 0 else {}, w1_done) for m in range(RT)])

            def conv(b, ms):
                pe.wait_ge(conv_high, 1)
                for m in ms:
                    if b and m == 1:
                        pe.wait_ge(gates_ready, 2 * RT)
                    waits = {0: [(k, h1_ready, RT * b + i + 1) for k, (i, o) in enumerate(CONV_K) if o == 0],
                             1: [(0, conv_low, 1)],
                             2: [(k, h1_low, RT * b + i + 1) for k, (i, o) in enumerate(CONV_K) if o == 0]}
                    products((bank[(7, 5, 6)[m]][0:R_ROWS[m], :],
                              both(convh, convl, lambda v: [v[:, k, m * P:m * P + R_ROWS[m]] for k in range(len(CONV_K))]),
                              both(h1h, h1l, lambda v: [v[i][:, o:o + S] for i, o in CONV_K]),
                              True, waits if m == ms[0] else {}, conv_done))

            def gates(b):
                pe.wait_ge(gate_high, 1)
                waits = {0: [(k, hc_high, RT * b + k + 1) for k in range(RT)], 1: [(0, gate_low, 1)],
                         2: [(k, hc_low, RT * b + k + 1) for k in range(RT)]}
                for i, ms in enumerate(GATE_ORDER[b]):
                    if b == 0 and i:
                        pe.wait_ge(h1_whole, 2 * RT)
                    if b and i:
                        pe.wait_ge(hc_whole, RT * 2)
                    products(*[(bank[2 + m][:, :],
                                both(gateh, gatel, lambda v: [v[0:R_ROWS[i], i, m * P:(m + 1) * P] for i in range(RT)]),
                                both(hch, hcl, lambda v: [v[0:R_ROWS[i], i, :] for i in range(RT)]),
                                True, waits if i == 0 and m == ms[0] else {}, gates_done) for m in ms])

            def project3(data, w, free, waits, ts=range(TB)):
                if free:
                    pe.wait_ge(*free)
                for t in ts:
                    products((bank[t // 2][:, (t % 2) * C:(t % 2 + 1) * C], w, data(t), False,
                              waits if t == ts[0] else {}, proj_done if t == TB - 1 else None))

            def recur_out(b, free):
                pe.wait_ge(ones_ready, 1)
                pe.wait_ge(w2_high, 1)
                rows = (P, P, R_ROWS[2] + 1)
                project3(lambda t: both(hsh, hsl, lambda v: [v[0:rows[k], k, t * P:(t + 1) * P] for k in range(RT)]),
                         both(w2h, w2l, lambda v: [v[0:rows[k], k, :] for k in range(RT)]), free,
                         {0: [(k, hs_high, RT * b + k + 1) for k in range(RT)], 1: [(0, w2_low, 1)],
                          2: [(k, hs_low, RT * b + k + 1) for k in range(RT)]})

            def ffn_in(b, hs_):
                x = both(xh, xl, lambda v: [v[:, k, :] for k in range(CT)])
                for pair in [(h,) for h in hs_] if hs_[0] else [(0, 1)] + [(h,) for h in hs_[2:]]:
                    n = HT * b + pair[-1]
                    if n >= 3:
                        pe.wait_ge(fhid_ready, n - 2)
                    waits = {0: [(0, f13_high, CT)] + [(k, hT_ready, CT * (6 + b) + k + 1) for k in range(CT)],
                             1: [(0, f13_low, CT)], 2: [(k, hT_low, CT * (2 + b) + k + 1) for k in range(CT)]}
                    products(*[(bank[2 + 2 * ((HT * b + h) % 3) + up][:, :],
                                both(f13h, f13l, lambda v: [v[:, k, up * H + h * P:up * H + (h + 1) * P] for k in range(CT)]),
                                x, True, waits if h == 0 and up == 0 else {}, fps_done) for h in pair for up in range(2)])

            def ffn_out(b, free, ts):
                waits = {0: [(0, f2_high, 1)] + [(k, fhid_high, HT * b + k + 1) for k in range(HT)],
                         1: [(0, f2_low, 1)], 2: [(k, fhid_low, HT * b + k + 1) for k in range(HT)]}
                project3(lambda t: both(fhh, fhl, lambda v: [v[:, k, t * P:(t + 1) * P] for k in range(HT)]),
                         both(f2h, f2l, lambda v: [v[:, k, :] for k in range(HT)]), free, waits if ts[0] == 0 else {}, ts)

            transposes(4, 0, (shy_ready, 2))
            hidden1(0)
            conv(0, range(RT))
            transposes(5, 1, (hT_whole, CT))
            hidden1(1)
            gates(0)
            conv(1, range(2))
            recur_out(0, (hT_whole, CT * 2))
            conv(1, range(2, RT))
            gates(1)
            transposes(6, 0, (x_done, 3))
            pe.wait_ge(gates_ready, 2 * RT * B)
            ffn_in(0, range(6))
            recur_out(1, (hT_whole, CT * 3))
            ffn_in(0, range(6, HT))
            ffn_out(0, (x_done, 4), range(2))
            transposes(7, 1, (fhid_ready, HT), (4, 5))
            ffn_out(0, None, range(2, TB))
            pe.wait_ge(hT_whole, CT * 4)
            ffn_in(1, range(HT))
            ffn_out(1, (x_done, 5), range(TB))

        @block.scalar
        def _(act):
            step, settle = counter(act, act_step)
            act.wait_ge(par_in, 32)
            act.activation(silc[:, :], par[:, P_C0:P_C0 + 8], ACT.Silu).then_inc(silc_ready, 1)
            step(act.activation(wneg[:, :], par[:, P_TD:P_TD + CT], ACT.Exp))
            settle()
            step(act.activation(wneg[:, :], wneg[:, :], ACT.Copy, scale=-1.0))

            def modulated(n, b, layer, sh, sc, banks=(0, 1)):
                if n in (0, 2, 4):
                    act.wait_ge(modcol_ready, n // 2 + 1)
                if layer == 1:
                    for dst, done in (([xh[:, c, :] for c in range(CT)], hT_ready),
                                      ([xw[:, c, :] for c in range(CT)], hT_whole)):
                        for c in range(CT):
                            if done is hT_ready:
                                act.wait_ge(normT_done, CT * n + c + 1)
                            act.activation(dst[c], bank[banks[c]][:, :], ACT.Identity,
                                           bias=modcol[:, layer, CT * sh + c, b:b + 1],
                                           scale=modcol[:, layer, CT * sc + c, b:b + 1]).then_inc(done, 1)
                    return
                for c in range(CT):
                    act.wait_ge(normT_done, CT * n + c + 1)
                    dst = hT[:, c, b * S:(b + 1) * S]
                    act.activation(dst, bank[c][:, :], ACT.Identity, bias=modcol[:, layer, CT * sh + c, b:b + 1],
                                   scale=modcol[:, layer, CT * sc + c, b:b + 1]).then_inc(hT_ready, 1)

            def kvr(u):
                if u >= 2:
                    act.wait_ge(yT_ready, u - 1)
                for i, dst in enumerate((kS[u % 2], vS[u % 2], er[u % 2])):
                    act.wait_ge(rvk_done, 3 * u + i + 1)
                    act.activation(dst, bank[2 + 3 * (u % 2) + i][:, :], ACT.Exp if i == 2 else ACT.Copy,
                                   scale=-1.0 if i == 2 else 1.0).then_inc(kvr_ready, 1)

            def exps(u):
                for i, (v, scale, bias) in enumerate(((t1, 1.0, wneg[:, u % 2:u % 2 + 1]), (t2, 1.0, 0.0),
                                                      (rz, -1.0, 0.0), (mz, 1.0, 0.0))):
                    act.wait_ge(exparg_ready, 4 * u + i + 1)
                    act.activation(v, v, ACT.Exp, bias=bias, scale=scale).then_inc(exp_ready, 1)

            modulated(0, 0, 0, SA, CA)
            settle()
            kvr(0)
            exps(0)
            kvr(1)
            modulated(1, 1, 0, SA, CA)
            exps(1)
            kvr(2)
            exps(2)
            kvr(3)
            exps(3)
            modulated(2, 0, 0, SB, CB)
            modulated(3, 1, 0, SB, CB)
            act.wait_ge(logit_done, 1)
            act.activation(scores[:, :, :].rearrange("p t e -> p (t e)"), bank[6][:, 0:NT * E], ACT.Sigmoid)\
               .then_inc(score_ready, 1)

            def shared_silu(b, extra=None):
                for m in range(SHT):
                    n = SHT * b + m
                    act.wait_ge(shps_done, 2 * n + 1)
                    if n:
                        act.wait_ge(shhid_ready, n)
                    act.activation(sh_sil[0:SH_ROWS[m], :], bank[2 + 2 * m][0:SH_ROWS[m], :], ACT.Silu)\
                       .then_inc(shsil_ready, 1)
                    if extra and m == 0:
                        extra()

            def shared_copy(b, banks):
                act.wait_ge(shy_done, b + 1)
                if b == 0:
                    act.wait_ge(h2_out, 16 * B)
                for h in range(2):
                    dst = shared_y[:, b * TB + 2 * h:b * TB + 2 * h + 2, :].rearrange("p t c -> p (t c)")
                    ins = act.activation(dst, bank[banks[h]][:, :], ACT.Copy)
                ins.then_inc(shy_ready, 1)

            act.wait_ge(h2_ready, B)
            shared_silu(0)

            for t in range(NT):
                act.wait_ge(onehot_j_ready, t + 1)
                v = onehot_j[:, t % TB * TOPK:(t % TB + 1) * TOPK, :]
                act.activation(v, v, ACT.Copy, scale=par[:, P_TOK + t:P_TOK + t + 1]).then_inc(tile_token_ready, 1)
            shared_copy(0, (2, 3))

            def copy_x(q, r):
                act.wait_ge(tx_done, 4 * q + (r + 1))
                act.activation(xgT[r % 2], bank[r % 2][:, 0:C], ACT.Copy).then_inc(xgT_ready, 1)

            def tile_silu(q, r):
                act.wait_ge(gu_done, 4 * q + (r + 1))
                act.activation(sil[r % 2], bank[2 + r % 2][:, 0:M], ACT.Silu).then_inc(sil_ready, 1)

            def quad(q):
                for r in range(4):
                    copy_x(*near(q, r, 1))
                    tile_silu(q, r)

            last_q = load_last(act)
            copy_x(0, 0)
            quad(0)
            with act.Fori(1, SURE_QUADS) as q:
                quad(q)
            with act.Fori(SURE_QUADS, QUADS) as q:
                with act.If(q <= last_q):
                    quad(q)

            act.wait_ge(th_done, 4 * last_q + 4)
            def weight_high(h, whole, loaded, done):
                act.wait_ge(*loaded)
                act.activation(h, whole, ACT.Copy).then_inc(done, 1)

            for i in range(2):
                act.wait_ge(y_out[i], 32 * last_q + 32)
            weight_high(w1h, w1w, (w1_in, 16), w1_high)
            shared_silu(1, lambda: weight_high(convh, convw, (conv_in, 16 * len(CONV_K) // 2), conv_high))
            for n in range(3):
                act.wait_ge(modps_done, 3 + n + 1)
                act.activation(modrow1[:, n * 512:(n + 1) * 512], bank[2 + n][0:B, :], ACT.Copy).then_inc(modrow_ready, 1)
            shared_copy(1, (0, 1))

            lam = par[:, P_LAM:P_LAM + RT]
            step(act.activation(sp[:, 0, :], lam, ACT.Abs))
            step(act.activation(sp[:, 1, :], lam, ACT.Relu))
            settle()
            step(act.activation(sp[:, 2, :], sp[:, 0, :], ACT.Exp, scale=-1.0))
            settle()
            step(act.activation(sp[:, 3, :], sp[:, 2, :], ACT.Ln, bias=1.0))
            for i, k in enumerate((6, 7, 2, 3)):
                act.wait_ge(had_done, i + 1)
                act.activation(f2t[:, 2 * i:2 * i + 2, :].rearrange("p h c -> p (h c)"), bank[k][:, :], ACT.Copy)\
                   .then_inc(had_ready, 1)

            def recur_hidden(b):
                if b:
                    act.wait_ge(conv_done, RT)
                for dst, done in ((h1h, h1_ready), (h1w, h1_whole)):
                    for m in range(RT):
                        n = R_ROWS[m]
                        if done is h1_ready:
                            act.wait_ge(w1_done, RT * b + m + 1)
                        places = [dst[m][0:n, PAD:PAD + S]]
                        if m == 2:
                            places.append(dst[m][64:128, PAD - 2:PAD - 2 + S])
                        for v in places:
                            ins = act.activation(v, bank[2 + m][0:n, :], ACT.Silu, bias=par[0:n, P_B1 + m:P_B1 + m + 1])
                        ins.then_inc(done, 1)

            def conv_out(b):
                if b:
                    act.wait_ge(ix_ready, b)
                    act.wait_ge(gates_done, 5 * b)
                for m in range(RT):
                    n = R_ROWS[m]
                    act.wait_ge(conv_done, RT * b + m + 1)
                    for v, done in ((hch[0:n, m, :], hc_high), (hc[0:n, m, :], hc_whole)):
                        act.activation(v, bank[(7, 5, 6)[m]][0:n, :], ACT.Identity,
                                       bias=par[0:n, P_CB + m:P_CB + m + 1]).then_inc(done, 1)

            def gate_sigmoids(b):
                if b:
                    act.wait_ge(proj_done, 3)
                else:
                    act.wait_ge(comb_done, NT)
                order = sum(GATE_ORDER[b], ())
                outs = ((rS[:, 0, :], 0, P_BA, 0), (rS[:, 1, :], 1, P_BA + 1, 0),
                        (iS[:, 0, :], 2, P_BX, 0), (iS[:, 1, :], 3, P_BX + 1, 0),
                        (rS[0:64, 2, :], 4, P_BA + 2, 0), (iS[0:64, 2, :], 4, P_BX + 2, 64))
                for dst, m, k, p0 in sorted(outs, key=lambda v: order.index(v[1])):
                    act.wait_ge(gates_done, 5 * b + order.index(m) + 1)
                    n = dst.shape[0]
                    act.activation(dst, bank[2 + m][p0:p0 + n, :], ACT.Sigmoid, bias=par[p0:p0 + n, k:k + 1])\
                       .then_inc(gates_ready, 1)

            def decays(b):
                act.wait_ge(gates_ready, 2 * RT * (b + 1))
                act.wait_ge(sp_ready, 1)
                for dst, row, done in ((a2, 5, a2_ready), (aS, 4, a_ready)):
                    for m in range(RT):
                        n = R_ROWS[m]
                        act.activation(dst[0:n, m, :], rS[0:n, m, :], ACT.Exp, scale=sp[0:n, row, m:m + 1]).then_inc(done, 1)

            def roots(b):
                act.wait_ge(a2min_ready, 2 * (b + 1))
                for v in (a2[:, 0:2, :], a2[0:64, 2, :]):
                    act.activation(v, v, ACT.Sqrt, bias=1.0, scale=-1.0).then_inc(mult_ready, 1)

            def recur_high(b):
                for m in range(RT):
                    n = R_ROWS[m]
                    act.wait_ge(hs_ready, RT * b + m + 1)
                    act.activation(hsh[0:n, m, :], iS[0:n, m, :], ACT.Copy).then_inc(hs_high, 1)

            def ffn_high(b, h):
                n = HT * b + h
                act.wait_ge(fhid_ready, n + 1)
                act.activation(fhh[:, h, :], fhw[:, h, :], ACT.Copy).then_inc(fhid_high, 1)

            def ffn_silu(b, extra=None):
                for h in range(HT):
                    n = HT * b + h
                    act.wait_ge(fps_done, 2 * n + 1)
                    if n >= 2:
                        act.wait_ge(fhid_ready, n - 1)
                    act.activation(fsil[n % 2], bank[2 + 2 * (n % 3)][:, :], ACT.Silu).then_inc(fsil_ready, 1)
                    if b and h == 1:
                        act.wait_ge(proj_done, 5)
                    if h:
                        ffn_high(b, h - 1)
                    if extra:
                        extra(h)
                ffn_high(b, HT - 1)

            modulated(4, 0, 1, SA, CA)
            act.wait_ge(pads_ready, 1)
            recur_hidden(0)
            weight_high(gateh, gatew, (gate_in, 16 * RT), gate_high)
            weight_high(w2h, w2w, (w2_in, 16), w2_high)
            conv_out(0)
            modulated(5, 1, 1, SA, CA)
            recur_hidden(1)
            for k in range(CT):
                weight_high(f13h[:, k, :], f13w[:, k, :], (f13_in, 16 * 2 * CT), f13_high)
            gate_sigmoids(0)
            decays(0)
            roots(0)
            recur_high(0)
            conv_out(1)
            weight_high(f2h, f2w, (f2_ready, 1), f2_high)
            gate_sigmoids(1)
            decays(1)
            ffn_silu(0, lambda h: h == 1 and roots(1) or h == 3 and recur_high(1))
            modulated(7, 1, 1, SB, CB, (4, 5))
            ffn_silu(1)

        @block.gpsimd
        def _(pool):
            step, settle = counter(pool, pool_step)

            def inverse_root(n):
                ts = slice((n % B) * TB, (n % B + 1) * TB)
                pool.wait_ge(ve_ready, n + 1)
                if n == 0:
                    pool.wait_ge(mhalf_ready, 1)
                pool.tensor_tensor(rstd[:, ts], ve[:, ts], mhalf[:, ts], ALU.pow).then_inc(rstd_ready, 1)

            for n in range(B):
                inverse_root(n)
            def gate_floor(g):
                step(pool.tensor_scalar(sign0, g, 0.0, 2.0, ALU.is_ge, ALU.mult))
                settle()
                step(pool.tensor_scalar(sign0, sign0, -1.0, None, ALU.add))
                settle()
                step(pool.tensor_tensor(g, g, sign0, ALU.mult))
                settle()
                step(pool.tensor_scalar(g, g, 0.25, None, ALU.max))
                settle()
                return step(pool.tensor_tensor(g, g, sign0, ALU.mult))

            for u in range(B * CT):
                if u == 1:
                    pool.wait_ge(modB_in[0], 16 * 3 * B)
                    gate_floor(modB0[:, :, 0:C])
                    scale = modB0[:, :, 2 * C:3 * C]
                    step(pool.tensor_scalar(scale, scale, 1.0, None, ALU.add))
                    settle()
                    pool.sem_inc(modB_floored, 1)
                if u == 2:
                    gate_floor(gb0[:, :, :])
                    settle()
                    pool.sem_inc(modB_floored, 1)
                pool.wait_ge(exp_ready, 4 * u + 4)
                pool.wait_ge(tv_ready, u + 1)
                pool.tensor_tensor(vS[u % 2], vS[u % 2], mz, ALU.mult).then_inc(mzv_ready, 1)
            for n in range(B, 2 * B):
                inverse_root(n)

            def gather(q, r):
                if not early(q, r, 4):
                    pool.wait_ge(tx_done, 4 * q + (r - 3))
                pool.tensor_copy(tile_idx[r][:, :], gidx[:, bass.ds(4 * q + r, 1)]).then_inc(tile_idx_ready, 1)
                pool.wait_ge(tile_idx_ready, 4 * q + (r + 1))
                pool.sem_inc(gathers_begun, 1)
                pool.indirect_dma_start(out=xg[r], out_offset=None, in_=h2_dram,
                                        in_offset=bass.IndirectOffsetOnAxis(ap=tile_idx[r][:, :], axis=0))\
                    .then_inc(xg_in[r], 16)

            pool.wait_ge(gidx_ready, 1)
            pool.wait_ge(h2_out, 16 * B)
            pool.wait_ge(shy_done, 1)
            for r in range(4):
                gather(0, r)
            last_q = load_last(pool)
            with pool.Fori(1, SURE_QUADS) as q:
                for r in range(4):
                    gather(q, r)
            with pool.Fori(SURE_QUADS, QUADS) as q:
                with pool.If(q <= last_q):
                    for r in range(4):
                        gather(q, r)
            gather(*near(last_q, 3, 1))

            for i in range(2):
                pool.wait_ge(y_out[i], 32 * last_q + 32)
            pool.sem_inc(gathers_begun, 1)
            pool.wait_ge(y_filled, 16 * (QUADS - SURE_QUADS))

            def pick(t, choices=range(TOPK)):
                if t >= YG:
                    pool.wait_ge(comb_done, t - YG + 1)
                for k in choices:
                    pool.indirect_dma_start(out=yg[t % YG][:, k, :], out_offset=None, in_=y_dram,
                                            in_offset=bass.IndirectOffsetOnAxis(ap=pidx[:, t, k:k + 1].bitcast(U32), axis=0))\
                        .then_inc(yg_in[t % YG][k // (TOPK // 2)], 16)

            pick(0)
            pick(1)
            for t in range(2, TB):
                pick(t)
            pick(TB, range(TOPK // 2))
            pool.wait_ge(shy_done, 2)
            zero = par[:, P_ZERO:P_ZERO + 1]
            for v in h1l + h1h:
                for cols in (slice(0, PAD), slice(PAD - 2 + S, SW)):
                    ins = pool.tensor_copy(v[:, cols], zero.to_broadcast([P, cols.stop - cols.start]))
            ins.then_inc(pads_ready, 1)
            pool.wait_ge(pads_ready, 1)
            inverse_root(4)
            pick(TB, range(TOPK // 2, TOPK))
            for t in range(TB + 1, NT):
                pick(t)
            for n in range(5, 8):
                inverse_root(n)

        @block.vector
        def _(dve):
            step, settle = counter(dve, dve_step)
            tt, ts_, stt = dve.tensor_tensor, dve.tensor_scalar, dve.scalar_tensor_tensor

            dve.memset(mhalf[:, :], -0.5).then_inc(mhalf_ready, 1)
            dve.memset(eoff[:, 0:1], 0)
            dve.memset(ones16[:, :], 1.0)
            dve.memset(onesE[:, :], 1.0)
            dve.memset(O[:, 0:1], START)
            dve.memset(Q[:, 0:1], 0.0)
            step(dve.memset(PP[:, 0:1], 0.0))
            dve.wait_ge(par_in, 32)
            dve.tensor_copy(tri16[:, :], con[:, K_TRI:K_TRI + P])
            step(dve.tensor_copy(iota16[:, :], con[:, K_IOTA:K_IOTA + P]))

            def mod_cols(layer, pairs, n):
                dve.wait_ge(modT_done, n + 1)
                for sh, sc in pairs:
                    w = CT * B
                    dst = modcol[:, layer, :, :].rearrange("p j b -> p (j b)")
                    dve.tensor_copy(dst[:, w * sh:w * (sh + 1)], bank[5][:, w * sh:w * (sh + 1)])
                    ins = ts_(dst[:, w * sc:w * (sc + 1)], bank[5][:, w * sc:w * (sc + 1)], 1.0, None, ALU.add)
                ins.then_inc(modcol_ready, 1)

            def gate_floor(g, sign, size):
                step(stt(size, g, -1.0, g, ALU.mult, ALU.max))
                settle()
                ts_(sign, g, 0.0, 2.0, ALU.is_ge, ALU.mult)
                step(ts_(size, size, 0.25, None, ALU.max))
                settle()
                return step(stt(g, sign, -1.0, size, ALU.add, ALU.mult))

            def norm_stats(t, src):
                step(dve.bn_stats(out=stats[:, t, :], in_=src[:, t, :]))

            def layer_norm(n, src, stats_done=False):
                b = n % B
                tiles = range(b * TB, (b + 1) * TB)
                if not stats_done:
                    for t in tiles:
                        norm_stats(t, src)
                settle()
                for t in tiles:
                    step(dve.bn_aggr(out=mv[:, t, :], in_=stats[:, t, :]))
                settle()
                ts_(ve[:, b * TB:(b + 1) * TB], mv[:, b * TB:(b + 1) * TB, 1], EPS, None, ALU.add).then_inc(ve_ready, 1)
                if n >= B:
                    dve.wait_ge(normT_done, CT * (n - B + 1))
                dve.wait_ge(rstd_ready, n + 1)
                for t in tiles:
                    ins = ts_(norm[:, t, :], src[:, t, :], mv[:, t, 0:1], rstd[:, t:t + 1], ALU.subtract, ALU.mult)
                ins.then_inc(norm_ready, 1)

            def residual(x, b, gate, done, free, tmp, banks=(0, 1)):
                dve.wait_ge(proj_done, done)
                g = gate.unsqueeze(1).to_broadcast([P, 2, C])
                for h in range(2):
                    step(tt(tmp[h].rearrange("p (t c) -> p t c", t=2),
                            bank[banks[h]][:, :].rearrange("p (t c) -> p t c", t=2), g, ALU.mult))
                settle()
                for h in range(2):
                    v = x[:, b * TB + 2 * h:b * TB + 2 * h + 2, :]
                    ins = tt(v, v, tmp[h].rearrange("p (t c) -> p t c", t=2), ALU.add)
                ins.then_inc(x_done, 1)
                dve.wait_ge(x_done, free)

            def row_copies(ns):
                for n in ns:
                    dve.wait_ge(modps_done, n + 1)
                    dve.tensor_copy(modrow0[:, n * 512:(n + 1) * 512], bank[2 + n][0:B, :]).then_inc(modrow_ready, 1)

            for b in range(B):
                dve.wait_ge(x_in_s[b], 16)
                if b == 0:
                    layer_norm(0, X)
                    row_copies(range(1))
                    mod_cols(0, ((SA, CA),), 0)
                else:
                    row_copies(range(1, 3))
                    layer_norm(1, X)
                    mod_cols(0, ((SB, CB),), 1)

            def wkv(u):
                b, c = divmod(u, CT)
                k, v, e = kS[u % 2], vS[u % 2], er[u % 2]
                dve.wait_ge(kvr_ready, 3 * u + 1)
                if u == 0:
                    dve.wait_ge(act_step, 2)
                step(dve.tensor_tensor_scan(O[:, 1:S + 1], wneg[:, c:c + 1].to_broadcast([P, S]), k, START,
                                            ALU.add, ALU.max))
                settle()
                tt(t1, O[:, 0:S], O[:, 1:S + 1], ALU.subtract).then_inc(exparg_ready, 1)
                tt(t2, k, O[:, 1:S + 1], ALU.subtract).then_inc(exparg_ready, 1)
                step(stt(z, k, par[:, P_TF + c:P_TF + c + 1], O[:, 0:S], ALU.add, ALU.subtract))
                settle()
                ts_(rz, z, 0.0, None, ALU.max).then_inc(exparg_ready, 1)
                ts_(mz, z, 0.0, None, ALU.min).then_inc(exparg_ready, 1)
                dve.wait_ge(kvr_ready, 3 * u + 2)
                dve.wait_ge(exp_ready, 4 * u + 2)
                tt(Bv, t2, v, ALU.mult).then_inc(tv_ready, 1)
                step(dve.tensor_tensor_scan(Q[:, 1:S + 1], t1, t2, 0.0, ALU.mult, ALU.add))
                dve.wait_ge(tv_ready, u + 1)
                step(dve.tensor_tensor_scan(PP[:, 1:S + 1], t1, Bv, 0.0, ALU.mult, ALU.add))
                dve.wait_ge(exp_ready, 4 * u + 4)
                settle()
                step(tt(z, rz, PP[:, 0:S], ALU.mult))
                step(tt(rz, rz, Q[:, 0:S], ALU.mult))
                settle()
                step(tt(rz, rz, mz, ALU.add))
                dve.wait_ge(mzv_ready, u + 1)
                tt(z, z, v, ALU.add)
                settle()
                dve.wait_ge(kvr_ready, 3 * u + 3)
                step(stt(rz, e, 1.0, rz, ALU.add, ALU.mult))
                settle()
                step(dve.reciprocal(t2, rz))
                settle()
                dve.wait_ge(rvk_done, 3 * CT * (b + 1))
                tt(hT[:, c, b * S:(b + 1) * S], z, t2, ALU.mult).then_inc(yT_ready, 1)

            for u in range(B * CT):
                wkv(u)
            tmp0 = [z, t1]
            dve.wait_ge(yT_ready, B * CT)
            dve.wait_ge(modB_floored, 1)
            residual(X, 0, modB0[:, 0, 0:C], 1, 1, tmp0)
            layer_norm(2, X)
            residual(X, 1, modB0[:, 1, 0:C], 2, 2, tmp0, (2, 3))
            layer_norm(3, X)
            for b in range(B):
                dve.wait_ge(normT_done, CT * (B + b + 1))
                v = norm[:, b * TB:(b + 1) * TB, :]
                sh, sc = [modB0[:, b, i * C:(i + 1) * C].unsqueeze(1).to_broadcast([P, TB, C]) for i in (1, 2)]
                step(tt(v, v, sc, ALU.mult))
                settle()
                tt(v, v, sh, ALU.add).then_inc(h2_ready, 1)

            dve.wait_ge(route_in, 32)
            dve.wait_ge(h2_ready, B)
            dve.memset(gsx[:, :, G:], BIG)
            dve.memset(sfx[:, :, E:], BIG)
            dve.wait_ge(score_ready, 1)
            step(tt(sfc, scores[:, :, :], cbias[:, :].unsqueeze(1).to_broadcast([P, NT, E]), ALU.add))
            settle()
            f4 = sfc.rearrange("p t (g a b) -> p (t g a) b", g=G, a=2)
            fl = lambda v: v.rearrange("p t g a -> p (t g a)")
            tt(fl(hi2), f4[:, :, 0], f4[:, :, 1], ALU.max)
            step(tt(fl(lo2), f4[:, :, 0], f4[:, :, 1], ALU.min))
            settle()
            tt(m1, hi2[:, :, :, 0], hi2[:, :, :, 1], ALU.max)
            tt(m2, hi2[:, :, :, 0], hi2[:, :, :, 1], ALU.min)
            step(tt(m3, lo2[:, :, :, 0], lo2[:, :, :, 1], ALU.max))
            settle()
            step(tt(m2, m2, m3, ALU.max))
            settle()
            step(tt(gsx[:, :, 0:G], m1, m2, ALU.add))
            settle()
            for t in range(NT):
                step(dve.max(gtop[:, t, :], gsx[:, t, :]))
            settle()
            for t in range(NT):
                step(dve.match_replace(grep[:, t, :], gtop[:, t, :], gsx[:, t, :], -BIG))
            settle()
            step(ts_(gmask, grep[:, :, 0:G], -0.5 * BIG, None, ALU.is_lt))
            settle()
            step(ts_(gpen, gmask, -1.0, -NONE, ALU.add, ALU.mult))
            f3 = sfc.rearrange("p t (g a) -> p t g a", g=G)
            bc = lambda v: v.unsqueeze(3).to_broadcast([P, NT, G, EG])
            x3 = sfx[:, :, 0:E].rearrange("p t (g a) -> p t g a", g=G)
            step(tt(x3, f3, bc(gmask), ALU.mult))
            settle()
            step(tt(x3, x3, bc(gpen), ALU.add))
            settle()
            for t in range(NT):
                step(dve.max(stop8[:, t, :], sfx[:, t, :]))
            settle()
            for t in range(NT):
                step(dve.match_replace(srep[:, t, :], stop8[:, t, :], sfx[:, t, :], -BIG))
            settle()
            step(ts_(mask[:, :, :], srep[:, :, 0:E], -0.5 * BIG, None, ALU.is_lt))
            settle()
            dve.tensor_copy(mask16[:, :, :], mask[:, :, :]).then_inc(mask_ready, 1)

            def shared_hidden(b, ms):
                for m in ms:
                    n = SHT * b + m
                    dve.wait_ge(shsil_ready, n + 1)
                    dve.wait_ge(shps_done, 2 * n + 2)
                    k = SH_ROWS[m]
                    tt(sh_hid[0:k, m, :], sh_sil[0:k, :], bank[3 + 2 * m][0:k, :], ALU.mult).then_inc(shhid_ready, 1)

            shared_hidden(0, range(1))

            dve.wait_ge(rank_done, 1)
            step(tt(cmp8[:, :, :], bank[1][:, 0:E].unsqueeze(2).to_broadcast([P, E, G]),
                    con[:, K_THR:K_THR + G].unsqueeze(1).to_broadcast([P, E, G]), ALU.is_gt))
            settle()
            step(dve.tensor_reduce(ntile[:, :], cmp8[:, :, :], AX.X, ALU.add))
            settle()
            step(dve.tensor_tensor_scan(incl[:, :], onesE[:, :], ntile[:, :], 0.0, ALU.mult, ALU.add))
            settle()
            step(ts_(last_quad[:, :], incl[0:1, E - 1:E], -1.0, None, ALU.add))
            step(tt(base[:, :], incl[:, :], ntile[:, :], ALU.subtract))
            step(ts_(ejcmp[:, :], incl[0:SLOT_TILES, :], par[0:SLOT_TILES, P_J:P_J + 1], None, ALU.is_le))
            settle()
            ts_(last_quad[:, :], last_quad[:, :], 2, None, ALU.arith_shift_right).then_inc(quads_ready, 1)
            step(ts_(base[:, :], base[:, :], float(P), 1.0, ALU.mult, ALU.add))
            dve.tensor_reduce(ej[:, :], ejcmp[:, :], AX.X, ALU.add).then_inc(ej_ready, 1)
            settle()
            shared_hidden(0, range(1, 2))
            step(tt(pos[:, :, :], bank[0][:, 0:NT * E].rearrange("p (t e) -> p t e", t=NT),
                    base[:, :].unsqueeze(1).to_broadcast([P, NT, E]), ALU.add))
            settle()
            step(tt(pos[:, :, :], pos[:, :, :], mask[:, :, :], ALU.mult))
            settle()
            for t in range(NT):
                step(dve.max(ptop[:, t, :], pos[:, t, :]))
            settle()
            step(ts_(pidx[:, :, :], ptop[:, :, :], -1.0, 0.0, ALU.add, ALU.max))
            settle()
            ts_(pint[:, 0, :, :], pidx[:, :, :], 7, None, ALU.arith_shift_right)
            step(ts_(pint[:, 1, :, :], pidx[:, :, :], P - 1, None, ALU.bitwise_and))
            settle()
            step(dve.tensor_copy(pflt[:, :, :, :], pint[:, :, :, :]))
            settle()

            def onehots_j(t):
                if t >= TB:
                    dve.wait_ge(onehot_used, TOPK * (t - TB + 1))
                shape = [P, TOPK, SLOT_TILES + 1]
                tt(onehot_j[:, t % TB * TOPK:(t % TB + 1) * TOPK, :],
                   iota16[:, 0:SLOT_TILES + 1].unsqueeze(1).to_broadcast(shape),
                   pflt[:, 0, t, 0:TOPK].unsqueeze(2).to_broadcast(shape), ALU.is_equal).then_inc(onehot_j_ready, 1)

            n = 0
            dve.wait_ge(h2_out, 16 * B)
            onehots_j(0)
            shared_hidden(0, range(2, SHT))
            onehots_j(1)
            for t in range(NT):
                if t + 2 < NT:
                    onehots_j(t + 2)
                for k in range(TOPK):
                    if n >= OS:
                        dve.wait_ge(onehot_used, n - OS + 1)
                    ts_(onehot_s[:, n % OS, :], iota16[:, :], pflt[:, 1, t, k:k + 1], None, ALU.is_equal)\
                        .then_inc(onehot_ready, 1)
                    n += 1
            dve.wait_ge(onehot_used, n)
            dve.tensor_copy(gidx[:, :], bank[1][:, 128:128 + SLOT_TILES + 1]).then_inc(gidx_ready, 1)
            dve.wait_ge(ejT_done, 1)
            ts_(eoff[:, 1:1 + SLOT_TILES], bank[1][0:1, 256:256 + SLOT_TILES], float(E - 1), None, ALU.min).then_inc(eoff_ready, 1)

            def copy_h(q, r):
                dve.wait_ge(th_done, 4 * q + (r + 1))
                dve.tensor_copy(hidT[r % 2], bank[4 + r % 2][0:MH, 0:2 * P]).then_inc(hidT_ready, 1)

            def tile_hidden(q, r):
                dve.wait_ge(sil_ready, 4 * q + (r + 1))
                tt(hid[r % 2], sil[r % 2], bank[2 + r % 2][:, M:2 * M], ALU.mult).then_inc(hid_ready, 1)

            def copy_y(q, r):
                dve.wait_ge(dn_done, 4 * q + (r + 1))
                if not early(q, r, 2):
                    dve.wait_ge(y_out[r % 2], 16 * (2 * q + r // 2))
                dve.tensor_copy(yt[r % 2], bank[6 + r % 2][:, 0:C]).then_inc(y_ready, 1)

            def quad(q, first=False):
                for r in range(4):
                    if not (first and r == 0):
                        copy_h(*near(q, r, -1))
                    tile_hidden(q, r)
                    if not (first and r == 0):
                        copy_y(*near(q, r, -1))

            last_q = load_last(dve)
            quad(0, first=True)
            with dve.Fori(1, SURE_QUADS) as q:
                quad(q)
            with dve.Fori(0, (QUADS + 1 - SURE_QUADS) // TAIL) as g:
                with dve.If(TAIL * g + SURE_QUADS <= last_q + 1):
                    with dve.Fori(0, TAIL) as i:
                        q = TAIL * g + i + SURE_QUADS
                        with dve.If(q <= last_q):
                            quad(q)
                        with dve.If(q == last_q + 1):
                            copy_h(*near(q, 0, -1))
                            copy_y(*near(q, 0, -1))
                    dve.nop()
            dve.wait_ge(gu_done, 4 * last_q + 4)

            def low_part(l, whole, h):
                return tt(l, whole, h.bitcast(F32), ALU.subtract)

            def weight_low(l, whole, h, rounded, done):
                dve.wait_ge(*rounded)
                low_part(l, whole, h).then_inc(done, 1)

            def choice_weights(ks):
                eq, eqs = srep[:, :, 0:E], sfx[:, :, 0:E]
                for k in ks:
                    step(tt(eq, pos[:, :, :], ptop[:, :, k:k + 1].to_broadcast([P, NT, E]), ALU.is_equal))
                    settle()
                    step(tt(eqs, eq, scores[:, :, :], ALU.mult))
                    settle()
                    step(dve.tensor_reduce(wk[:, :, k], eqs, AX.X, ALU.add))
                    settle()

            choice_weights(range(TOPK // 2))
            weight_low(w1l, w1w, w1h, (w1_high, 1), w1_low)
            choice_weights(range(TOPK // 2, TOPK))
            shared_hidden(1, range(SHT))

            def decay_rates():
                dve.wait_ge(act_step, 6)
                step(tt(sp[:, 3, :], sp[:, 3, :], sp[:, 1, :], ALU.add))
                settle()
                ts_(sp[:, 4, :], sp[:, 3, :], -8.0, None, ALU.mult)
                ts_(sp[:, 5, :], sp[:, 3, :], -16.0, None, ALU.mult).then_inc(sp_ready, 1)

            def combine(*ts):
                dve.wait_ge(shy_ready, ts[-1] // TB + 1)
                for k in range(TOPK):
                    for t in ts:
                        acc = shared_y[:, t, :]
                        if k % (TOPK // 2) == 0:
                            dve.wait_ge(yg_in[t % YG][k // (TOPK // 2)], 16 * TOPK // 2 * (t // YG + 1))
                        last = step(stt(acc, yg[t % YG][:, k, :], wk[:, t, k:k + 1], acc, ALU.mult, ALU.add))
                        settle(last - len(ts) + 1)
                for t in ts:
                    last = step(tt(shared_y[:, t, :], shared_y[:, t, :], gb0[:, t // TB, :], ALU.mult))
                    settle(last - len(ts) + 1)
                for t in ts:
                    settle(last - len(ts) + 1 + ts.index(t))
                    tt(X2[:, t, :], X2[:, t, :], shared_y[:, t, :], ALU.add).then_inc(comb_done, 1)
                dve.wait_ge(comb_done, ts[-1] + 1)

            def gated_input(b):
                dve.wait_ge(a2_ready, RT * (b + 1))
                for v in (a2[:, 0:2, :], a2[0:64, 2, :]):
                    ts_(v, v, 1.0, None, ALU.min).then_inc(a2min_ready, 1)
                dve.wait_ge(gates_ready, 2 * RT * (b + 1))
                for rows, ms in ((P, slice(0, 2)), (64, slice(2, 3))):
                    ins = tt(iS[0:rows, ms, :], iS[0:rows, ms, :], hc[0:rows, ms, :], ALU.mult)
                ins.then_inc(ix_ready, 1)

            def recurrence(b):
                dve.wait_ge(ix_ready, b + 1)
                dve.wait_ge(mult_ready, 2 * (b + 1))
                for rows, ms in ((P, slice(0, 2)), (64, slice(2, 3))):
                    last = step(tt(iS[0:rows, ms, :], iS[0:rows, ms, :], a2[0:rows, ms, :], ALU.mult))
                settle()
                dve.wait_ge(a_ready, RT * (b + 1))
                for m in range(RT):
                    n = R_ROWS[m]
                    dve.tensor_tensor_scan(iS[0:n, m, :], aS[0:n, m, :], iS[0:n, m, :], 0.0, ALU.mult, ALU.add)\
                       .then_inc(hs_ready, 1)

            def hadamard_adds():
                dve.wait_ge(had_ready, 4)
                src, dst = f2t, f2w
                for w in (1, 2, 4):
                    s5 = src.rearrange("p (i a j) c -> p i a (j c)", a=2, j=w)
                    d5 = dst.rearrange("p (i a j) c -> p i a (j c)", a=2, j=w)
                    ins = [tt(d5[:, :, 0, :], s5[:, :, 0, :], s5[:, :, 1, :], ALU.add),
                           tt(d5[:, :, 1, :], s5[:, :, 0, :], s5[:, :, 1, :], ALU.subtract)]
                    if w < 4:
                        step(ins[1])
                        settle()
                    else:
                        ins[1].then_inc(f2_ready, 1)
                    src, dst = dst, src

            def gate_floor1(v, loaded):
                dve.wait_ge(modB_in[1], loaded)
                gate_floor(v.rearrange("p b n -> p (b n)"), *tmp1)
                settle()

            def input_low(n):
                for c in range(CT):
                    dve.wait_ge(hT_whole, CT * (n - 4) + c + 1)
                    low_part(xl[:, c, :], xw[:, c, :], xh[:, c, :]).then_inc(hT_low, 1)

            def modulated1(n, b, sh, sc):
                for dst, done in ((xh, hT_ready), (xw, hT_whole)):
                    for c in range(CT):
                        dve.wait_ge(normT_done, CT * n + c + 1)
                        ts_(dst[:, c, :], bank[c][:, :], modcol[:, 1, CT * sc + c, b:b + 1],
                            modcol[:, 1, CT * sh + c, b:b + 1], ALU.mult, ALU.add).then_inc(done, 1)

            def hidden_low(b):
                for m in range(RT):
                    dve.wait_ge(h1_whole, RT * b + m + 1)
                    places = [(slice(0, R_ROWS[m]), slice(PAD, PAD + S))]
                    if m == 2:
                        places.append((slice(64, P), slice(PAD - 2, PAD - 2 + S)))
                    for rows, cols in places:
                        ins = low_part(h1l[m][rows, cols], h1w[m][rows, cols], h1h[m][rows, cols])
                    ins.then_inc(h1_low, 1)

            def conv_low_part(b):
                for m in range(RT):
                    n = R_ROWS[m]
                    dve.wait_ge(hc_whole, RT * b + m + 1)
                    low_part(hcl[0:n, m, :], hc[0:n, m, :], hch[0:n, m, :]).then_inc(hc_low, 1)

            def recur_low(b):
                for m in range(RT):
                    n = R_ROWS[m]
                    dve.wait_ge(hs_high, RT * b + m + 1)
                    low_part(hsl[0:n, m, :], iS[0:n, m, :], hsh[0:n, m, :]).then_inc(hs_low, 1)

            def ffn_low(b, h):
                dve.wait_ge(fhid_high, HT * b + h + 1)
                low_part(fhl[:, h, :], fhw[:, h, :], fhh[:, h, :]).then_inc(fhid_low, 1)

            def ffn_hidden(b, extra=None):
                for h in range(HT):
                    n = HT * b + h
                    dve.wait_ge(fsil_ready, n + 1)
                    dve.wait_ge(fps_done, 2 * n + 2)
                    if b and h == 0:
                        dve.wait_ge(proj_done, 5)
                    tt(fhw[:, h, :], fsil[n % 2], bank[3 + 2 * (n % 3)][:, :], ALU.mult).then_inc(fhid_ready, 1)
                    if h:
                        ffn_low(b, h - 1)
                    if extra:
                        extra(h)
                ffn_low(b, HT - 1)

            dve.wait_ge(x1_in, 32)
            dve.wait_ge(modB_floored, 2)
            combine(0, 1)
            norm_stats(0, X2)
            norm_stats(1, X2)
            combine(2)
            norm_stats(2, X2)
            mod_cols(1, ((SA, CA), (SB, CB)), 2)
            combine(3)
            norm_stats(3, X2)
            layer_norm(4, X2, stats_done=True)
            weight_low(convl, convw, convh, (conv_high, 1), conv_low)
            input_low(4)
            combine(4)
            norm_stats(4, X2)
            hidden_low(0)
            decay_rates()
            combine(5)
            norm_stats(5, X2)
            combine(6, 7)
            norm_stats(6, X2)
            norm_stats(7, X2)
            layer_norm(5, X2, stats_done=True)
            dve.tensor_copy(hsl[64:65, 2, :], par[64:65, P_ZERO:P_ZERO + 1].to_broadcast([1, S]))
            dve.tensor_copy(hsh[64:65, 2, :], onesE[64:65, 0:1].to_broadcast([1, S])).then_inc(ones_ready, 1)
            weight_low(gatel, gatew, gateh, (gate_high, 1), gate_low)
            conv_low_part(0)
            input_low(5)
            hidden_low(1)
            weight_low(w2l, w2w, w2h, (w2_high, 1), w2_low)
            gate_floor1(ga1, 16 * B)
            for k in range(CT):
                weight_low(f13l[:, k, :], f13w[:, k, :], f13h[:, k, :], (f13_high, k + 1), f13_low)
            gated_input(0)
            recurrence(0)
            recur_low(0)
            hadamard_adds()
            residual(X2, 0, ga1[:, 0, :], 3, 3, tmp1)
            layer_norm(6, X2)
            conv_low_part(1)
            weight_low(f2l, f2w, f2h, (f2_high, 1), f2_low)
            modulated1(6, 0, SB, CB)
            input_low(6)
            gated_input(1)

            def other_sequence(h):
                if h == 1:
                    recurrence(1)
                if h == 3:
                    recur_low(1)
                if h == 5:
                    residual(X2, 1, ga1[:, 1, :], 4, 4, tmp1)

            ffn_hidden(0, other_sequence)
            layer_norm(7, X2)
            gate_floor1(gb1, 32 * B)
            residual(X2, 0, gb1[:, 0, :], 5, 5, tmp1)
            input_low(7)
            ffn_hidden(1)
            residual(X2, 1, gb1[:, 1, :], 6, 6, tmp1)


def early(q, r, n):
    return isinstance(q, int) and 4 * q + r < n


def near(q, r, d):
    return q + (r + d) // 4, (r + d) % 4


def _cols(a, rows=P):
    n = -(-a.shape[0] // rows) * rows
    padded = np.zeros((n,) + a.shape[1:], a.dtype)
    padded[:a.shape[0]] = a
    return np.ascontiguousarray(np.moveaxis(padded.reshape((n // rows, rows) + a.shape[1:]), 0, 1))


def _flat(a):
    return np.ascontiguousarray(a.reshape(a.shape[0], -1))


def _hadamard(n):
    h = np.ones((1, 1), np.float32)
    while h.shape[0] < n:
        h = np.block([[h, h], [h, -h]])
    return h


def _lay_out(i):
    f = np.float32
    small = np.zeros((P, P_COLS), f)
    for col, a in ((P_TD, i["L0_attn_time_decay"]), (P_TF, i["L0_attn_time_first"]), (P_B1, i["L1_attn_b1"]),
                   (P_CB, i["L1_attn_conv_b"]), (P_BA, i["L1_attn_ba"]), (P_LAM, i["L1_attn_lam"])):
        c = _cols(a)
        small[:, col:col + c.shape[1]] = c
    bx = i["L1_attn_bx"]
    small[:, P_BX:P_BX + 2] = _cols(bx[:2 * P])
    small[64:128, P_BX + 2] = bx[2 * P:]
    for col, c in ((P_C0, i["L0_c"]), (P_C1, i["L1_c"])):
        small[:, col:col + CT * B] = _flat(_cols(np.ascontiguousarray(c.T)))
    small[:, P_TOK:P_TOK + NT] = np.arange(NT * P, dtype=f).reshape(NT, P).T
    small[:, P_J] = np.arange(P, dtype=f)
    consts = np.zeros((P, K_COLS), f)
    consts[:, K_ID:K_ID + P] = np.eye(P)
    consts[:, K_TRI:K_TRI + P] = np.triu(np.ones((P, P)), 1)
    consts[:, K_HAD:K_HAD + P] = _hadamard(P) / 32.0
    consts[:, K_IOTA:K_IOTA + P] = np.arange(P)
    consts[:, K_THR:K_THR + G] = np.arange(G) * P
    gate, up, down = i["L0_ffn_gate_w"], i["L0_ffn_up_w"], i["L0_ffn_down_w"]
    gu = np.concatenate([gate, up], axis=2)
    gu = np.ascontiguousarray(gu.reshape(E, CT, P, 2 * M).transpose(2, 0, 1, 3)).reshape(P, -1)
    dn = np.ascontiguousarray(down.reshape(E, 2, MH, C).transpose(2, 0, 1, 3)).reshape(MH, -1)
    taps = _cols(i["L1_attn_conv_w"].transpose(1, 2, 0))
    conv = np.concatenate([taps[:, :2].reshape(P, 2 * TAPS, R),
                           np.concatenate([taps[:64, 2, 0::2], taps[:64, 2, 1::2]], axis=0)], axis=1)
    wa, wx = i["L1_attn_wa"].T, i["L1_attn_wx"].T
    gates = np.concatenate([wa[:, :2 * P], wx[:, :2 * P], wa[:, 2 * P:], wx[:, 2 * P:]], axis=1)
    w2 = np.concatenate([i["L1_attn_w2"].T, i["L1_attn_b2"][None]], axis=0)
    return {
        "x": i["L0_attn_x"].reshape(B * S, C),
        "small": small, "consts": consts,
        "wmod0": _cols(i["L0_wmod"]), "wmod1": _cols(i["L1_wmod"]),
        "w_rvk": _cols(i["L0_attn_W_rvk"].T), "w_out": _cols(i["L0_attn_W_out"].T),
        "w_router": _cols(i["L0_ffn_w_router"]),
        "corr_bias": np.ascontiguousarray(np.broadcast_to(i["L0_ffn_corr_bias"], (P, E))),
        "w_gu": gu, "w_dn": dn,
        "w_shgu": _cols(np.concatenate([i["L0_ffn_sh_gate_w"], i["L0_ffn_sh_up_w"]], axis=1)),
        "w_shdn": _cols(i["L0_ffn_sh_down_w"]),
        "w_1": _cols(i["L1_attn_w1"].T),
        "w_conv": conv,
        "w_gates": _cols(gates), "w_2": _cols(w2),
        "w_f13": _cols(np.concatenate([i["L1_ffn_W1"].T, i["L1_ffn_W3"].T], axis=1)),
        "w_f2": _cols(i["L1_ffn_W2"].T),
    }


def kernel(**inputs):
    import concourse.bacc as bacc
    from concourse.bass_utils import run_bass_kernel_spmd

    arrays = {n: np.ascontiguousarray(a) for n, a in _lay_out({k: np.asarray(v) for k, v in inputs.items()}).items()}
    nc = bacc.Bacc("TRN2", target_bir_lowering=False, num_devices=1)
    args = [nc.dram_tensor(n, a.shape, mybir.dt.from_np(a.dtype), kind="ExternalInput").ap() for n, a in arrays.items()]
    out = nc.dram_tensor("out", (B * S, C), F32, kind="ExternalOutput").ap()
    two_layers(nc, *args, out)
    r = run_bass_kernel_spmd(nc, [arrays], core_ids=[0])
    return r.results[0]["out"].reshape(B, S, C)
```
